# Optimizing a Trainium2 kernel written in Bass

```python
import numpy as np
import jax
import jax.numpy as jnp

def _softmax(x, axis=-1):
    return jax.nn.softmax(x, axis=axis)

def _gelu(x):
    return jax.nn.gelu(x, approximate=True)

def _silu(x):
    return jax.nn.silu(x)

def _sigmoid(x):
    return jax.nn.sigmoid(x)

def _layernorm(x, axis=-1, eps=1e-05):
    m = jnp.mean(x, axis=axis, keepdims=True)
    v = jnp.var(x, axis=axis, keepdims=True)
    return (x - m) / jnp.sqrt(v + eps)

def _scatter_add(tgt, idx, src, axis=0):
    return tgt.at[idx].add(src)

def _segment_sum(src, seg, n):
    return jax.ops.segment_sum(src, seg, n)
kernel_name = 'mk_sandwich_d2_jaxref_r8_f0081d'

def setup_inputs(seed: int=0):
    np.random.seed(seed)
    _w = jnp.asarray

    def _L0_attn_setup():
        import jax, jax.numpy as jnp
        import numpy as np
        B, T, D, H, NT = (2, 256, 128, 16, 7)
        HD = D // H
        TEMP = 0.5
        key = jax.random.key(seed)
        ks = jax.random.split(key, 6)
        x = jax.random.normal(ks[0], (B, T, D), jnp.float32)
        qkv_w = jax.random.normal(ks[1], (3 * D, D), jnp.float32) / np.sqrt(D)
        out_w = jax.random.normal(ks[2], (D, D), jnp.float32) / np.sqrt(D)
        hex_w = jax.random.normal(ks[3], (6, D), jnp.float32) * 0.02
        q6_w = jax.random.normal(ks[4], (6, D), jnp.float32) * 0.02
        tr = np.zeros((NT, 6, 6), dtype=np.float32)
        for i in range(6):
            tr[i] = np.eye(6)
            tr[i, i, i] = -1.0
        tr[6] = -np.eye(6)
        transforms = jnp.asarray(tr)
        transform_weights = jax.random.normal(ks[5], (H, NT), jnp.float32) * 0.01
        hamming_lambda_logit = jnp.asarray(np.log(0.1 / 0.9), jnp.float32)
        scale_logit = jnp.zeros((), jnp.float32)
        sips_alpha = jnp.ones((1,), jnp.float32)
        sips_beta = jnp.full((1,), np.sqrt(HD), jnp.float32)
        return {'x': x, 'qkv_w': qkv_w, 'out_w': out_w, 'hex_w': hex_w, 'hamming_lambda_logit': hamming_lambda_logit, 'q6_w': q6_w, 'transforms': transforms, 'transform_weights': transform_weights, 'scale_logit': scale_logit, 'sips_alpha': sips_alpha, 'sips_beta': sips_beta}
    _L0_attn_in = _L0_attn_setup()

    def _L0_ffn_setup():
        import jax, jax.numpy as jnp
        import numpy as np
        DIM = 128
        DEPTH = 2
        HEADS = 8
        DIM_HEAD = 64
        WINDOW = 64
        INNER = HEADS * DIM_HEAD
        HID = int(DIM * 4 * 2 / 3)
        B, N = (2, 1024)
        QK_SCALE = 8.0

        def shift_token(t):
            t1, t2 = jnp.split(t, 2, axis=-1)
            t2 = jnp.pad(t2, ((0, 0), (1, 0), (0, 0)))[:, :-1]
            return jnp.concatenate([t1, t2], axis=-1)

        def l2norm(t):
            return t / jnp.clip(jnp.linalg.norm(t, axis=-1, keepdims=True), 1e-12)

        def rotate_half(x):
            x1, x2 = jnp.split(x, 2, axis=-1)
            return jnp.concatenate([-x2, x1], axis=-1)

        def rotary_xpos(q, k):
            n = q.shape[-2]
            half_idx = jnp.arange(0, DIM_HEAD, 2, dtype=jnp.float32)
            inv_freq = 1.0 / 10000.0 ** (half_idx / DIM_HEAD)
            t = jnp.arange(n, dtype=jnp.float32)
            freqs = t[:, None] * inv_freq[None, :]
            freqs = jnp.concatenate([freqs, freqs], axis=-1)
            base = (half_idx + 0.4 * DIM_HEAD) / (1.4 * DIM_HEAD)
            power = (t - n // 2) / float(WINDOW // 2)
            scale = base[None, :] ** power[:, None]
            scale = jnp.concatenate([scale, scale], axis=-1)
            cos, sin = (jnp.cos(freqs), jnp.sin(freqs))
            q = q * cos * scale + rotate_half(q) * sin * scale
            k = k * cos / scale + rotate_half(k) * sin / scale
            return (q, k)

        def local_attention(q, k, v):
            b, h, n, d = q.shape
            w = n // WINDOW
            bq = q.reshape(b, h, w, WINDOW, d) * QK_SCALE
            bk = k.reshape(b, h, w, WINDOW, d)
            bv = v.reshape(b, h, w, WINDOW, d)

            def look_around(t):
                p = jnp.pad(t, ((0, 0), (0, 0), (1, 0), (0, 0), (0, 0)))
                return jnp.concatenate([p[:, :, :w], p[:, :, 1:]], axis=3)
            bk, bv = (look_around(bk), look_around(bv))
            bt = jnp.arange(n).reshape(w, WINDOW)
            btp = jnp.pad(bt, ((1, 0), (0, 0)), constant_values=-1)
            btk = jnp.concatenate([btp[:w], btp[1:]], axis=1)
            sim = jnp.einsum('bhwid,bhwjd->bhwij', bq, bk)
            i = bt[:, :, None]
            j = btk[:, None, :]
            mask = (i < j) | (i > j + WINDOW) | (j == -1)
            sim = jnp.where(mask, -jnp.finfo(sim.dtype).max, sim)
            attn = jax.nn.softmax(sim, axis=-1)
            out = jnp.einsum('bhwij,bhwjd->bhwid', attn, bv)
            return out.reshape(b, h, n, d)

        def _layer(x, wqkv, qs, ksc, wo, lg, lb, w1, b1, w2, b2):
            b, n, _ = x.shape
            h = shift_token(x)
            qkv = h @ wqkv
            q, k, v = jnp.split(qkv, 3, axis=-1)
            to_heads = lambda t: t.reshape(b, n, HEADS, DIM_HEAD).transpose(0, 2, 1, 3)
            q, k, v = (to_heads(q), to_heads(k), to_heads(v))
            q = l2norm(q) * qs
            k = l2norm(k) * ksc
            q, k = rotary_xpos(q, k)
            o = local_attention(q, k, v)
            o = o.transpose(0, 2, 1, 3).reshape(b, n, INNER)
            x = x + o @ wo
            h = shift_token(x)
            mu = h.mean(-1, keepdims=True)
            var = h.var(-1, keepdims=True)
            h = (h - mu) / jnp.sqrt(var + 1e-05) * lg + lb
            h = h @ w1 + b1
            a, g = jnp.split(h, 2, axis=-1)
            h = a * jax.nn.gelu(g, approximate=False)
            x = x + h @ w2 + b2
            return x
        key = jax.random.key(seed)
        ks = jax.random.split(key, 6)
        return {'x': jax.random.normal(ks[0], (B, N, DIM), jnp.float32), 'wqkv': jax.random.normal(ks[1], (DEPTH, DIM, 3 * INNER), jnp.float32) * 0.02, 'q_scale': jnp.ones((DEPTH, DIM_HEAD), jnp.float32), 'k_scale': jnp.ones((DEPTH, DIM_HEAD), jnp.float32), 'wo': jax.random.normal(ks[2], (DEPTH, INNER, DIM), jnp.float32) * 0.02, 'ln_g': jnp.ones((DEPTH, DIM), jnp.float32), 'ln_b': jnp.zeros((DEPTH, DIM), jnp.float32), 'w1': jax.random.normal(ks[3], (DEPTH, DIM, 2 * HID), jnp.float32) * 0.02, 'b1': jnp.zeros((DEPTH, 2 * HID), jnp.float32), 'w2': jax.random.normal(ks[4], (DEPTH, HID, DIM), jnp.float32) * 0.02, 'b2': jnp.zeros((DEPTH, DIM), jnp.float32)}
    _L0_ffn_in = _L0_ffn_setup()

    def _L1_attn_setup():
        import jax, jax.numpy as jnp
        import numpy as np
        B, T, C = (64, 32, 128)
        N_HEAD, HEAD_SIZE, KV_RANK = (16, 64, 128)
        BLOCK_SIZE = 32
        key = jax.random.key(seed)
        ks = jax.random.split(key, 5)
        HD = N_HEAD * HEAD_SIZE

        def init(k, shape):
            fan_in = shape[0]
            bound = 1.0 / np.sqrt(fan_in)
            return jax.random.uniform(k, shape, jnp.float32, -bound, bound)
        return {'x': jax.random.normal(ks[0], (B, T, C), jnp.float32), 'w_kv_down': init(ks[1], (C, KV_RANK)), 'w_kv_up': init(ks[2], (KV_RANK, 2 * HD)), 'w_q': init(ks[3], (C, HD)), 'w_out': init(ks[4], (HD, C))}
    _L1_attn_in = _L1_attn_setup()

    def _L1_ffn_setup():
        import jax, jax.numpy as jnp
        import numpy as np
        EPS = 1e-09
        key = jax.random.key(seed)
        k0, k1, k2, k3 = jax.random.split(key, 4)
        B, S, H, F, E = (4, 256, 128, 256, 8)
        return {'hidden_states': jax.random.normal(k0, (B, S, H), dtype=jnp.float32), 'router_w': jax.random.normal(k1, (H, E), dtype=jnp.float32) * 0.02, 'w1': jax.random.normal(k2, (E, H, F), dtype=jnp.float32) * 0.02, 'w2': jax.random.normal(k3, (E, F, H), dtype=jnp.float32) * 0.02}
    _L1_ffn_in = _L1_ffn_setup()
    _d = {'L0_attn_x': _L0_attn_in['x'], 'L0_attn_qkv_w': _L0_attn_in['qkv_w'], 'L0_attn_out_w': _L0_attn_in['out_w'], 'L0_attn_hex_w': _L0_attn_in['hex_w'], 'L0_attn_hamming_lambda_logit': _L0_attn_in['hamming_lambda_logit'], 'L0_attn_q6_w': _L0_attn_in['q6_w'], 'L0_attn_transforms': _L0_attn_in['transforms'], 'L0_attn_transform_weights': _L0_attn_in['transform_weights'], 'L0_attn_scale_logit': _L0_attn_in['scale_logit'], 'L0_attn_sips_alpha': _L0_attn_in['sips_alpha'], 'L0_attn_sips_beta': _L0_attn_in['sips_beta'], 'L0_ffn_wqkv': _L0_ffn_in['wqkv'], 'L0_ffn_q_scale': _L0_ffn_in['q_scale'], 'L0_ffn_k_scale': _L0_ffn_in['k_scale'], 'L0_ffn_wo': _L0_ffn_in['wo'], 'L0_ffn_ln_g': _L0_ffn_in['ln_g'], 'L0_ffn_ln_b': _L0_ffn_in['ln_b'], 'L0_ffn_w1': _L0_ffn_in['w1'], 'L0_ffn_b1': _L0_ffn_in['b1'], 'L0_ffn_w2': _L0_ffn_in['w2'], 'L0_ffn_b2': _L0_ffn_in['b2'], 'L1_attn_w_kv_down': _L1_attn_in['w_kv_down'], 'L1_attn_w_kv_up': _L1_attn_in['w_kv_up'], 'L1_attn_w_q': _L1_attn_in['w_q'], 'L1_attn_w_out': _L1_attn_in['w_out'], 'L1_ffn_router_w': _L1_ffn_in['router_w'], 'L1_ffn_w1': _L1_ffn_in['w1'], 'L1_ffn_w2': _L1_ffn_in['w2']}
    _x0 = _d['L0_attn_x']
    _d['L0_attn_x'] = jax.random.normal(jax.random.fold_in(jax.random.key(seed), 1), (32, 256, 128), dtype=_x0.dtype)
    del _x0
    return _d

def reference(L0_attn_x, L0_attn_qkv_w, L0_attn_out_w, L0_attn_hex_w, L0_attn_hamming_lambda_logit, L0_attn_q6_w, L0_attn_transforms, L0_attn_transform_weights, L0_attn_scale_logit, L0_attn_sips_alpha, L0_attn_sips_beta, L0_ffn_wqkv, L0_ffn_q_scale, L0_ffn_k_scale, L0_ffn_wo, L0_ffn_ln_g, L0_ffn_ln_b, L0_ffn_w1, L0_ffn_b1, L0_ffn_w2, L0_ffn_b2, L1_attn_w_kv_down, L1_attn_w_kv_up, L1_attn_w_q, L1_attn_w_out, L1_ffn_router_w, L1_ffn_w1, L1_ffn_w2):

    def _L0_attn_ref(x, qkv_w, out_w, hex_w, hamming_lambda_logit, q6_w, transforms, transform_weights, scale_logit, sips_alpha, sips_beta):
        import jax, jax.numpy as jnp
        import numpy as np
        B, T, D, H, NT = (2, 256, 128, 16, 7)
        HD = D // H
        TEMP = 0.5
        b, t, _ = x.shape
        qkv = (x @ qkv_w.T).reshape(b, t, 3, H, HD)
        q = jnp.transpose(qkv[:, :, 0], (0, 2, 1, 3))
        k = jnp.transpose(qkv[:, :, 1], (0, 2, 1, 3))
        v = jnpp = jnp.transpose(qkv[:, :, 2], (0, 2, 1, 3))
        raw = jnp.einsum('bhid,bhjd->bhij', q, k)
        scores = sips_alpha[0] * jnp.tanh(raw / sips_beta[0])
        soft_bits = jnp.tanh(x @ hex_w.T)
        hamming = jnp.einsum('bid,bjd->bij', soft_bits, soft_bits) / 2.0
        lam = jax.nn.sigmoid(hamming_lambda_logit)
        scores = scores + lam * hamming[:, None, :, :]
        hexc = jnp.tanh(x @ q6_w.T)
        w = jax.nn.softmax(transform_weights / TEMP, axis=-1)
        Mh = jnp.einsum('ht,tde->hde', w, transforms)
        lat = jnp.einsum('bid,hde,bje->bhij', hexc, Mh, hexc) / 6.0
        lat = lat * (jax.nn.sigmoid(scale_logit) * 2.0)
        scores = scores + lat
        causal = jnp.tril(jnp.ones((t, t), bool))
        scores = jnp.where(causal[None, None], scores, -jnp.inf)
        attn = jax.nn.softmax(scores, axis=-1)
        out = jnp.einsum('bhij,bhjd->bhid', attn, v)
        out = jnp.transpose(out, (0, 2, 1, 3)).reshape(b, t, D)
        return out @ out_w.T

    def _L0_ffn_ref(x, wqkv, q_scale, k_scale, wo, ln_g, ln_b, w1, b1, w2, b2):
        import jax, jax.numpy as jnp
        import numpy as np
        DIM = 128
        DEPTH = 2
        HEADS = 8
        DIM_HEAD = 64
        WINDOW = 64
        INNER = HEADS * DIM_HEAD
        HID = int(DIM * 4 * 2 / 3)
        B, N = (2, 1024)
        QK_SCALE = 8.0

        def shift_token(t):
            t1, t2 = jnp.split(t, 2, axis=-1)
            t2 = jnp.pad(t2, ((0, 0), (1, 0), (0, 0)))[:, :-1]
            return jnp.concatenate([t1, t2], axis=-1)

        def l2norm(t):
            return t / jnp.clip(jnp.linalg.norm(t, axis=-1, keepdims=True), 1e-12)

        def rotate_half(x):
            x1, x2 = jnp.split(x, 2, axis=-1)
            return jnp.concatenate([-x2, x1], axis=-1)

        def rotary_xpos(q, k):
            n = q.shape[-2]
            half_idx = jnp.arange(0, DIM_HEAD, 2, dtype=jnp.float32)
            inv_freq = 1.0 / 10000.0 ** (half_idx / DIM_HEAD)
            t = jnp.arange(n, dtype=jnp.float32)
            freqs = t[:, None] * inv_freq[None, :]
            freqs = jnp.concatenate([freqs, freqs], axis=-1)
            base = (half_idx + 0.4 * DIM_HEAD) / (1.4 * DIM_HEAD)
            power = (t - n // 2) / float(WINDOW // 2)
            scale = base[None, :] ** power[:, None]
            scale = jnp.concatenate([scale, scale], axis=-1)
            cos, sin = (jnp.cos(freqs), jnp.sin(freqs))
            q = q * cos * scale + rotate_half(q) * sin * scale
            k = k * cos / scale + rotate_half(k) * sin / scale
            return (q, k)

        def local_attention(q, k, v):
            b, h, n, d = q.shape
            w = n // WINDOW
            bq = q.reshape(b, h, w, WINDOW, d) * QK_SCALE
            bk = k.reshape(b, h, w, WINDOW, d)
            bv = v.reshape(b, h, w, WINDOW, d)

            def look_around(t):
                p = jnp.pad(t, ((0, 0), (0, 0), (1, 0), (0, 0), (0, 0)))
                return jnp.concatenate([p[:, :, :w], p[:, :, 1:]], axis=3)
            bk, bv = (look_around(bk), look_around(bv))
            bt = jnp.arange(n).reshape(w, WINDOW)
            btp = jnp.pad(bt, ((1, 0), (0, 0)), constant_values=-1)
            btk = jnp.concatenate([btp[:w], btp[1:]], axis=1)
            sim = jnp.einsum('bhwid,bhwjd->bhwij', bq, bk)
            i = bt[:, :, None]
            j = btk[:, None, :]
            mask = (i < j) | (i > j + WINDOW) | (j == -1)
            sim = jnp.where(mask, -jnp.finfo(sim.dtype).max, sim)
            attn = jax.nn.softmax(sim, axis=-1)
            out = jnp.einsum('bhwij,bhwjd->bhwid', attn, bv)
            return out.reshape(b, h, n, d)

        def _layer(x, wqkv, qs, ksc, wo, lg, lb, w1, b1, w2, b2):
            b, n, _ = x.shape
            h = shift_token(x)
            qkv = h @ wqkv
            q, k, v = jnp.split(qkv, 3, axis=-1)
            to_heads = lambda t: t.reshape(b, n, HEADS, DIM_HEAD).transpose(0, 2, 1, 3)
            q, k, v = (to_heads(q), to_heads(k), to_heads(v))
            q = l2norm(q) * qs
            k = l2norm(k) * ksc
            q, k = rotary_xpos(q, k)
            o = local_attention(q, k, v)
            o = o.transpose(0, 2, 1, 3).reshape(b, n, INNER)
            x = x + o @ wo
            h = shift_token(x)
            mu = h.mean(-1, keepdims=True)
            var = h.var(-1, keepdims=True)
            h = (h - mu) / jnp.sqrt(var + 1e-05) * lg + lb
            h = h @ w1 + b1
            a, g = jnp.split(h, 2, axis=-1)
            h = a * jax.nn.gelu(g, approximate=False)
            x = x + h @ w2 + b2
            return x
        for l in range(DEPTH):
            x = _layer(x, wqkv[l], q_scale[l], k_scale[l], wo[l], ln_g[l], ln_b[l], w1[l], b1[l], w2[l], b2[l])
        return x

    def _L1_attn_ref(x, w_kv_down, w_kv_up, w_q, w_out):
        import jax, jax.numpy as jnp
        import numpy as np
        B, T, C = (64, 32, 128)
        N_HEAD, HEAD_SIZE, KV_RANK = (16, 64, 128)
        BLOCK_SIZE = 32
        Bx, Tx, Cx = x.shape
        HD = N_HEAD * HEAD_SIZE
        latent_kv = x @ w_kv_down
        kv = latent_kv @ w_kv_up
        k, v = (kv[..., :HD], kv[..., HD:])
        k = k.reshape(Bx, Tx, N_HEAD, HEAD_SIZE)
        v = v.reshape(Bx, Tx, N_HEAD, HEAD_SIZE)
        q = (x @ w_q).reshape(Bx, Tx, N_HEAD, HEAD_SIZE)
        scale = HEAD_SIZE ** (-0.5)
        att = jnp.einsum('bqhd,bkhd->bhqk', q, k) * scale
        causal = jnp.tril(jnp.ones((Tx, Tx), dtype=bool))
        att = jnp.where(causal, att, -jnp.inf)
        att = jax.nn.softmax(att, axis=-1)
        y = jnp.einsum('bhqk,bkhd->bqhd', att, v)
        y = y.reshape(Bx, Tx, HD)
        return y @ w_out

    def _L1_ffn_ref(hidden_states, router_w, w1, w2):
        import jax, jax.numpy as jnp
        import numpy as np
        EPS = 1e-09
        TOP_K = 2
        orig_shape = hidden_states.shape
        H = orig_shape[-1]
        E = router_w.shape[-1]
        flat = hidden_states.reshape(-1, H)
        T = flat.shape[0]
        gate_logits = flat @ router_w
        gate_probs = jax.nn.softmax(gate_logits, axis=-1)
        topk_w, topk_idx = jax.lax.top_k(gate_probs, TOP_K)
        topk_w = topk_w / jnp.clip(topk_w.sum(-1, keepdims=True), EPS)
        cw = jnp.zeros((T, E), dtype=flat.dtype).at[jnp.arange(T)[:, None], topk_idx].add(topk_w)
        h = jax.nn.silu(jnp.einsum('td,edf->etf', flat, w1))
        y = jnp.einsum('etf,efd->etd', h, w2)
        out = jnp.einsum('etd,te->td', y, cw)
        return out.reshape(orig_shape)
    x = L0_attn_x
    x = x + _layernorm(_L0_attn_ref(_layernorm(x, axis=-1), L0_attn_qkv_w, L0_attn_out_w, L0_attn_hex_w, L0_attn_hamming_lambda_logit, L0_attn_q6_w, L0_attn_transforms, L0_attn_transform_weights, L0_attn_scale_logit, L0_attn_sips_alpha, L0_attn_sips_beta), axis=-1)
    x = x + _layernorm(_L0_ffn_ref(_layernorm(x, axis=-1), L0_ffn_wqkv, L0_ffn_q_scale, L0_ffn_k_scale, L0_ffn_wo, L0_ffn_ln_g, L0_ffn_ln_b, L0_ffn_w1, L0_ffn_b1, L0_ffn_w2, L0_ffn_b2), axis=-1)
    x = x + _layernorm(_L1_attn_ref(_layernorm(x, axis=-1), L1_attn_w_kv_down, L1_attn_w_kv_up, L1_attn_w_q, L1_attn_w_out), axis=-1)
    x = x + _layernorm(_L1_ffn_ref(_layernorm(x, axis=-1), L1_ffn_router_w, L1_ffn_w1, L1_ffn_w2), axis=-1)
    return x

_drawn_inputs = setup_inputs


def setup_inputs(seed=0):
    import zlib

    import numpy as np

    out = dict(_drawn_inputs(seed))
    spreads = {'L0_ffn_q_scale': (1.0, 0.6),
     'L0_ffn_k_scale': (1.0, 0.6),
     'L0_ffn_ln_g': (1.0, 0.6),
     'L0_ffn_ln_b': (0.0, 0.63),
     'L0_ffn_b1': (0.0, 0.339),
     'L0_ffn_b2': (0.0, 0.1)}
    factors = {'L0_attn_hex_w': 2.834, 'L0_attn_transform_weights': 58.285}
    for name, (base, spread) in spreads.items():
        noise = np.random.default_rng([zlib.crc32(name.encode()), seed]).standard_normal(out[name].shape)
        drawn = base * np.exp(spread * noise) if base else spread * noise
        out[name] = jnp.asarray(drawn.astype(out[name].dtype))
    for name, factor in factors.items():
        out[name] = (out[name] * factor).astype(out[name].dtype)
    return out
```

```python
from contextlib import ExitStack

import numpy as np

import concourse.bass as bass
from concourse import mybir

F32 = mybir.dt.float32
F32R = mybir.dt.float32r
BF16 = mybir.dt.bfloat16
ACT = mybir.ActivationFunctionType
ALU = mybir.AluOpType
AX = mybir.AxisListType

P = 128
D = 128
T = 256
TILES = T // P
BANK = 512
RING = 4
LN_EPS = 1e-5
MASKED = -1e30


class Seq:

    def __init__(self, number, parity, first=False, last=False):
        self.number, self.parity, self.first, self.last = number, parity, first, last

    def before(self):
        return Seq(self.number - 1, 1 - self.parity, first=isinstance(self.number, int) and self.number == 1)

    def tiles(self, whole):
        return whole[:, bass.ds(self.number * TILES, TILES), :]

    def tile(self, whole, t):
        return whole[:, bass.ds(self.number * TILES + t, 1), :].rearrange("p a d -> p (a d)")


def pipeline(eng, n_seq, step):
    step(Seq(0, 0, first=True), None)
    step(Seq(1, 1), Seq(0, 0, first=True))
    with eng.Fori(0, (n_seq - 2) // 2) as k:
        step(Seq(k * 2 + 2, 0), Seq(k * 2 + 1, 1))
        step(Seq(k * 2 + 3, 1), Seq(k * 2 + 2, 0))
    step(None, Seq(n_seq - 1, 1, last=True))


class Count:

    def __init__(self, sem, order, front):
        self.sem, self.order = sem, list(order)
        assert len(set(self.order)) == len(self.order)
        self.front = [e for e in self.order if e in front]
        self.back = [e for e in self.order if e not in front]

    def place(self, event, seq):
        if event in self.front:
            if seq.first:
                return self.front.index(event)
            return (seq.number - 1) * len(self.order) + (len(self.front) + self.order.index(event))
        before = len(self.front) + (self.back if seq.last else self.order).index(event)
        return seq.number * len(self.order) + before

    def done(self, event, seq):
        return self.place(event, seq) + 1

    def slot(self, event, seq, slots):
        step = len(self.order)
        if event in self.front:
            if seq.first:
                return self.front.index(event) % slots
            return ((seq.parity + 1) % 2 * step + len(self.front) + self.order.index(event)) % slots
        before = len(self.front) + (self.back if seq.last else self.order).index(event)
        return (seq.parity * step + before) % slots


class Ring:

    def __init__(self, banks, filled, drained, order, front):
        assert 2 * len(order) % len(banks) == 0
        self.banks = banks
        self.filled, self.drained = Count(filled, order, front), Count(drained, order, front)

    def bank(self, job, seq):
        return self.banks[self.filled.slot(job, seq, len(self.banks))]

    def wait_free(self, pe, job, seq):
        ring = len(self.banks)
        place = self.filled.place(job, seq)
        if not (isinstance(place, int) and place < ring):
            pe.wait_ge(self.drained.sem, place - (ring - 1))

    def wait_filled(self, eng, job, seq):
        eng.wait_ge(self.filled.sem, self.filled.done(job, seq))

    def wait_drained(self, eng, job, seq):
        eng.wait_ge(self.drained.sem, self.drained.done(job, seq))


def wait_apart(nc, eng, c, sem, value):
    eng.wait_ge(sem, value)
    nc.vector.tensor_copy(c["carrier"][:, 0:1], c["eps"][:, 0:1])


PRE_NORM = ["stats0", "stats1", "mv0", "mv1", "xn0", "xn1"]
POST_NORM = ["ystats0", "ystats1", "ymv0", "ymv1", "yn0"]
RSQRT = ["var", "rstd", "yvar", "yrstd"]


class Norm:

    def __init__(self, nc, ctx, prefix, vec, rst, c):
        def sb(name, shape):
            return ctx.enter_context(nc.sbuf_tensor(prefix + name, shape, F32))

        self.nc, self.vec, self.rst, self.c = nc, vec, rst, c
        self.stats = {"": sb("stats", [P, TILES, 6]), "y": sb("ystats", [P, TILES, 6])}
        self.mv = {"": sb("mv", [P, TILES, 2]), "y": sb("ymv", [P, TILES, 2])}
        self.var = {"": sb("var", [P, TILES]), "y": sb("yvar", [P, TILES])}
        self.rstd = {"": sb("rstd", [P, TILES]), "y": sb("yrstd", [P, TILES])}
        self.xn = sb("xn", [P, TILES, D])
        self.yn = sb("yn", [P, TILES, D])

    def rsqrt(self, pool, which, seq):
        nc, vec, rst = self.nc, self.vec, self.rst
        pool.wait_ge(vec.sem, vec.done(which + "mv1", seq))
        nc.gpsimd.tensor_tensor(self.var[which][:, :], self.mv[which][:, :, 1], self.c["eps"][:, 0:TILES],
                                ALU.add)\
            .then_inc(rst.sem, 1)
        pool.wait_ge(rst.sem, rst.done(which + "var", seq))
        nc.gpsimd.tensor_tensor(self.rstd[which][:, :], self.var[which][:, :],
                                self.c["minus_half"][:, 0:TILES], ALU.pow).then_inc(rst.sem, 1)

    def moments(self, dve, which, seq, tiles):
        nc, vec = self.nc, self.vec
        for t in range(TILES):
            nc.vector.bn_stats(self.stats[which][:, t], tiles[t]).then_inc(vec.sem, 1)
        wait_apart(nc, dve, self.c, vec.sem, vec.done(f"{which}stats{TILES - 1}", seq))
        for t in range(TILES):
            nc.vector.bn_aggr(self.mv[which][:, t], self.stats[which][:, t]).then_inc(vec.sem, 1)

    def scaled(self, which, t, out, tile):
        mv, rstd = self.mv[which], self.rstd[which]
        return self.nc.vector.tensor_scalar(out, tile, mv[:, t, 0:1], rstd[:, t:t + 1],
                                            ALU.subtract, ALU.mult)

    def pre(self, dve, seq, x, to_act):
        self.moments(dve, "", seq, [seq.tile(x, t) for t in range(TILES)])
        dve.wait_ge(self.rst.sem, self.rst.done("rstd", seq))
        if not seq.first:
            to_act.wait_filled(dve, "xnT", seq.before())
        for t in range(TILES):
            self.scaled("", t, self.xn[:, t], seq.tile(x, t)).then_inc(self.vec.sem, 1)

    def post(self, dve, seq, x, ring, job):
        nc, vec = self.nc, self.vec
        bank = ring.bank(job, seq)
        wait_apart(nc, dve, self.c, ring.filled.sem, ring.filled.done(job, seq))
        self.moments(dve, "y", seq, [bank[:, t * D:(t + 1) * D] for t in range(TILES)])
        dve.wait_ge(self.rst.sem, self.rst.done("yrstd", seq))
        self.scaled("y", 0, self.yn[:, 0], bank[:, 0:D]).then_inc(vec.sem, 1)
        self.scaled("y", 1, self.yn[:, 1], bank[:, D:2 * D]).then_inc(ring.drained.sem, 1)
        dve.wait_ge(vec.sem, vec.done("yn0", seq))
        ring.wait_drained(dve, job, seq)
        return nc.vector.tensor_tensor(seq.tiles(x), seq.tiles(x), self.yn[:, :, :], ALU.add)


TH, TD = 16, 8
GROUPS = 4
ROWS = 32
BITS = 6
NT = 7


def token_attention(nc, n_seq, x, w, c):
    units = [f"{n}.{kind}" for n in range(GROUPS) for kind in ("i1a", "i1b", "i0")]
    LAG_EXP, LAG_T = 2, 4
    act_front, dve_front = ["xnT", "q0", "q1", "right", "v"], ["k0", "k1", "left0", "left1"]
    act_order, dve_order = [], []
    for i in range(len(units) + LAG_T):
        if i < len(units):
            act_order.append("raw" + units[i])
            dve_order.append("bil" + units[i])
        if i >= LAG_T:
            (act_order if i % 2 == 0 else dve_order).append("pT" + units[i - LAG_T])
    act_order += act_front + ["oT"]
    dve_order += dve_front + ["av", "out"]
    SLOTS = 5

    def unit(name):
        n, kind = name.split(".")
        return int(n), {"i1a": (0, 1), "i1b": (2, 3), "i0": (0, 1, 2, 3)}[kind], int(kind[1])

    with ExitStack() as ctx:
        def sb(name, shape, dt=F32):
            return ctx.enter_context(nc.sbuf_tensor("t_" + name, shape, dt))

        def sem(name):
            return ctx.enter_context(nc.semaphore("t_" + name))

        qT = [sb(f"qT{u}", [P, GROUPS, T]) for u in range(2)]
        kT = [sb(f"kT{u}", [P, GROUPS, T]) for u in range(2)]
        left = [sb(f"left{u}", [P, GROUPS, T]) for u in range(2)]
        right = [sb(f"right{u}", [P, T]) for u in range(2)]
        v = [sb(f"v{u}", [P, TILES, TH, TD + 1]) for u in range(2)]
        xnT = sb("xnT", [P, T])
        bilinear = sb("bilinear", [2 * BITS, TH, ROWS])
        tanh_qk = sb("tanh_qk", [P, 3, BANK])
        scores = sb("scores", [P, SLOTS, BANK])
        neg_max = sb("neg_max", [P, 3, 4])
        pT = sb("pT", [P, len(units), BANK])
        rden = sb("rden", [P, TILES, TH])
        o = sb("o", [P, TILES, D])
        oT = sb("oT", [P, T])
        act_banks = [ctx.enter_context(nc.psum_tensor(f"t_act{i}", [P, BANK], F32)) for i in range(RING)]
        dve_banks = [ctx.enter_context(nc.psum_tensor(f"t_dve{i}", [P, BANK], F32)) for i in range(RING)]
        to_act = Ring(act_banks, sem("act_filled"), sem("act_drained"), act_order, act_front)
        to_dve = Ring(dve_banks, sem("dve_filled"), sem("dve_drained"), dve_order, dve_front)
        vec = Count(sem("vec"), PRE_NORM + ["max" + n for n in units] + ["rden"] + POST_NORM, PRE_NORM)
        rst = Count(sem("rst"), RSQRT, RSQRT[:2])
        shifted = Count(sem("shifted"), units, [])
        exped = Count(sem("exped"), units, [])
        norm = Norm(nc, ctx, "t_", vec, rst, c)
        setup_pool, setup_act, setup_dve, setup_pe = (sem("setup_" + e) for e in ("pool", "act", "dve", "pe"))
        lam, scl = w["scalars"][:, 0:1], w["scalars"][:, 1:2]
        alpha, beta = w["scalars"][:, 2:3], w["scalars"][:, 3:4]
        sig = sb("sig", [P, 2, 3])
        inv_beta = sb("inv_beta", [P, 1])
        tw = sb("tw", [TH, 3, 8])
        tw_sum = sb("tw_sum", [TH, 3])
        twT = sb("twT", [8, TH])

        with nc.Block() as block:
            @block.gpsimd
            def _(pool):
                for u in range(2):
                    nc.gpsimd.memset(v[u][:, :, :, TD:TD + 1], 1.0).then_inc(setup_pool, 1)
                nc.gpsimd.memset(bilinear[:, :, :], 0.0).then_inc(setup_pool, 1)

                def step(front, back):
                    if front:
                        norm.rsqrt(pool, "", front)
                    if back:
                        for i, name in enumerate(units):
                            n, gs, t = unit(name)
                            pool.wait_ge(vec.sem, vec.done("max" + name, back))
                            s = scores[:, i % SLOTS, :].rearrange("p (h j) -> p h j", h=len(gs))
                            nc.gpsimd.tensor_tensor(
                                s, s, neg_max[:, i % 3, 0:len(gs)].unsqueeze(2)
                                .broadcast_to((P, len(gs), BANK // len(gs))), ALU.add)\
                                .then_inc(shifted.sem, 1)
                        norm.rsqrt(pool, "y", back)

                pipeline(pool, n_seq, step)

            @block.vector
            def _(dve):
                nc.vector.reciprocal(inv_beta[:, :], beta).then_inc(setup_dve, 1)
                nc.vector.tensor_reduce(tw_sum[:, 0:1], w["transform"][:, :], AX.X, ALU.max)\
                    .then_inc(setup_dve, 1)
                dve.wait_ge(setup_dve, 2)
                nc.vector.tensor_scalar(tw[:, 0, 0:NT], w["transform"][:, :], tw_sum[:, 0:1], None,
                                        ALU.subtract).then_inc(setup_dve, 1)
                dve.wait_ge(setup_act, 2)
                nc.vector.tensor_scalar(sig[:, :, 1], sig[:, :, 0], 1.0, None, ALU.add)\
                    .then_inc(setup_dve, 1)
                dve.wait_ge(setup_dve, 4)
                nc.vector.reciprocal(sig[:, :, 2], sig[:, :, 1]).then_inc(setup_dve, 1)
                nc.vector.reciprocal(tw_sum[:, 2:3], tw_sum[:, 1:2]).then_inc(setup_dve, 1)
                dve.wait_ge(setup_dve, 6)
                nc.vector.tensor_scalar(tw[:, 2, 0:NT], tw[:, 1, 0:NT], tw_sum[:, 2:3],
                                        sig[0:TH, 1, 2:3], ALU.mult, ALU.mult).then_inc(setup_dve, 1)
                nc.vector.tensor_scalar(tw[:, 2, NT:NT + 1], sig[0:TH, 0, 2:3], 0.5, None, ALU.mult)\
                    .then_inc(setup_dve, 1)
                dve.wait_ge(setup_dve, 7)
                nc.vector.tensor_scalar(tw[:, 2, 0:NT], tw[:, 2, 0:NT], 1.0 / 3.0, None, ALU.mult)\
                    .then_inc(setup_dve, 1)
                dve.wait_ge(setup_pe, 1)
                nc.vector.tensor_copy(twT[:, :], dve_banks[0][0:8, 0:TH]).then_inc(setup_dve, 1)
                dve.wait_ge(setup_pe, 2)
                dve.wait_ge(setup_pool, 3)
                nc.vector.tensor_copy(
                    bilinear[:, :, 0:2 * BITS],
                    dve_banks[1][0:2 * BITS, 0:2 * BITS * TH].rearrange("a (b h) -> a h b", h=TH))\
                    .then_inc(setup_dve, 1)

                def step(front, back):
                    if front:
                        norm.pre(dve, front, x, to_act)
                    if back:
                        for i in range(len(units) + LAG_T):
                            if i < len(units):
                                name = units[i]
                                n, gs, t = unit(name)
                                to_act.wait_drained(dve, "raw" + name, back)
                                to_dve.wait_filled(dve, "bil" + name, back)
                                if i >= SLOTS and (i - SLOTS + LAG_T) % 2 == 0:
                                    to_act.wait_filled(dve, "pT" + units[i - SLOTS], back)
                                nc.vector.scalar_tensor_tensor(
                                    scores[:, i % SLOTS, :], tanh_qk[:, i % 3, :], alpha,
                                    to_dve.bank("bil" + name, back)[:, :], ALU.mult, ALU.add)\
                                    .then_inc(to_dve.drained.sem, 1)
                                to_dve.wait_drained(dve, "bil" + name, back)
                                if i >= 3:
                                    dve.wait_ge(shifted.sem, shifted.done(units[i - 3], back))
                                nc.vector.tensor_reduce(
                                    neg_max[:, i % 3, 0:len(gs)],
                                    scores[:, i % SLOTS, :].rearrange("p (h j) -> p h j", h=len(gs)),
                                    AX.X, ALU.max, negate=True).then_inc(vec.sem, 1)
                            if i >= LAG_T and i % 2 == 1:
                                job = "pT" + units[i - LAG_T]
                                to_dve.wait_filled(dve, job, back)
                                nc.vector.tensor_copy(pT[:, i - LAG_T, :], to_dve.bank(job, back)[:, :])\
                                    .then_inc(to_dve.drained.sem, 1)
                    if front:
                        u = front.parity
                        for name, out in (("k", kT[u]), ("left", left[u])):
                            for i in range(2):
                                to_dve.wait_filled(dve, f"{name}{i}", front)
                                nc.vector.tensor_copy(
                                    out[:, 2 * i:2 * i + 2, :].rearrange("p a t -> p (a t)"),
                                    to_dve.bank(f"{name}{i}", front)[:, :]).then_inc(to_dve.drained.sem, 1)
                    if back:
                        to_dve.wait_filled(dve, "av", back)
                        got = to_dve.bank("av", back)[:, 0:TILES * TH * (TD + 1)].rearrange(
                            "p (a d) -> p a d", d=TD + 1)
                        nc.vector.reciprocal(rden[:, :, :].rearrange("p a h -> p (a h)"), got[:, :, TD])\
                            .then_inc(vec.sem, 1)
                        dve.wait_ge(vec.sem, vec.done("rden", back))
                        nc.vector.tensor_tensor(
                            o[:, :, :].rearrange("p a (h d) -> p (a h) d", d=TD), got[:, :, 0:TD],
                            rden[:, :, :].rearrange("p a h -> p (a h)").unsqueeze(2)
                            .broadcast_to((P, TILES * TH, TD)), ALU.mult).then_inc(to_dve.drained.sem, 1)
                        norm.post(dve, back, x, to_dve, "out")

                pipeline(dve, n_seq, step)

            @block.scalar
            def _(act):
                nc.scalar.activation(sig[:, :, 0], w["scalars"][:, 0:2], ACT.Exp, scale=-1.0)\
                    .then_inc(setup_act, 1)
                act.wait_ge(setup_dve, 3)
                nc.scalar.activation(tw[:, 1, 0:NT], tw[:, 0, 0:NT], ACT.Exp, scale=2.0,
                                     accum_out=tw_sum[:, 1:2]).then_inc(setup_act, 1)

                def step(front, back):
                    if back:
                        for i in range(len(units) + LAG_T):
                            if i < len(units):
                                to_act.wait_filled(act, "raw" + units[i], back)
                                if i >= 3:
                                    to_dve.wait_drained(act, "bil" + units[i - 3], back)
                                nc.scalar.activation(tanh_qk[:, i % 3, :],
                                                     to_act.bank("raw" + units[i], back)[:, :],
                                                     ACT.Tanh, scale=inv_beta[:, :])\
                                    .then_inc(to_act.drained.sem, 1)
                            if 0 <= i - LAG_EXP < len(units):
                                act.wait_ge(shifted.sem, shifted.done(units[i - LAG_EXP], back))
                                s = scores[:, (i - LAG_EXP) % SLOTS, :]
                                nc.scalar.activation(s, s, ACT.Exp).then_inc(exped.sem, 1)
                            if i >= LAG_T and i % 2 == 0:
                                job = "pT" + units[i - LAG_T]
                                to_act.wait_filled(act, job, back)
                                nc.scalar.copy(pT[:, i - LAG_T, :], to_act.bank(job, back)[:, :])\
                                    .then_inc(to_act.drained.sem, 1)
                    if front:
                        u = front.parity
                        to_act.wait_filled(act, "xnT", front)
                        nc.scalar.copy(xnT[:, :], to_act.bank("xnT", front)[:, 0:T])\
                            .then_inc(to_act.drained.sem, 1)
                        for i in range(2):
                            to_act.wait_filled(act, f"q{i}", front)
                            nc.scalar.copy(qT[u][:, 2 * i:2 * i + 2, :].rearrange("p a t -> p (a t)"),
                                           to_act.bank(f"q{i}", front)[:, :])\
                                .then_inc(to_act.drained.sem, 1)
                        to_act.wait_filled(act, "right", front)
                        nc.scalar.activation(right[u][:, :], to_act.bank("right", front)[:, 0:T], ACT.Tanh)\
                            .then_inc(to_act.drained.sem, 1)
                        to_act.wait_filled(act, "v", front)
                        nc.scalar.copy(
                            v[u][:, :, :, 0:TD].rearrange("p a h d -> p (a h) d"),
                            to_act.bank("v", front)[:, 0:T].rearrange("p (a d) -> p a d", d=TD))\
                            .then_inc(to_act.drained.sem, 1)
                    if back:
                        to_act.wait_filled(act, "oT", back)
                        nc.scalar.copy(oT[:, :], to_act.bank("oT", back)[:, 0:T])\
                            .then_inc(to_act.drained.sem, 1)

                pipeline(act, n_seq, step)

            @block.tensor
            def _(pe):
                pe.wait_ge(setup_dve, 9)
                nc.tensor.transpose(dve_banks[0][0:8, 0:TH], tw[:, 2, :], c["ident"][0:TH, 0:TH])\
                    .then_inc(setup_pe, 1)
                pe.wait_ge(setup_dve, 10)
                for b in range(2 * BITS):
                    ins = nc.tensor.matmul(dve_banks[1][0:2 * BITS, b * TH:(b + 1) * TH],
                                           w["basis"][:, b, :], twT[:, :], start=True, stop=True)
                ins.then_inc(setup_pe, 1)
                pe.wait_ge(setup_dve, 11)

                def step(front, back):
                    if back:
                        u = back.parity
                        to_act.wait_drained(pe, "v", back)
                        to_dve.wait_drained(pe, "left1", back)
                        for i in range(len(units) + LAG_T):
                            if i < len(units):
                                n, gs, t = unit(units[i])
                                width = P * (t + 1)
                                raw, bil = "raw" + units[i], "bil" + units[i]
                                to_act.wait_free(pe, raw, back)
                                for s, g in enumerate(gs):
                                    ins = nc.tensor.matmul(
                                        to_act.bank(raw, back)[:, s * width:(s + 1) * width],
                                        qT[u][ROWS * n:ROWS * n + TD, g, P * t:P * t + P],
                                        kT[u][ROWS * n:ROWS * n + TD, g, 0:width], start=True, stop=True)
                                ins.then_inc(to_act.filled.sem, 1)
                                to_dve.wait_free(pe, bil, back)
                                bank = to_dve.bank(bil, back)
                                for s, g in enumerate(gs):
                                    nc.tensor.matmul(
                                        bank[:, s * width:(s + 1) * width],
                                        left[u][ROWS * n:ROWS * n + 2 * BITS, g, P * t:P * t + P],
                                        right[u][ROWS * n:ROWS * n + 2 * BITS, 0:width],
                                        start=True, stop=False)
                                    ins = nc.tensor.matmul(bank[:, (s + 1) * width - P:(s + 1) * width],
                                                           c["ident_bf"][:, :], c["mask_rows"][:, :],
                                                           start=False, stop=True)
                                ins.then_inc(to_dve.filled.sem, 1)
                            if i >= LAG_T:
                                name = units[i - LAG_T]
                                ring = to_act if i % 2 == 0 else to_dve
                                ring.wait_free(pe, "pT" + name, back)
                                pe.wait_ge(exped.sem, exped.done(name, back))
                                for b in range(BANK // P):
                                    ins = nc.tensor.transpose(
                                        ring.bank("pT" + name, back)[:, b * P:(b + 1) * P],
                                        scores[:, (i - LAG_T) % SLOTS, b * P:(b + 1) * P], c["ident"][:, :])
                                ins.then_inc(ring.filled.sem, 1)
                    if front:
                        to_act.wait_free(pe, "xnT", front)
                        for t in range(TILES):
                            pe.wait_ge(vec.sem, vec.done(f"xn{t}", front))
                            ins = nc.tensor.transpose(to_act.bank("xnT", front)[:, t * P:(t + 1) * P],
                                                      norm.xn[:, t], c["ident"][:, :])
                        ins.then_inc(to_act.filled.sem, 1)
                        to_act.wait_drained(pe, "xnT", front)
                        for name, ring, weights in (("q", to_act, w["tq"]), ("k", to_dve, w["tk"])):
                            for i in range(2):
                                ring.wait_free(pe, f"{name}{i}", front)
                                for j in range(2):
                                    g = 2 * i + j
                                    ins = nc.tensor.matmul(
                                        ring.bank(f"{name}{i}", front)[:, j * T:(j + 1) * T],
                                        weights[:, g, :], xnT[:, :], start=True, stop=True)
                                ins.then_inc(ring.filled.sem, 1)
                        to_act.wait_free(pe, "right", front)
                        nc.tensor.matmul(to_act.bank("right", front)[:, 0:T], w["bits"][:, :], xnT[:, :],
                                         start=True, stop=True).then_inc(to_act.filled.sem, 1)
                        to_act.wait_free(pe, "v", front)
                        for t in range(TILES):
                            ins = nc.tensor.matmul(to_act.bank("v", front)[:, t * D:(t + 1) * D],
                                                   xnT[:, t * P:(t + 1) * P], w["tv"][:, :],
                                                   start=True, stop=True)
                        ins.then_inc(to_act.filled.sem, 1)
                        to_act.wait_drained(pe, "right", front)
                        for i in range(2):
                            to_dve.wait_free(pe, f"left{i}", front)
                            for j in range(2):
                                g = 2 * i + j
                                ins = nc.tensor.matmul(
                                    to_dve.bank(f"left{i}", front)[:, j * T:(j + 1) * T],
                                    bilinear[:, 4 * g:4 * g + 4, :].rearrange("a h b -> a (h b)"),
                                    right[front.parity][0:2 * BITS, :], start=True, stop=True)
                            ins.then_inc(to_dve.filled.sem, 1)
                    if back:
                        to_act.wait_drained(pe, "pT" + units[-2], back)
                        if front:
                            to_dve.wait_free(pe, "av", back)
                        else:
                            to_dve.wait_drained(pe, "pT" + units[-1], back)
                        for i, name in enumerate(units):
                            n, gs, t = unit(name)
                            for s, g in enumerate(gs):
                                h = 4 * g + n
                                at = (t * TH + h) * (TD + 1)
                                for j in range(t + 1):
                                    b = s * (t + 1) + j
                                    ins = nc.tensor.matmul(
                                        to_dve.bank("av", back)[:, at:at + TD + 1],
                                        pT[:, i, b * P:(b + 1) * P], v[back.parity][:, j, h, :],
                                        start=j == 0, stop=j == t)
                        ins.then_inc(to_dve.filled.sem, 1)
                        to_act.wait_free(pe, "oT", back)
                        to_dve.wait_drained(pe, "av", back)
                        for t in range(TILES):
                            ins = nc.tensor.transpose(to_act.bank("oT", back)[:, t * P:(t + 1) * P],
                                                      o[:, t], c["ident"][:, :])
                        ins.then_inc(to_act.filled.sem, 1)
                        to_dve.wait_free(pe, "out", back)
                        to_act.wait_drained(pe, "oT", back)
                        for t in range(TILES):
                            ins = nc.tensor.matmul(to_dve.bank("out", back)[:, t * D:(t + 1) * D],
                                                   oT[:, t * P:(t + 1) * P], w["t_out"][:, :],
                                                   start=True, stop=True)
                        ins.then_inc(to_dve.filled.sem, 1)

                pipeline(pe, n_seq, step)


LAYERS, NH, HD = 2, 8, 64
INNER = NH * HD
WINDOW = 64
HID = 341
CHUNKS = [128, 128, 85]
QK_SCALE = 8.0
SPAN = P + WINDOW


def window_attention(nc, n_seq, x, z, w, c, layer):
    first_layer = layer == 0
    row_jobs = ["i1.0", "i1.1", "i1.2", "i1.3", "i0.0", "i0.1"]
    col_jobs = ["j0.0", "j0.1", "j0.2", "j0.3", "j1.0", "j1.1"]
    av_jobs = [f"av{t}.{q}" for q in range(2) for t in range(TILES)]
    parts = ["q0", "k0", "q1", "k1"]
    act_front = ["xnT"] + parts + ["v0", "v1"] + [p + "T" for p in parts]
    dve_front = []
    act_order = act_front + ["shift"] + col_jobs + ["yT0", "yT1"]
    dve_order = row_jobs + av_jobs + ["out"]
    front_vec = (PRE_NORM if first_layer else []) + [f"{e}.{p}" for p in parts for e in ("sum", "clip", "cos", "rot", "unit")]

    def heads(kind, n):
        if kind in ("i1", "j0"):
            return [4 * (n // 2) + n % 2 + 2 * i for i in range(2)]
        return [n + 2 * i for i in range(4)]

    with ExitStack() as ctx:
        pre = f"w{layer}_"

        def sb(name, shape, dt=F32):
            return ctx.enter_context(nc.sbuf_tensor(pre + name, shape, dt))

        def sem(name):
            return ctx.enter_context(nc.semaphore(pre + name))

        table = sb("table", [P, TILES, 4, HD])
        hT = sb("hT", [P, T])
        raw = sb("raw", [P, 2, INNER])
        squares = sb("squares", [P, 2, INNER])
        swapped = sb("swapped", [P, 2, INNER])
        turned = sb("turned", [P, 2, INNER])
        sums = sb("sums", [P, 2, NH])
        inv = sb("inv", [P, 2, NH])
        qT = [sb(f"qT{u}", [P, INNER // P, T]) for u in range(2)]
        kT = [sb(f"kT{u}", [P, INNER // P, T]) for u in range(2)]
        v = [sb(f"v{u}", [P, TILES, NH, HD + 1]) for u in range(2)]
        neg_max = sb("neg_max", [P, TILES, NH])
        neg2 = sb("neg2", [P, TILES, 2 * NH])
        negT = sb("negT", [2 * NH, T], F32R)
        p0 = sb("p0", [P, NH, T])
        p1 = sb("p1", [P, NH, P])
        rden = sb("rden", [P, TILES, NH])
        y = sb("y", [P, TILES, INNER])
        yT = sb("yT", [P, INNER // P, T])
        act_banks = [ctx.enter_context(nc.psum_tensor(f"{pre}act{i}", [P, BANK], F32)) for i in range(4)]
        dve_banks = [ctx.enter_context(nc.psum_tensor(f"{pre}dve{i}", [P, BANK], F32)) for i in range(2)]
        to_act = Ring(act_banks, sem("act_filled"), sem("act_drained"), act_order, act_front)
        to_dve = Ring(dve_banks, sem("dve_filled"), sem("dve_drained"), dve_order, dve_front)
        vec = Count(sem("vec"), ["neg_hi", "neg_lo"] + front_vec
                    + [f"rden{t}.{q}" for q in range(2) for t in range(TILES)], front_vec)
        rst = Count(sem("rst"), RSQRT[:2], RSQRT[:2])
        pool_front = ["keep"] + [f"{e}.{p}" for p in parts for e in ("sin", "inv")]
        gps = Count(sem("gps"), pool_front, pool_front)
        sq = Count(sem("sq"), ["square." + p for p in parts], ["square." + p for p in parts])
        norm = Norm(nc, ctx, pre, vec, rst, c)
        setup, tables_done = sem("setup"), sem("tables_done")

        with nc.Block() as block:
            @block.gpsimd
            def _(pool):
                for u in range(2):
                    nc.gpsimd.memset(v[u][:, :, :, HD:HD + 1], 1.0).then_inc(setup, 1)
                nc.gpsimd.memset(p0[:, :, SPAN:T], 0.0).then_inc(setup, 1)
                nc.gpsimd.memset(hT[:, 0:1], 0.0).then_inc(setup, 1)
                pool.wait_ge(tables_done, 4)

                def step(front, back):
                    if front:
                        if first_layer:
                            norm.rsqrt(pool, "", front)
                            pool.wait_ge(vec.sem, vec.done("xn1", front))
                            nc.gpsimd.tensor_copy(front.tiles(z), norm.xn[:, :, :]).then_inc(gps.sem, 1)
                        else:
                            if not front.first:
                                to_act.wait_filled(pool, "xnT", front.before())
                            nc.gpsimd.tensor_copy(norm.xn[:, :, :], front.tiles(z)).then_inc(gps.sem, 1)
                        for i, p in enumerate(parts):
                            kind, t, s = "qk".index(p[0]), int(p[1]), i % 2
                            to_act.wait_drained(pool, p, front)
                            halves = raw[:, s, :].rearrange("p (h a d) -> p h a d", a=2, d=HD // 2)
                            nc.gpsimd.tensor_tensor(
                                swapped[:, s, :].rearrange("p (h a d) -> p h a d", a=2, d=HD // 2),
                                halves[:, :, ::-1, :],
                                table[:, t, 2 * kind + 1, :].rearrange("p (a d) -> p a d", a=2)
                                .unsqueeze(1).broadcast_to((P, NH, 2, HD // 2)), ALU.mult)\
                                .then_inc(gps.sem, 1)
                            pool.wait_ge(vec.sem, vec.done("clip." + p, front))
                            nc.gpsimd.tensor_tensor(inv[:, s, :], sums[:, s, :], c["minus_half"][:, 0:NH],
                                                    ALU.pow).then_inc(gps.sem, 1)

                pipeline(pool, n_seq, step)

            @block.vector
            def _(dve):
                for kind, scales in enumerate((w["q_scale"], w["k_scale"])):
                    for swap in range(2):
                        row = scales[:, layer, :]
                        if swap:
                            row = scales[:, layer, :].rearrange("p (a d) -> p a d", a=2)[:, ::-1, :]
                        for t in range(TILES):
                            ins = nc.vector.scalar_tensor_tensor(
                                table[:, t, 2 * kind + swap, :].rearrange("p (a d) -> p a d", a=2),
                                c["rotary"][:, t, 2 * kind + swap, :].rearrange("p (a d) -> p a d", a=2),
                                QK_SCALE if kind == 0 else 1.0,
                                row if swap else row.rearrange("p (a d) -> p a d", a=2),
                                ALU.mult, ALU.mult)
                        ins.then_inc(tables_done, 1)
                dve.wait_ge(tables_done, 4)

                def step(front, back):
                    if back:
                        for job in row_jobs:
                            kind, n = job.split(".")
                            hs, t = heads(kind, int(n)), int(kind[1])
                            width = SPAN if t else P
                            to_dve.wait_filled(dve, job, back)
                            nc.vector.tensor_reduce(
                                neg_max[:, t, hs[0]:hs[-1] + 1:2],
                                to_dve.bank(job, back)[:, 0:width * len(hs)].rearrange(
                                    "p (h j) -> p h j", h=len(hs)),
                                AX.X, ALU.max, negate=True).then_inc(to_dve.drained.sem, 1)
                        to_dve.wait_drained(dve, row_jobs[-1], back)
                        nc.vector.tensor_copy(neg2[:, :, 0:NH].bitcast(F32R), neg_max[:, :, :])\
                            .then_inc(vec.sem, 1)
                        dve.wait_ge(vec.sem, vec.done("neg_hi", back))
                        nc.vector.tensor_tensor(neg2[:, :, NH:2 * NH], neg_max[:, :, :], neg2[:, :, 0:NH],
                                                ALU.subtract).then_inc(vec.sem, 1)
                    if front:
                        if first_layer:
                            if not front.first:
                                dve.wait_ge(gps.sem, gps.done("keep", front.before()))
                            norm.pre(dve, front, x, to_act)
                        for i, p in enumerate(parts):
                            kind, t, s = "qk".index(p[0]), int(p[1]), i % 2
                            dve.wait_ge(sq.sem, sq.done("square." + p, front))
                            per_head = lambda a: a.rearrange("p (h d) -> p h d", h=NH)
                            nc.vector.tensor_reduce(sums[:, s, :], per_head(squares[:, s, :]), AX.X, ALU.add)\
                                .then_inc(vec.sem, 1)
                            dve.wait_ge(vec.sem, vec.done("sum." + p, front))
                            nc.vector.tensor_scalar(sums[:, s, :], sums[:, s, :], 1e-24, None, ALU.max)\
                                .then_inc(vec.sem, 1)
                            if i >= 2:
                                to_act.wait_filled(dve, parts[i - 2] + "T", front)
                            elif not front.first:
                                to_act.wait_filled(dve, parts[i + 2] + "T", front.before())
                            to_act.wait_drained(dve, p, front)
                            nc.vector.tensor_tensor(
                                per_head(turned[:, s, :]), per_head(raw[:, s, :]),
                                table[:, t, 2 * kind, :].unsqueeze(1).broadcast_to((P, NH, HD)), ALU.mult)\
                                .then_inc(vec.sem, 1)
                            dve.wait_ge(vec.sem, vec.done("cos." + p, front))
                            dve.wait_ge(gps.sem, gps.done("sin." + p, front))
                            nc.vector.tensor_tensor(turned[:, s, :], turned[:, s, :], swapped[:, s, :],
                                                    ALU.add).then_inc(vec.sem, 1)
                            dve.wait_ge(vec.sem, vec.done("rot." + p, front))
                            dve.wait_ge(gps.sem, gps.done("inv." + p, front))
                            nc.vector.tensor_tensor(
                                per_head(turned[:, s, :]), per_head(turned[:, s, :]),
                                inv[:, s, :].unsqueeze(2).broadcast_to((P, NH, HD)), ALU.mult)\
                                .then_inc(vec.sem, 1)
                    if back:
                        for job in av_jobs:
                            t, q = int(job[2]), int(job[4])
                            o = to_dve.bank(job, back)[:, 0:4 * (HD + 1)].rearrange("p (h d) -> p h d", h=4)
                            to_dve.wait_filled(dve, job, back)
                            nc.vector.reciprocal(rden[:, t, 4 * q:4 * q + 4], o[:, :, HD])\
                                .then_inc(vec.sem, 1)
                            dve.wait_ge(vec.sem, vec.done(f"rden{t}.{q}", back))
                            nc.vector.tensor_tensor(
                                y[:, t, 256 * q:256 * q + 256].rearrange("p (h d) -> p h d", h=4),
                                o[:, :, 0:HD],
                                rden[:, t, 4 * q:4 * q + 4].unsqueeze(2).broadcast_to((P, 4, HD)),
                                ALU.mult).then_inc(to_dve.drained.sem, 1)
                        to_dve.wait_filled(dve, "out", back)
                        nc.vector.tensor_tensor(
                            back.tiles(z), back.tiles(z),
                            to_dve.bank("out", back)[:, 0:T].rearrange("p (a d) -> p a d", a=TILES),
                            ALU.add).then_inc(to_dve.drained.sem, 1)

                pipeline(dve, n_seq, step)

            @block.scalar
            def _(act):
                act.wait_ge(setup, 4)

                def step(front, back):
                    if front:
                        u = front.parity
                        to_act.wait_filled(act, "xnT", front)
                        bank = to_act.bank("xnT", front)
                        nc.scalar.copy(hT[0:HD, :], bank[0:HD, 0:T])
                        nc.scalar.copy(hT[HD:P, 1:T], bank[HD:P, 0:T - 1]).then_inc(to_act.drained.sem, 1)
                        for i, p in enumerate(parts):
                            s = i % 2
                            to_act.wait_filled(act, p, front)
                            if i >= 2:
                                act.wait_ge(vec.sem, vec.done("cos." + parts[i - 2], front))
                                act.wait_ge(gps.sem, gps.done("sin." + parts[i - 2], front))
                            elif not front.first:
                                act.wait_ge(vec.sem, vec.done("cos." + parts[i + 2], front.before()))
                                act.wait_ge(gps.sem, gps.done("sin." + parts[i + 2], front.before()))
                            nc.scalar.square(squares[:, s, :], to_act.bank(p, front)[:, :])\
                                .then_inc(sq.sem, 1)
                            nc.scalar.copy(raw[:, s, :], to_act.bank(p, front)[:, :])\
                                .then_inc(to_act.drained.sem, 1)
                        for t in range(TILES):
                            to_act.wait_filled(act, f"v{t}", front)
                            nc.scalar.copy(v[u][:, t, :, 0:HD],
                                           to_act.bank(f"v{t}", front)[:, :].rearrange(
                                               "p (h d) -> p h d", h=NH)).then_inc(to_act.drained.sem, 1)
                        for p in parts:
                            t, out = int(p[1]), (qT if p[0] == "q" else kT)[u]
                            to_act.wait_filled(act, p + "T", front)
                            nc.scalar.copy(out[:, :, t * P:(t + 1) * P],
                                           to_act.bank(p + "T", front)[:, :].rearrange(
                                               "p (a t) -> p a t", a=INNER // P))\
                                .then_inc(to_act.drained.sem, 1)
                    if back:
                        to_act.wait_filled(act, "shift", back)
                        nc.scalar.copy(negT[:, :], to_act.bank("shift", back)[0:2 * NH, 0:T])\
                            .then_inc(to_act.drained.sem, 1)
                        for job in col_jobs:
                            kind, n = job.split(".")
                            hs = heads(kind, int(n))
                            probs, width = (p0, SPAN) if kind == "j0" else (p1, P)
                            to_act.wait_filled(act, job, back)
                            nc.scalar.activation(
                                probs[:, hs[0]:hs[-1] + 1:2, 0:width],
                                to_act.bank(job, back)[:, 0:width * len(hs)].rearrange(
                                    "p (h j) -> p h j", h=len(hs)),
                                ACT.Exp).then_inc(to_act.drained.sem, 1)
                        for n in range(2):
                            to_act.wait_filled(act, f"yT{n}", back)
                            nc.scalar.copy(yT[:, 2 * n:2 * n + 2, :].rearrange("p a t -> p (a t)"),
                                           to_act.bank(f"yT{n}", back)[:, :])\
                                .then_inc(to_act.drained.sem, 1)

                pipeline(act, n_seq, step)

            @block.tensor
            def _(pe):
                pe.wait_ge(setup, 4)

                def step(front, back):
                    if back:
                        u = back.parity
                        to_act.wait_drained(pe, "k1T", back)
                        for job in row_jobs:
                            kind, n = job.split(".")
                            t = int(kind[1])
                            width = SPAN if t else P
                            bank = to_dve.bank(job, back)
                            to_dve.wait_free(pe, job, back)
                            for i, h in enumerate(heads(kind, int(n))):
                                rows = slice(HD * (h % 2), HD * (h % 2) + HD)
                                out = bank[:, width * i:width * (i + 1)]
                                nc.tensor.matmul(out, qT[u][rows, h // 2, P * t:P * t + P],
                                                 kT[u][rows, h // 2, (t + 1) * P - width:(t + 1) * P],
                                                 start=True, stop=False)
                                ins = nc.tensor.matmul(out, c["ident_bf"][:, :],
                                                       c["mask_window"][:, SPAN - width:SPAN],
                                                       start=False, stop=True)
                            ins.then_inc(to_dve.filled.sem, 1)
                    if front:
                        u = front.parity
                        to_act.wait_free(pe, "xnT", front)
                        for t in range(TILES):
                            if first_layer:
                                pe.wait_ge(vec.sem, vec.done(f"xn{t}", front))
                            else:
                                pe.wait_ge(gps.sem, gps.done("keep", front))
                            ins = nc.tensor.transpose(to_act.bank("xnT", front)[:, t * P:(t + 1) * P],
                                                      norm.xn[:, t], c["ident"][:, :])
                        ins.then_inc(to_act.filled.sem, 1)
                        to_act.wait_drained(pe, "xnT", front)
                        for p in parts + ["v0", "v1"]:
                            t, at = int(p[1]), "qkv".index(p[0]) * INNER
                            to_act.wait_free(pe, p, front)
                            nc.tensor.matmul(to_act.bank(p, front)[:, :], hT[:, t * P:(t + 1) * P],
                                             w["wqkv"][:, layer, at:at + INNER], start=True, stop=True)\
                                .then_inc(to_act.filled.sem, 1)
                        for i, p in enumerate(parts):
                            to_act.wait_free(pe, p + "T", front)
                            pe.wait_ge(vec.sem, vec.done("unit." + p, front))
                            for a in range(INNER // P):
                                ins = nc.tensor.transpose(
                                    to_act.bank(p + "T", front)[:, a * P:(a + 1) * P],
                                    turned[:, i % 2, a * P:(a + 1) * P], c["ident"][:, :])
                            ins.then_inc(to_act.filled.sem, 1)
                    if back:
                        u = back.parity
                        to_act.wait_free(pe, "shift", back)
                        pe.wait_ge(vec.sem, vec.done("neg_lo", back))
                        for t in range(TILES):
                            ins = nc.tensor.transpose(to_act.bank("shift", back)[0:2 * NH, t * P:(t + 1) * P],
                                                      neg2[:, t], c["ident"][:, :])
                        ins.then_inc(to_act.filled.sem, 1)
                        to_act.wait_drained(pe, "shift", back)
                        for job in col_jobs:
                            kind, n = job.split(".")
                            j = int(kind[1])
                            width = P if j else SPAN
                            bank = to_act.bank(job, back)
                            to_act.wait_free(pe, job, back)
                            for i, h in enumerate(heads(kind, int(n))):
                                rows = slice(HD * (h % 2), HD * (h % 2) + HD)
                                out = bank[:, width * i:width * i + width]
                                queries = slice(P * j, P * j + width)
                                nc.tensor.matmul(out, kT[u][rows, h // 2, P * j:P * j + P],
                                                 qT[u][rows, h // 2, queries], start=True, stop=False)
                                nc.tensor.matmul(out, c["pick8"][:, h * P:(h + 1) * P], negT[:, queries],
                                                 start=False, stop=False)
                                ins = nc.tensor.matmul(out, c["ident_bf"][:, :], c["mask_window"][:, 0:width],
                                                       start=False, stop=True)
                            ins.then_inc(to_act.filled.sem, 1)
                        to_act.wait_drained(pe, col_jobs[-1], back)
                        for job in av_jobs:
                            t, q = int(job[2]), int(job[4])
                            to_dve.wait_free(pe, job, back)
                            for i in range(4):
                                h = 4 * q + i
                                out = to_dve.bank(job, back)[:, (HD + 1) * i:(HD + 1) * (i + 1)]
                                ins = nc.tensor.matmul(out, p0[:, h, t * P:(t + 1) * P], v[u][:, 0, h, :],
                                                       start=True, stop=t == 0)
                                if t == 1:
                                    ins = nc.tensor.matmul(out, p1[:, h, :], v[u][:, 1, h, :],
                                                           start=False, stop=True)
                            ins.then_inc(to_dve.filled.sem, 1)
                        for n in range(2):
                            to_act.wait_free(pe, f"yT{n}", back)
                            to_dve.wait_drained(pe, f"av1.{n}", back)
                            for i in range(2):
                                for t in range(TILES):
                                    pair = 2 * n + i
                                    ins = nc.tensor.transpose(
                                        to_act.bank(f"yT{n}", back)[:, i * T + t * P:i * T + (t + 1) * P],
                                        y[:, t, pair * P:(pair + 1) * P], c["ident"][:, :])
                            ins.then_inc(to_act.filled.sem, 1)
                        to_dve.wait_free(pe, "out", back)
                        to_act.wait_drained(pe, "yT1", back)
                        for t in range(TILES):
                            for pair in range(INNER // P):
                                ins = nc.tensor.matmul(to_dve.bank("out", back)[:, t * D:(t + 1) * D],
                                                       yT[:, pair, t * P:(t + 1) * P],
                                                       w["wo"][:, layer, pair, :],
                                                       start=pair == 0, stop=pair == INNER // P - 1)
                        ins.then_inc(to_dve.filled.sem, 1)

                pipeline(pe, n_seq, step)


def gated_mlp(nc, n_seq, x, z, w, c, layer):
    last_layer = layer == LAYERS - 1
    act_front, dve_front = ["xnT"], ["moved"]
    act_order = ["g0", "g1", "g2"] + act_front
    dve_order = dve_front + ["a0", "a1", "a2", "out"]
    after = ["ystats0", "ystats1", "ymv0", "ymv1", "yn0", "yn1"] if last_layer else []

    with ExitStack() as ctx:
        pre = f"m{layer}_"

        def sb(name, shape, dt=F32):
            return ctx.enter_context(nc.sbuf_tensor(pre + name, shape, dt))

        def sem(name):
            return ctx.enter_context(nc.semaphore(pre + name))

        h = sb("h", [P, TILES, D])
        hT = [sb(f"hT{u}", [P, T]) for u in range(2)]
        gate = sb("gate", [P, 3, T])
        hidden = sb("hidden", [P, 3, T])
        act_banks = [ctx.enter_context(nc.psum_tensor(f"{pre}act{i}", [P, BANK], F32)) for i in range(2)]
        dve_banks = [ctx.enter_context(nc.psum_tensor(f"{pre}dve{i}", [P, BANK], F32)) for i in range(5)]
        to_act = Ring(act_banks, sem("act_filled"), sem("act_drained"), act_order, act_front)
        to_dve = Ring(dve_banks, sem("dve_filled"), sem("dve_drained"), dve_order, dve_front)
        vec = Count(sem("vec"), PRE_NORM + after, PRE_NORM)
        rst = Count(sem("rst"), RSQRT if last_layer else RSQRT[:2], RSQRT[:2])
        gps = Count(sem("gps"), ["own"], ["own"])
        norm = Norm(nc, ctx, pre, vec, rst, c)
        setup = sem("setup")

        with nc.Block() as block:
            @block.gpsimd
            def _(pool):
                nc.gpsimd.memset(hidden[:, 2, :], 1.0).then_inc(setup, 1)

                def step(front, back):
                    if front:
                        if not front.first:
                            pool.wait_ge(vec.sem, vec.done("xn1", front.before()))
                        nc.gpsimd.tensor_copy(h[:, :, 0:D // 2], front.tiles(z)[:, :, 0:D // 2])\
                            .then_inc(gps.sem, 1)
                        norm.rsqrt(pool, "", front)
                    if back and last_layer:
                        norm.rsqrt(pool, "y", back)

                pipeline(pool, n_seq, step)

            @block.vector
            def _(dve):
                dve.wait_ge(setup, 1)

                def step(front, back):
                    if front:
                        to_dve.wait_filled(dve, "moved", front)
                        nc.vector.tensor_copy(
                            h[:, :, D // 2:D],
                            to_dve.bank("moved", front)[:, 0:D].rearrange("p (a d) -> p a d", a=TILES))\
                            .then_inc(to_dve.drained.sem, 1)
                        wait_apart(nc, dve, c, to_dve.drained.sem, to_dve.drained.done("moved", front))
                        dve.wait_ge(gps.sem, gps.done("own", front))
                        norm.moments(dve, "", front, [h[:, t] for t in range(TILES)])
                        dve.wait_ge(rst.sem, rst.done("rstd", front))
                        if not front.first:
                            to_act.wait_filled(dve, "xnT", front.before())
                        for t in range(TILES):
                            norm.scaled("", t, norm.xn[:, t], h[:, t]).then_inc(vec.sem, 1)
                    if back:
                        for n, rows in enumerate(CHUNKS):
                            to_dve.wait_filled(dve, f"a{n}", back)
                            to_act.wait_drained(dve, f"g{n}", back)
                            nc.vector.scalar_tensor_tensor(
                                hidden[0:rows, n, :], to_dve.bank(f"a{n}", back)[0:rows, 0:T],
                                w["b1"][0:rows, layer, 0, n:n + 1], gate[0:rows, n, :], ALU.add, ALU.mult)\
                                .then_inc(to_dve.drained.sem, 1)
                        to_dve.wait_filled(dve, "out", back)
                        nc.vector.tensor_tensor(
                            back.tiles(z), back.tiles(z),
                            to_dve.bank("out", back)[:, 0:T].rearrange("p (a d) -> p a d", a=TILES),
                            ALU.add).then_inc(to_dve.drained.sem, 1)
                        if last_layer:
                            wait_apart(nc, dve, c, to_dve.drained.sem, to_dve.drained.done("out", back))
                            norm.moments(dve, "y", back, [back.tile(z, t) for t in range(TILES)])
                            dve.wait_ge(rst.sem, rst.done("yrstd", back))
                            for t in range(TILES):
                                norm.scaled("y", t, norm.yn[:, t], back.tile(z, t)).then_inc(vec.sem, 1)
                            dve.wait_ge(vec.sem, vec.done("yn1", back))
                            nc.vector.tensor_tensor(back.tiles(x), back.tiles(x), norm.yn[:, :, :], ALU.add)

                pipeline(dve, n_seq, step)

            @block.scalar
            def _(act):
                def step(front, back):
                    if back:
                        for n, rows in enumerate(CHUNKS):
                            to_act.wait_filled(act, f"g{n}", back)
                            nc.scalar.activation(gate[0:rows, n, :], to_act.bank(f"g{n}", back)[0:rows, 0:T],
                                                 ACT.Gelu, bias=w["b1"][0:rows, layer, 1, n:n + 1])\
                                .then_inc(to_act.drained.sem, 1)
                    if front:
                        to_act.wait_filled(act, "xnT", front)
                        nc.scalar.activation(hT[front.parity][:, :], to_act.bank("xnT", front)[:, 0:T],
                                             ACT.Identity, scale=w["ln_g"][:, layer:layer + 1],
                                             bias=w["ln_b"][:, layer:layer + 1])\
                            .then_inc(to_act.drained.sem, 1)

                pipeline(act, n_seq, step)

            @block.tensor
            def _(pe):
                def step(front, back):
                    if front:
                        to_dve.wait_free(pe, "moved", front)
                        bank = to_dve.bank("moved", front)
                        for t in range(TILES):
                            out = bank[:, t * HD:(t + 1) * HD]
                            own, ahead = front.tile(z, t)[:, HD:D], front.tile(z, 0)[:, HD:D]
                            ins = nc.tensor.matmul(out, c["next"][:, 0, :], own, start=True, stop=t == 0)
                            if t == 1:
                                ins = nc.tensor.matmul(out, c["next"][:, 1, :], ahead,
                                                       start=False, stop=True)
                        ins.then_inc(to_dve.filled.sem, 1)
                    if back:
                        u, col = back.parity, 0
                        to_act.wait_drained(pe, "xnT", back)
                        for n, rows in enumerate(CHUNKS):
                            for name, ring, at in (("g", to_act, HID), ("a", to_dve, 0)):
                                ring.wait_free(pe, f"{name}{n}", back)
                                nc.tensor.matmul(ring.bank(f"{name}{n}", back)[0:rows, 0:T],
                                                 w["w1"][:, layer, at + col:at + col + rows], hT[u][:, :],
                                                 start=True, stop=True).then_inc(ring.filled.sem, 1)
                            col += rows
                    if front:
                        to_act.wait_free(pe, "xnT", front)
                        for t in range(TILES):
                            pe.wait_ge(vec.sem, vec.done(f"xn{t}", front))
                            ins = nc.tensor.transpose(to_act.bank("xnT", front)[:, t * P:(t + 1) * P],
                                                      norm.xn[:, t], c["ident"][:, :])
                        ins.then_inc(to_act.filled.sem, 1)
                    if back:
                        to_dve.wait_free(pe, "out", back)
                        to_dve.wait_drained(pe, "a2", back)
                        for t in range(TILES):
                            for n, rows in enumerate(CHUNKS):
                                rows = rows + (n == len(CHUNKS) - 1)
                                ins = nc.tensor.matmul(to_dve.bank("out", back)[:, t * D:(t + 1) * D],
                                                       hidden[0:rows, n, t * P:(t + 1) * P],
                                                       w["w2"][0:rows, layer, n, :],
                                                       start=n == 0, stop=n == len(CHUNKS) - 1)
                        ins.then_inc(to_dve.filled.sem, 1)

                pipeline(pe, n_seq, step)


def ffn_layers(nc, n_seq, x, w, c):
    with nc.sbuf_tensor("z", [P, n_seq * TILES, D], F32) as z:
        for layer in range(LAYERS):
            window_attention(nc, n_seq, x, z, w, c, layer)
            gated_mlp(nc, n_seq, x, z, w, c, layer)


LH, LD = 16, 64


def latent_attention(nc, n_seq, x, w, c):
    pairs = LH * LD // P
    row_jobs = [f"i1.{n}" for n in range(8)] + [f"i0.{n}" for n in range(4)]
    col_jobs = [f"{kind}.{n}" for q in range(4) for kind, n in (("j0", 2 * q), ("j0", 2 * q + 1), ("j1", q))]
    av_jobs = [f"av{t}.{q}" for q in range(4) for t in range(TILES)]
    act_front = ["xnT", "latT", "q0", "q1", "q2", "q3", "v0.0", "v0.1", "v1.0"]
    dve_front = ["k0", "k1", "k2", "k3", "v1.1"]
    act_order = act_front + ["shift"] + col_jobs + ["yT0", "yT1", "yT2", "yT3"]
    dve_order = row_jobs + dve_front + av_jobs + ["out"]

    def heads(kind, n):
        if kind in ("i1", "j0"):
            return [4 * (n // 2) + n % 2 + 2 * i for i in range(2)]
        return [8 * (n // 2) + n % 2 + 2 * i for i in range(4)]

    with ExitStack() as ctx:
        def sb(name, shape, dt=F32):
            return ctx.enter_context(nc.sbuf_tensor("l_" + name, shape, dt))

        def sem(name):
            return ctx.enter_context(nc.semaphore("l_" + name))

        qT = [sb(f"qT{u}", [P, pairs, T]) for u in range(2)]
        kT = [sb(f"kT{u}", [P, pairs, T]) for u in range(2)]
        v = [sb(f"v{u}", [P, TILES, LH, LD + 1]) for u in range(2)]
        xnT = sb("xnT", [P, T])
        latT = sb("latT", [P, T])
        neg_max = sb("neg_max", [P, TILES, LH])
        neg2 = sb("neg2", [P, TILES, 2 * LH])
        negT = sb("negT", [2 * LH, T], F32R)
        p0 = sb("p0", [P, LH, T])
        p1 = sb("p1", [P, LH, P])
        rden = sb("rden", [P, TILES, LH])
        y = sb("y", [P, TILES, LH * LD])
        yT = sb("yT", [P, pairs, T])
        act_banks = [ctx.enter_context(nc.psum_tensor(f"l_act{i}", [P, BANK], F32)) for i in range(RING)]
        dve_banks = [ctx.enter_context(nc.psum_tensor(f"l_dve{i}", [P, BANK], F32)) for i in range(RING)]
        to_act = Ring(act_banks, sem("act_filled"), sem("act_drained"), act_order, act_front)
        to_dve = Ring(dve_banks, sem("dve_filled"), sem("dve_drained"), dve_order, dve_front)
        vec = Count(sem("vec"), ["neg_hi", "neg_lo"] + PRE_NORM
                    + [f"rden{t}.{q}" for q in range(4) for t in range(TILES)] + POST_NORM, PRE_NORM)
        rst = Count(sem("rst"), RSQRT, RSQRT[:2])
        norm = Norm(nc, ctx, "l_", vec, rst, c)
        ones_set = sem("ones_set")

        with nc.Block() as block:
            @block.gpsimd
            def _(pool):
                for u in range(2):
                    nc.gpsimd.memset(v[u][:, :, :, LD:LD + 1], 1.0).then_inc(ones_set, 1)

                def step(front, back):
                    if front:
                        norm.rsqrt(pool, "", front)
                    if back:
                        norm.rsqrt(pool, "y", back)

                pipeline(pool, n_seq, step)

            @block.vector
            def _(dve):
                def step(front, back):
                    if back:
                        for job in row_jobs:
                            kind, n = job.split(".")
                            hs, t = heads(kind, int(n)), int(kind[1])
                            to_dve.wait_filled(dve, job, back)
                            nc.vector.tensor_reduce(
                                neg_max[:, t, hs[0]:hs[-1] + 1:2],
                                to_dve.bank(job, back)[:, :].rearrange("p (h j) -> p h j", h=len(hs)),
                                AX.X, ALU.max, negate=True).then_inc(to_dve.drained.sem, 1)
                        to_dve.wait_drained(dve, row_jobs[-1], back)
                        nc.vector.tensor_copy(neg2[:, :, 0:LH].bitcast(F32R), neg_max[:, :, :])\
                            .then_inc(vec.sem, 1)
                        dve.wait_ge(vec.sem, vec.done("neg_hi", back))
                        nc.vector.tensor_tensor(neg2[:, :, LH:2 * LH], neg_max[:, :, :], neg2[:, :, 0:LH],
                                                ALU.subtract).then_inc(vec.sem, 1)
                    if front:
                        norm.pre(dve, front, x, to_act)
                        u = front.parity
                        for n in range(4):
                            to_dve.wait_filled(dve, f"k{n}", front)
                            nc.vector.tensor_copy(
                                kT[u][:, 2 * n:2 * n + 2, :].rearrange("p a t -> p (a t)"),
                                to_dve.bank(f"k{n}", front)[:, :]).then_inc(to_dve.drained.sem, 1)
                        to_dve.wait_filled(dve, "v1.1", front)
                        nc.vector.tensor_copy(
                            v[u][:, 1, 8:16, 0:LD],
                            to_dve.bank("v1.1", front)[:, :].rearrange("p (h d) -> p h d", h=8))\
                            .then_inc(to_dve.drained.sem, 1)
                    if back:
                        for job in av_jobs:
                            t, q = int(job[2]), int(job[4])
                            o = to_dve.bank(job, back)[:, 0:4 * (LD + 1)].rearrange("p (h d) -> p h d", h=4)
                            to_dve.wait_filled(dve, job, back)
                            nc.vector.reciprocal(rden[:, t, 4 * q:4 * q + 4], o[:, :, LD])\
                                .then_inc(vec.sem, 1)
                            dve.wait_ge(vec.sem, vec.done(f"rden{t}.{q}", back))
                            nc.vector.tensor_tensor(
                                y[:, t, 256 * q:256 * q + 256].rearrange("p (h d) -> p h d", h=4),
                                o[:, :, 0:LD],
                                rden[:, t, 4 * q:4 * q + 4].unsqueeze(2).broadcast_to((P, 4, LD)),
                                ALU.mult).then_inc(to_dve.drained.sem, 1)
                        norm.post(dve, back, x, to_dve, "out")

                pipeline(dve, n_seq, step)

            @block.scalar
            def _(act):
                def step(front, back):
                    if front:
                        u = front.parity
                        for job, out in (("xnT", xnT), ("latT", latT)):
                            to_act.wait_filled(act, job, front)
                            nc.scalar.copy(out[:, :], to_act.bank(job, front)[:, 0:T])\
                                .then_inc(to_act.drained.sem, 1)
                        for n in range(4):
                            to_act.wait_filled(act, f"q{n}", front)
                            nc.scalar.mul(qT[u][:, 2 * n:2 * n + 2, :].rearrange("p a t -> p (a t)"),
                                          to_act.bank(f"q{n}", front)[:, :], LD ** -0.5)\
                                .then_inc(to_act.drained.sem, 1)
                        for t, half in ((0, 0), (0, 1), (1, 0)):
                            job = f"v{t}.{half}"
                            to_act.wait_filled(act, job, front)
                            nc.scalar.copy(v[u][:, t, 8 * half:8 * half + 8, 0:LD],
                                           to_act.bank(job, front)[:, :].rearrange("p (h d) -> p h d", h=8))\
                                .then_inc(to_act.drained.sem, 1)
                    if back:
                        to_act.wait_filled(act, "shift", back)
                        nc.scalar.copy(negT[:, :], to_act.bank("shift", back)[0:2 * LH, 0:T])\
                            .then_inc(to_act.drained.sem, 1)
                        for job in col_jobs:
                            kind, n = job.split(".")
                            hs = heads(kind, int(n))
                            probs = p0 if kind == "j0" else p1
                            to_act.wait_filled(act, job, back)
                            nc.scalar.activation(
                                probs[:, hs[0]:hs[-1] + 1:2, :],
                                to_act.bank(job, back)[:, :].rearrange("p (h j) -> p h j", h=len(hs)),
                                ACT.Exp).then_inc(to_act.drained.sem, 1)
                        for n in range(4):
                            to_act.wait_filled(act, f"yT{n}", back)
                            nc.scalar.copy(yT[:, 2 * n:2 * n + 2, :].rearrange("p a t -> p (a t)"),
                                           to_act.bank(f"yT{n}", back)[:, :])\
                                .then_inc(to_act.drained.sem, 1)

                pipeline(act, n_seq, step)

            @block.tensor
            def _(pe):
                pe.wait_ge(ones_set, 2)

                def step(front, back):
                    if back:
                        u = back.parity
                        to_act.wait_drained(pe, "v1.0", back)
                        to_dve.wait_drained(pe, "v1.1", back)
                        for job in row_jobs:
                            kind, n = job.split(".")
                            t = int(kind[1])
                            width = P * (t + 1)
                            bank = to_dve.bank(job, back)
                            to_dve.wait_free(pe, job, back)
                            for i, h in enumerate(heads(kind, int(n))):
                                rows = slice(LD * (h % 2), LD * (h % 2) + LD)
                                nc.tensor.matmul(bank[:, width * i:width * i + width],
                                                 qT[u][rows, h // 2, P * t:P * t + P],
                                                 kT[u][rows, h // 2, 0:width], start=True, stop=False)
                                ins = nc.tensor.matmul(bank[:, width * (i + 1) - P:width * (i + 1)],
                                                       c["ident_bf"][:, :], c["mask_rows"][:, :],
                                                       start=False, stop=True)
                            ins.then_inc(to_dve.filled.sem, 1)
                    if front:
                        u = front.parity
                        to_act.wait_free(pe, "xnT", front)
                        for t in range(TILES):
                            pe.wait_ge(vec.sem, vec.done(f"xn{t}", front))
                            ins = nc.tensor.transpose(to_act.bank("xnT", front)[:, t * P:(t + 1) * P],
                                                      norm.xn[:, t], c["ident"][:, :])
                        ins.then_inc(to_act.filled.sem, 1)
                        to_act.wait_free(pe, "latT", front)
                        to_act.wait_drained(pe, "xnT", front)
                        nc.tensor.matmul(to_act.bank("latT", front)[:, 0:T], w["kv_down"][:, :], xnT[:, :],
                                         start=True, stop=True).then_inc(to_act.filled.sem, 1)
                        for n in range(4):
                            to_act.wait_free(pe, f"q{n}", front)
                            for i in range(2):
                                pair = 2 * n + i
                                ins = nc.tensor.matmul(to_act.bank(f"q{n}", front)[:, i * T:(i + 1) * T],
                                                       w["q"][:, pair * P:(pair + 1) * P], xnT[:, :],
                                                       start=True, stop=True)
                            ins.then_inc(to_act.filled.sem, 1)
                        to_act.wait_drained(pe, "latT", front)
                        for n in range(4):
                            to_dve.wait_free(pe, f"k{n}", front)
                            for i in range(2):
                                pair = 2 * n + i
                                ins = nc.tensor.matmul(to_dve.bank(f"k{n}", front)[:, i * T:(i + 1) * T],
                                                       w["kv_up"][:, pair * P:(pair + 1) * P], latT[:, :],
                                                       start=True, stop=True)
                            ins.then_inc(to_dve.filled.sem, 1)
                        for t in range(TILES):
                            for half in range(2):
                                job = f"v{t}.{half}"
                                ring = to_dve if job == "v1.1" else to_act
                                ring.wait_free(pe, job, front)
                                at = LH * LD + BANK * half
                                nc.tensor.matmul(ring.bank(job, front)[:, :], latT[:, t * P:(t + 1) * P],
                                                 w["kv_up"][:, at:at + BANK], start=True, stop=True)\
                                    .then_inc(ring.filled.sem, 1)
                    if back:
                        u = back.parity
                        to_act.wait_free(pe, "shift", back)
                        pe.wait_ge(vec.sem, vec.done("neg_lo", back))
                        for t in range(TILES):
                            ins = nc.tensor.transpose(to_act.bank("shift", back)[0:2 * LH, t * P:(t + 1) * P],
                                                      neg2[:, t], c["ident"][:, :])
                        ins.then_inc(to_act.filled.sem, 1)

                        def col_scores(job):
                            kind, n = job.split(".")
                            j = int(kind[1])
                            width = T - P * j
                            bank = to_act.bank(job, back)
                            to_act.wait_free(pe, job, back)
                            for i, h in enumerate(heads(kind, int(n))):
                                rows = slice(LD * (h % 2), LD * (h % 2) + LD)
                                out = bank[:, width * i:width * i + width]
                                nc.tensor.matmul(out, kT[u][rows, h // 2, P * j:P * j + P],
                                                 qT[u][rows, h // 2, P * j:T], start=True, stop=False)
                                nc.tensor.matmul(out, c["pick"][:, h * P:(h + 1) * P], negT[:, P * j:T],
                                                 start=False, stop=False)
                                ins = nc.tensor.matmul(bank[:, width * i:width * i + P],
                                                       c["ident_bf"][:, :], c["mask_cols"][:, :],
                                                       start=False, stop=True)
                            ins.then_inc(to_act.filled.sem, 1)

                        def attend(q):
                            if q % 2 == 0:
                                to_act.wait_drained(pe, f"j1.{q + 1}", back)
                            for t in range(TILES):
                                job = f"av{t}.{q}"
                                to_dve.wait_free(pe, job, back)
                                for i in range(4):
                                    h = 4 * q + i
                                    out = to_dve.bank(job, back)[:, (LD + 1) * i:(LD + 1) * (i + 1)]
                                    ins = nc.tensor.matmul(out, p0[:, h, t * P:(t + 1) * P], v[u][:, 0, h, :],
                                                           start=True, stop=t == 0)
                                    if t == 1:
                                        ins = nc.tensor.matmul(out, p1[:, h, :], v[u][:, 1, h, :],
                                                               start=False, stop=True)
                                ins.then_inc(to_dve.filled.sem, 1)

                        to_act.wait_drained(pe, "shift", back)
                        for job in col_jobs[0:6]:
                            col_scores(job)
                        for job in col_jobs[6:9]:
                            col_scores(job)
                        attend(0)
                        for job in col_jobs[9:12]:
                            col_scores(job)
                        for q in range(1, 4):
                            attend(q)
                        for n in range(4):
                            to_act.wait_free(pe, f"yT{n}", back)
                            to_dve.wait_drained(pe, f"av1.{n}", back)
                            for i in range(2):
                                for t in range(TILES):
                                    pair = 2 * n + i
                                    ins = nc.tensor.transpose(
                                        to_act.bank(f"yT{n}", back)[:, i * T + t * P:i * T + (t + 1) * P],
                                        y[:, t, pair * P:(pair + 1) * P], c["ident"][:, :])
                            ins.then_inc(to_act.filled.sem, 1)
                        to_dve.wait_free(pe, "out", back)
                        to_act.wait_drained(pe, "yT3", back)
                        for t in range(TILES):
                            for pair in range(pairs):
                                ins = nc.tensor.matmul(to_dve.bank("out", back)[:, t * D:(t + 1) * D],
                                                       yT[:, pair, t * P:(t + 1) * P], w["l_out"][:, pair, :],
                                                       start=pair == 0, stop=pair == pairs - 1)
                        ins.then_inc(to_dve.filled.sem, 1)

                pipeline(pe, n_seq, step)


EXPERTS, EF = 8, 256
NOT_A_LOGIT, TAKEN = -3.0e38, 3.0e38


def experts_layer(nc, n_seq, x, w, c, out_dram, finished):
    act_front, dve_front = ["xnT"], ["router"]
    act_order = act_front + [f"h{e}" for e in range(EXPERTS)]
    dve_order = dve_front + [f"y{t}.{g}" for g in range(2) for t in range(TILES)]
    route = ["best0", "best1", "pair", "rest0", "rest1", "chosen", "first0", "first1",
             "second", "mix0", "mix1", "weight"]
    sums = [f"sum{e}.{t}" for e in range(EXPERTS) if e % 4 < 3 for t in range(TILES)]

    with ExitStack() as ctx:
        def sb(name, shape, dt=F32):
            return ctx.enter_context(nc.sbuf_tensor("e_" + name, shape, dt))

        def sem(name):
            return ctx.enter_context(nc.semaphore("e_" + name))

        xnT = [sb(f"xnT{u}", [P, T]) for u in range(2)]
        hT = sb("hT", [P, 2, EF // P, T])
        logits = sb("logits", [P, TILES, 2 * EXPERTS])
        best = sb("best", [P, TILES, 8])
        pair = sb("pair", [P, TILES, 8])
        rest = sb("rest", [P, TILES, 2 * EXPERTS])
        diff = sb("diff", [P, TILES])
        lead = sb("lead", [P, TILES])
        second = sb("second", [P, TILES])
        chosen = sb("chosen", [P, TILES, EXPERTS])
        first = sb("first", [P, TILES, EXPERTS])
        weight = [sb(f"weight{u}", [P, TILES, EXPERTS]) for u in range(2)]
        acc = sb("acc", [P, TILES, D])
        act_banks = [ctx.enter_context(nc.psum_tensor(f"e_act{i}", [P, BANK], F32)) for i in range(3)]
        dve_banks = [ctx.enter_context(nc.psum_tensor(f"e_dve{i}", [P, BANK], F32)) for i in range(5)]
        to_act = Ring(act_banks, sem("act_filled"), sem("act_drained"), act_order, act_front)
        to_dve = Ring(dve_banks, sem("dve_filled"), sem("dve_drained"), dve_order, dve_front)
        vec = Count(sem("vec"), PRE_NORM + route + sums + ["ystats0", "ystats1", "ymv0", "ymv1", "yn0", "yn1"],
                    PRE_NORM + route)
        rst = Count(sem("rst"), RSQRT, RSQRT[:2])
        lead_done = Count(sem("lead_done"), ["diff", "lead"], ["diff", "lead"])
        updated = Count(sem("updated"), ["x"], [])
        norm = Norm(nc, ctx, "e_", vec, rst, c)
        setup = sem("setup")

        with nc.Block() as block:
            @block.gpsimd
            def _(pool):
                nc.gpsimd.memset(logits[:, :, EXPERTS:], NOT_A_LOGIT).then_inc(setup, 1)
                nc.gpsimd.memset(pair[:, :, 2:], NOT_A_LOGIT).then_inc(setup, 1)

                def step(front, back):
                    if front:
                        norm.rsqrt(pool, "", front)
                        pool.wait_ge(vec.sem, vec.done("best1", front))
                        nc.gpsimd.tensor_tensor(diff[:, :], best[:, :, 0], best[:, :, 1], ALU.subtract)\
                            .then_inc(lead_done.sem, 1)
                    if back:
                        norm.rsqrt(pool, "y", back)

                pipeline(pool, n_seq, step)

            @block.vector
            def _(dve):
                dve.wait_ge(setup, 2)

                def step(front, back):
                    if front:
                        norm.pre(dve, front, x, to_act)
                        to_dve.wait_filled(dve, "router", front)
                        got = to_dve.bank("router", front)[:, 0:TILES * EXPERTS]
                        nc.vector.tensor_copy(logits[:, :, 0:EXPERTS],
                                              got.rearrange("p (a e) -> p a e", a=TILES))\
                            .then_inc(to_dve.drained.sem, 1)
                        wait_apart(nc, dve, c, to_dve.drained.sem, to_dve.drained.done("router", front))
                        for t in range(TILES):
                            nc.vector.max(best[:, t, :], logits[:, t, 0:EXPERTS]).then_inc(vec.sem, 1)
                        dve.wait_ge(vec.sem, vec.done("best1", front))
                        nc.vector.tensor_copy(pair[:, :, 0:2], best[:, :, 0:2]).then_inc(vec.sem, 1)
                        wait_apart(nc, dve, c, vec.sem, vec.done("pair", front))
                        for t in range(TILES):
                            nc.vector.match_replace(rest[:, t, :], pair[:, t, :], logits[:, t, :], TAKEN)\
                                .then_inc(vec.sem, 1)
                        dve.wait_ge(vec.sem, vec.done("rest1", front))
                        nc.vector.tensor_scalar(chosen[:, :, :], rest[:, :, 0:EXPERTS], TAKEN, None,
                                                ALU.is_equal).then_inc(vec.sem, 1)
                        dve.wait_ge(lead_done.sem, lead_done.done("lead", front))
                        for t in range(TILES):
                            nc.vector.tensor_scalar(first[:, t, :], logits[:, t, 0:EXPERTS],
                                                    best[:, t, 0:1], lead[:, t:t + 1],
                                                    ALU.is_equal, ALU.mult).then_inc(vec.sem, 1)
                        nc.vector.tensor_scalar(second[:, :], lead[:, :], -0.5, 0.5, ALU.mult, ALU.add)\
                            .then_inc(vec.sem, 1)
                        dve.wait_ge(vec.sem, vec.done("second", front))
                        for t in range(TILES):
                            nc.vector.tensor_scalar(first[:, t, :], first[:, t, :], second[:, t:t + 1],
                                                    None, ALU.add).then_inc(vec.sem, 1)
                        dve.wait_ge(vec.sem, vec.done("mix1", front))
                        nc.vector.tensor_tensor(weight[front.parity][:, :, :], first[:, :, :],
                                                chosen[:, :, :], ALU.mult).then_inc(vec.sem, 1)
                    if back:
                        u = back.parity
                        for e in range(EXPERTS):
                            g = e // 4
                            for t in range(TILES):
                                if e % 4 == 0:
                                    to_dve.wait_filled(dve, f"y{t}.{g}", back)
                                bank = to_dve.bank(f"y{t}.{g}", back)
                                y = bank[:, (e % 4) * D:(e % 4 + 1) * D]
                                cw = weight[u][:, t, e:e + 1]
                                if e == 0:
                                    ins = nc.vector.tensor_scalar(acc[:, t], y, cw, None, ALU.mult)
                                else:
                                    if e % 4 == 0:
                                        to_dve.wait_drained(dve, f"y{t}.{g - 1}", back)
                                    else:
                                        dve.wait_ge(vec.sem, vec.done(f"sum{e - 1}.{t}", back))
                                    ins = nc.vector.scalar_tensor_tensor(acc[:, t], y, cw, acc[:, t],
                                                                         ALU.mult, ALU.add)
                                ins.then_inc(to_dve.drained.sem if e % 4 == 3 else vec.sem, 1)
                        wait_apart(nc, dve, c, to_dve.drained.sem, to_dve.drained.done("y1.1", back))
                        norm.moments(dve, "y", back, [acc[:, t] for t in range(TILES)])
                        dve.wait_ge(rst.sem, rst.done("yrstd", back))
                        for t in range(TILES):
                            norm.scaled("y", t, norm.yn[:, t], acc[:, t]).then_inc(vec.sem, 1)
                        dve.wait_ge(vec.sem, vec.done("yn1", back))
                        nc.vector.tensor_tensor(back.tiles(x), back.tiles(x), norm.yn[:, :, :], ALU.add)\
                            .then_inc(updated.sem, 1)

                pipeline(dve, n_seq, step)

            @block.scalar
            def _(act):
                def step(front, back):
                    if front:
                        to_act.wait_filled(act, "xnT", front)
                        nc.scalar.copy(xnT[front.parity][:, :], to_act.bank("xnT", front)[:, 0:T])\
                            .then_inc(to_act.drained.sem, 1)
                        act.wait_ge(lead_done.sem, lead_done.done("diff", front))
                        nc.scalar.activation(lead[:, :], diff[:, :], ACT.Tanh, scale=0.5)\
                            .then_inc(lead_done.sem, 1)
                    if back:
                        for e in range(EXPERTS):
                            to_act.wait_filled(act, f"h{e}", back)
                            nc.scalar.activation(hT[:, e % 2, :, :].rearrange("p a t -> p (a t)"),
                                                 to_act.bank(f"h{e}", back)[:, :], ACT.Silu)\
                                .then_inc(to_act.drained.sem, 1)

                pipeline(act, n_seq, step)

            @block.tensor
            def _(pe):
                def step(front, back):
                    if front:
                        to_act.wait_free(pe, "xnT", front)
                        for t in range(TILES):
                            pe.wait_ge(vec.sem, vec.done(f"xn{t}", front))
                            ins = nc.tensor.transpose(to_act.bank("xnT", front)[:, t * P:(t + 1) * P],
                                                      norm.xn[:, t], c["ident"][:, :])
                        ins.then_inc(to_act.filled.sem, 1)
                        to_act.wait_drained(pe, "xnT", front)
                        to_dve.wait_free(pe, "router", front)
                        for t in range(TILES):
                            ins = nc.tensor.matmul(
                                to_dve.bank("router", front)[:, t * EXPERTS:(t + 1) * EXPERTS],
                                xnT[front.parity][:, t * P:(t + 1) * P], w["router"][:, :],
                                start=True, stop=True)
                        ins.then_inc(to_dve.filled.sem, 1)
                    if back:
                        u = back.parity

                        def hidden(e):
                            to_act.wait_free(pe, f"h{e}", back)
                            for f in range(EF // P):
                                ins = nc.tensor.matmul(to_act.bank(f"h{e}", back)[:, f * T:(f + 1) * T],
                                                       w["e1"][:, e, f * P:(f + 1) * P], xnT[u][:, :],
                                                       start=True, stop=True)
                            ins.then_inc(to_act.filled.sem, 1)

                        def output(e):
                            to_act.wait_drained(pe, f"h{e}", back)
                            for t in range(TILES):
                                job = f"y{t}.{e // 4}"
                                if e % 4 == 0:
                                    to_dve.wait_free(pe, job, back)
                                for f in range(EF // P):
                                    ins = nc.tensor.matmul(
                                        to_dve.bank(job, back)[:, (e % 4) * D:(e % 4 + 1) * D],
                                        hT[:, e % 2, f, t * P:(t + 1) * P], w["e2"][:, e, f, :],
                                        start=f == 0, stop=f == EF // P - 1)
                                if e % 4 == 3:
                                    ins.then_inc(to_dve.filled.sem, 1)

                        hidden(0)
                        for e in range(1, EXPERTS):
                            hidden(e)
                            output(e - 1)
                        output(EXPERTS - 1)

                pipeline(pe, n_seq, step)

            @block.sync
            def _(sp):
                with sp.Fori(0, n_seq) as s:
                    sp.wait_ge(updated.sem, s + 1)
                    sp.dma_start(out_dram[:, bass.ds(s * TILES, TILES), :], x[:, bass.ds(s * TILES, TILES), :])\
                        .then_inc(finished, 16)
                sp.wait_ge(finished, 16 * n_seq)


def load(nc, name, pairs):
    with nc.semaphore(name) as loaded, nc.Block() as block:
        @block.sync
        def _(sp):
            for out, source in pairs:
                sp.dma_start(out, source).then_inc(loaded, 16)
            sp.wait_ge(loaded, 16 * len(pairs))


def chip_constants(nc, ctx, d):
    def sb(name, shape, dt=F32):
        return ctx.enter_context(nc.sbuf_tensor(name, shape, dt))

    c = {
        "ident": sb("ident_sb", [P, P]),
        "ident_bf": sb("ident_bf", [P, P], BF16),
        "mask_rows": sb("mask_rows", [P, P], BF16),
        "mask_cols": sb("mask_cols", [P, P], BF16),
        "mask_window": sb("mask_window", [P, SPAN], BF16),
        "pick": sb("pick_sb", [2 * LH, LH * P], F32R),
        "pick8": sb("pick8_sb", [2 * NH, NH * P], F32R),
        "next": sb("next_sb", [P, 2, P]),
        "minus_half": sb("minus_half", [P, 16]),
        "eps": sb("eps", [P, TILES]),
        "carrier": sb("carrier", [P, 1]),
    }
    with ExitStack() as staging:
        def st(name, shape):
            return staging.enter_context(nc.sbuf_tensor(name, shape, F32))

        masks, window = st("masks_f32", [P, 2, P]), st("window_f32", [P, SPAN])
        pick, pick8 = st("pick_f32", [2 * LH, LH * P]), st("pick8_f32", [2 * NH, NH * P])
        ready = c["ready"] = ctx.enter_context(nc.semaphore("constants_ready"))
        load(nc, "constants_loaded", [
            (c["ident"][:, :], d["ident"]), (c["next"][:, :, :], d["next_mat"]),
            (masks[:, :, :], d["masks"]), (window[:, :], d["window_mat"]),
            (pick[:, :], d["pick"]), (pick8[:, :], d["pick8_mat"])])
        with nc.Block() as block:
            @block.vector
            def _(dve):
                for out, source in ((c["ident_bf"], c["ident"][:, :]), (c["mask_rows"], masks[:, 0]),
                                    (c["mask_cols"], masks[:, 1]), (c["mask_window"], window[:, :]),
                                    (c["pick"], pick[:, :]), (c["pick8"], pick8[:, :])):
                    nc.vector.tensor_copy(out[:, :], source).then_inc(ready, 1)
                nc.vector.memset(c["minus_half"][:, :], -0.5).then_inc(ready, 1)
                nc.vector.memset(c["eps"][:, :], LN_EPS).then_inc(ready, 1)
                dve.wait_ge(ready, 8)
    return c


def build(nc, n_seq, d, phases=None):
    with ExitStack() as ctx:
        x = ctx.enter_context(nc.sbuf_tensor("x_sb", [P, n_seq * TILES, D], F32))
        c = chip_constants(nc, ctx, d)
        finished = ctx.enter_context(nc.semaphore("finished"))

        with ExitStack() as scope:
            def sb(name, shape, dt=F32):
                return scope.enter_context(nc.sbuf_tensor(name + "_sb", shape, dt))

            w = {
                "tq": sb("tq", [D, GROUPS, P]),
                "tk": sb("tk", [D, GROUPS, P]),
                "tv": sb("tv", [D, D]),
                "t_out": sb("t_out", [D, D]),
                "bits": sb("bits", [D, P]),
                "basis": sb("basis", [8, 2 * BITS, 2 * BITS]),
                "transform": sb("transform", [TH, NT]),
                "scalars": sb("scalars", [P, 4]),
            }
            load(nc, "token_loaded", [
                (x[:, :, :], d["x"].rearrange("(n p) d -> p n d", p=P)),
                *((w[name][:], d[name]) for name in list(w)[:-1]),
                (w["scalars"][:, :], d["scalars"].partition_broadcast(P))])
            token_attention(nc, n_seq, x, w, c)

        with ExitStack() as scope:
            def sb(name, shape, dt=F32):
                return scope.enter_context(nc.sbuf_tensor(name + "_sb", shape, dt))

            c["rotary"] = sb("rotary", [P, TILES, 4, HD])
            w = {
                "wqkv": sb("wqkv", [D, LAYERS, 3 * INNER]),
                "wo": sb("wo", [P, LAYERS, INNER // P, D]),
                "w1": sb("w1", [D, LAYERS, 2 * HID]),
                "w2": sb("w2", [P, LAYERS, 3, D]),
                "b1": sb("b1", [P, LAYERS, 2, 3]),
                "ln_g": sb("ln_g", [D, LAYERS]),
                "ln_b": sb("ln_b", [D, LAYERS]),
                "q_scale": sb("q_scale", [P, LAYERS, HD]),
                "k_scale": sb("k_scale", [P, LAYERS, HD]),
            }
            pairs = [(c["rotary"][:], d["rotary_tab"])]
            pairs += [(w[name][:], d[name]) for name in ("w2", "b1", "ln_g", "ln_b")]
            for layer in range(LAYERS):
                pairs += [
                    (w["wqkv"][:, layer], d["L0_ffn_wqkv"][layer]),
                    (w["wo"][:, layer], d["L0_ffn_wo"][layer].rearrange("(a p) n -> p a n", p=P)),
                    (w["w1"][:, layer], d["L0_ffn_w1"][layer]),
                    (w["q_scale"][:, layer], d["L0_ffn_q_scale"][layer].partition_broadcast(P)),
                    (w["k_scale"][:, layer], d["L0_ffn_k_scale"][layer].partition_broadcast(P))]
            load(nc, "ffn_loaded", pairs)
            ffn_layers(nc, n_seq, x, w, c)

        with ExitStack() as scope:
            def sb(name, shape, dt=F32):
                return scope.enter_context(nc.sbuf_tensor(name + "_sb", shape, dt))

            w = {
                "kv_down": sb("kv_down", [D, D]),
                "kv_up": sb("kv_up", [D, 2 * LH * LD]),
                "q": sb("wq", [D, LH * LD]),
                "l_out": sb("l_out", [P, LH * LD // P, D]),
            }
            load(nc, "latent_loaded", [
                (w["kv_down"][:, :], d["L1_attn_w_kv_down"]), (w["kv_up"][:, :], d["L1_attn_w_kv_up"]),
                (w["q"][:, :], d["L1_attn_w_q"]),
                (w["l_out"][:, :, :], d["L1_attn_w_out"].rearrange("(c p) n -> p c n", p=P))])
            latent_attention(nc, n_seq, x, w, c)

        with ExitStack() as scope:
            def sb(name, shape, dt=F32):
                return scope.enter_context(nc.sbuf_tensor(name + "_sb", shape, dt))

            w = {
                "router": sb("router", [D, EXPERTS]),
                "e1": sb("e1", [D, EXPERTS, EF]),
                "e2": sb("e2", [P, EXPERTS, EF // P, D]),
            }
            load(nc, "experts_loaded", [
                (w["router"][:, :], d["L1_ffn_router_w"]),
                (w["e1"][:, :, :], d["L1_ffn_w1"].rearrange("e d f -> d e f")),
                *((w["e2"][:, e], d["L1_ffn_w2"][e].rearrange("(a p) n -> p a n", p=P))
                  for e in range(EXPERTS))])
            experts_layer(nc, n_seq, x, w, c, d["out"].rearrange("(n p) d -> p n d", p=P), finished)


def constants():
    f32 = np.float32
    row, col = np.arange(P)[:, None], np.arange(P)[None]
    causal = np.where(col > row, MASKED, 0.0).astype(f32)
    window = np.arange(SPAN)[None]

    def picker(heads):
        out = np.zeros((2, heads, heads, P), f32)
        for h in range(heads):
            out[:, h, h] = 1.0
        return out.reshape(2 * heads, heads * P)

    half = np.arange(0, HD, 2, dtype=f32)
    inv_freq = (1.0 / 10000.0 ** (half / HD)).astype(f32)
    angle = (np.arange(T, dtype=f32)[:, None] * inv_freq[None]).astype(f32)
    angle = np.concatenate([angle, angle], -1).astype(np.float64)
    base = (half.astype(np.float64) + 0.4 * HD) / (1.4 * HD)
    scale = base[None] ** ((np.arange(T) - T // 2) / float(WINDOW // 2))[:, None]
    scale = np.concatenate([scale, scale], -1)
    sign = np.where(np.arange(HD) < HD // 2, -1.0, 1.0)
    cos, sin = np.cos(angle), np.sin(angle) * sign
    rotary = np.stack([cos * scale, sin * scale, cos / scale, sin / scale], 1)

    following = np.zeros((P, 2, P), f32)
    following[np.arange(P - 1), 0, np.arange(1, P)] = 1.0
    following[P - 1, 1, 0] = 1.0
    return {
        "ident": np.eye(P, dtype=f32),
        "masks": np.ascontiguousarray(np.stack([causal, causal.T], 1)),
        "pick": picker(LH),
        "pick8_mat": picker(NH),
        "window_mat": np.where((window >= row) & (window <= row + WINDOW), 0.0, MASKED).astype(f32),
        "rotary_tab": np.ascontiguousarray(
            rotary.reshape(TILES, P, 4, HD).transpose(1, 0, 2, 3)).astype(f32),
        "next_mat": following,
    }


def layouts(a):
    f32 = np.float32
    qkv = a["L0_attn_qkv_w"].reshape(3, TH, TD, D)

    def grouped(weights):
        out = np.zeros((D, GROUPS, GROUPS, ROWS), f32)
        out[..., :TD] = weights.reshape(GROUPS, GROUPS, TD, D).transpose(3, 0, 1, 2)
        return out.reshape(D, GROUPS, P)

    bits = np.zeros((D, GROUPS, ROWS), f32)
    bits[..., :BITS] = a["L0_attn_hex_w"].T[:, None]
    bits[..., BITS:2 * BITS] = a["L0_attn_q6_w"].T[:, None]
    basis = np.zeros((NT + 1, 2 * BITS, 2 * BITS), f32)
    basis[:NT, BITS:, BITS:] = a["L0_attn_transforms"].transpose(0, 2, 1)
    basis[NT, np.arange(BITS), np.arange(BITS)] = 1.0

    w2 = np.zeros((P, LAYERS, 3, D), f32)
    b1 = np.zeros((P, LAYERS, 2, 3), f32)
    at = 0
    for n, rows in enumerate(CHUNKS):
        w2[:rows, :, n] = a["L0_ffn_w2"][:, at:at + rows].transpose(1, 0, 2)
        for part in range(2):
            b1[:rows, :, part, n] = a["L0_ffn_b1"][:, part * HID + at:part * HID + at + rows].T
        at += rows
    w2[CHUNKS[-1], :, 2] = a["L0_ffn_b2"]
    out = {
        "x": a["L0_attn_x"].reshape(-1, D),
        "tq": grouped(qkv[0]), "tk": grouped(qkv[1]), "tv": qkv[2].reshape(TH * TD, D).T,
        "t_out": a["L0_attn_out_w"].T,
        "bits": bits.reshape(D, P), "basis": basis,
        "transform": a["L0_attn_transform_weights"],
        "scalars": np.concatenate([a["L0_attn_hamming_lambda_logit"].reshape(1),
                                   a["L0_attn_scale_logit"].reshape(1),
                                   a["L0_attn_sips_alpha"], a["L0_attn_sips_beta"]]),
        "w2": w2, "b1": b1, "ln_g": a["L0_ffn_ln_g"].T, "ln_b": a["L0_ffn_ln_b"].T,
    }
    for name in ("L0_ffn_wqkv", "L0_ffn_wo", "L0_ffn_w1", "L0_ffn_q_scale", "L0_ffn_k_scale",
                 "L1_attn_w_kv_down", "L1_attn_w_kv_up", "L1_attn_w_q", "L1_attn_w_out",
                 "L1_ffn_router_w", "L1_ffn_w1", "L1_ffn_w2"):
        out[name] = a[name]
    return {k: np.ascontiguousarray(v) for k, v in out.items()}


def kernel(**inputs):
    import concourse.bacc as bacc
    from concourse.bass_utils import run_bass_kernel_spmd

    given = {k: np.asarray(v) for k, v in inputs.items()}
    n_seq = given["L0_attn_x"].shape[0]
    arrays = {**constants(), **layouts(given)}
    nc = bacc.Bacc("TRN2", target_bir_lowering=False, num_devices=1)
    dram = {k: nc.dram_tensor(k, v.shape, F32, kind="ExternalInput").ap() for k, v in arrays.items()}
    dram["out"] = nc.dram_tensor("out", (n_seq * T, D), F32, kind="ExternalOutput").ap()
    build(nc, n_seq, dram)
    result = run_bass_kernel_spmd(nc, [arrays], core_ids=[0])
    return result.results[0]["out"].reshape(n_seq, T, D)
```

```python
from contextlib import ExitStack

import numpy as np

import concourse.bass as bass
from concourse import mybir

F32 = mybir.dt.float32
F32R = mybir.dt.float32r
BF16 = mybir.dt.bfloat16
ACT = mybir.ActivationFunctionType
ALU = mybir.AluOpType
AX = mybir.AxisListType

P = 128
D = 128
T = 256
TILES = T // P
BANK = 512
RING = 4
LN_EPS = 1e-5
MASKED = -1e30


class Seq:

    def __init__(self, number, parity, first=False, last=False):
        self.number, self.parity, self.first, self.last = number, parity, first, last

    def before(self):
        return Seq(self.number - 1, 1 - self.parity, first=isinstance(self.number, int) and self.number == 1)

    def tiles(self, whole):
        return whole[:, bass.ds(self.number * TILES, TILES), :]

    def tile(self, whole, t):
        return whole[:, bass.ds(self.number * TILES + t, 1), :].rearrange("p a d -> p (a d)")


def pipeline(eng, n_seq, step):
    step(Seq(0, 0, first=True), None)
    step(Seq(1, 1), Seq(0, 0, first=True))
    with eng.Fori(0, (n_seq - 2) // 2) as k:
        step(Seq(k * 2 + 2, 0), Seq(k * 2 + 1, 1))
        step(Seq(k * 2 + 3, 1), Seq(k * 2 + 2, 0))
    step(None, Seq(n_seq - 1, 1, last=True))


def pipeline3(eng, n_seq, step):
    step(Seq(0, 0, first=True), None, None)
    step(Seq(1, 1), Seq(0, 0, first=True), None)
    with eng.Fori(0, (n_seq - 2) // 2) as k:
        step(Seq(k * 2 + 2, 0), Seq(k * 2 + 1, 1), Seq(k * 2, 0))
        step(Seq(k * 2 + 3, 1), Seq(k * 2 + 2, 0), Seq(k * 2 + 1, 1))
    step(None, Seq(n_seq - 1, 1, last=True), Seq(n_seq - 2, 0))
    step(None, None, Seq(n_seq - 1, 1, last=True))


class Count:

    def __init__(self, sem, order, front):
        self.sem, self.order = sem, list(order)
        assert len(set(self.order)) == len(self.order)
        self.front = [e for e in self.order if e in front]
        self.back = [e for e in self.order if e not in front]

    def place(self, event, seq):
        if event in self.front:
            if seq.first:
                return self.front.index(event)
            return (seq.number - 1) * len(self.order) + (len(self.front) + self.order.index(event))
        before = len(self.front) + (self.back if seq.last else self.order).index(event)
        return seq.number * len(self.order) + before

    def done(self, event, seq):
        return self.place(event, seq) + 1

    def slot(self, event, seq, slots):
        step = len(self.order)
        if event in self.front:
            if seq.first:
                return self.front.index(event) % slots
            return ((seq.parity + 1) % 2 * step + len(self.front) + self.order.index(event)) % slots
        before = len(self.front) + (self.back if seq.last else self.order).index(event)
        return (seq.parity * step + before) % slots


class Ring:

    def __init__(self, banks, filled, drained, order, front):
        assert 2 * len(order) % len(banks) == 0
        self.banks = banks
        self.filled, self.drained = Count(filled, order, front), Count(drained, order, front)

    def bank(self, job, seq):
        return self.banks[self.filled.slot(job, seq, len(self.banks))]

    def wait_free(self, pe, job, seq):
        ring = len(self.banks)
        place = self.filled.place(job, seq)
        if not (isinstance(place, int) and place < ring):
            pe.wait_ge(self.drained.sem, place - (ring - 1))

    def wait_filled(self, eng, job, seq):
        eng.wait_ge(self.filled.sem, self.filled.done(job, seq))

    def wait_drained(self, eng, job, seq):
        eng.wait_ge(self.drained.sem, self.drained.done(job, seq))


def wait_apart(nc, eng, c, sem, value):
    eng.wait_ge(sem, value)
    nc.vector.tensor_copy(c["carrier"][:, 0:1], c["eps"][:, 0:1])


PRE_NORM = ["stats0", "stats1", "mv0", "mv1", "xn0", "xn1"]
POST_NORM = ["ystats0", "ystats1", "ymv0", "ymv1", "yn0"]
RSQRT = ["var", "rstd", "yvar", "yrstd"]


class Norm:

    def __init__(self, nc, ctx, prefix, vec, rst, c):
        def sb(name, shape):
            return ctx.enter_context(nc.sbuf_tensor(prefix + name, shape, F32))

        self.nc, self.vec, self.rst, self.c = nc, vec, rst, c
        self.stats = {"": sb("stats", [P, TILES, 6]), "y": sb("ystats", [P, TILES, 6])}
        self.mv = {"": sb("mv", [P, TILES, 2]), "y": sb("ymv", [P, TILES, 2])}
        self.var = {"": sb("var", [P, TILES]), "y": sb("yvar", [P, TILES])}
        self.rstd = {"": sb("rstd", [P, TILES]), "y": sb("yrstd", [P, TILES])}
        self.xn = sb("xn", [P, TILES, D])
        self.yn = sb("yn", [P, TILES, D])

    def rsqrt(self, pool, which, seq):
        nc, vec, rst = self.nc, self.vec, self.rst
        pool.wait_ge(vec.sem, vec.done(which + "mv1", seq))
        nc.gpsimd.tensor_tensor(self.var[which][:, :], self.mv[which][:, :, 1], self.c["eps"][:, 0:TILES],
                                ALU.add)\
            .then_inc(rst.sem, 1)
        pool.wait_ge(rst.sem, rst.done(which + "var", seq))
        nc.gpsimd.tensor_tensor(self.rstd[which][:, :], self.var[which][:, :],
                                self.c["minus_half"][:, 0:TILES], ALU.pow).then_inc(rst.sem, 1)

    def moments(self, dve, which, seq, tiles):
        nc, vec = self.nc, self.vec
        for t in range(TILES):
            nc.vector.bn_stats(self.stats[which][:, t], tiles[t]).then_inc(vec.sem, 1)
        wait_apart(nc, dve, self.c, vec.sem, vec.done(f"{which}stats{TILES - 1}", seq))
        for t in range(TILES):
            nc.vector.bn_aggr(self.mv[which][:, t], self.stats[which][:, t]).then_inc(vec.sem, 1)

    def scaled(self, which, t, out, tile):
        mv, rstd = self.mv[which], self.rstd[which]
        return self.nc.vector.tensor_scalar(out, tile, mv[:, t, 0:1], rstd[:, t:t + 1],
                                            ALU.subtract, ALU.mult)

    def pre(self, dve, seq, x, to_act):
        self.pre_moments(dve, seq, x)
        self.pre_scaled(dve, seq, x, to_act)

    def pre_moments(self, dve, seq, x):
        self.moments(dve, "", seq, [seq.tile(x, t) for t in range(TILES)])

    def pre_scaled(self, dve, seq, x, to_act):
        dve.wait_ge(self.rst.sem, self.rst.done("rstd", seq))
        if not seq.first:
            to_act.wait_filled(dve, "xnT", seq.before())
        for t in range(TILES):
            self.scaled("", t, self.xn[:, t], seq.tile(x, t)).then_inc(self.vec.sem, 1)

    def post(self, dve, seq, x, ring, job):
        self.post_moments(dve, seq, ring, job)
        return self.post_scaled(dve, seq, x, ring, job)

    def post_moments(self, dve, seq, ring, job):
        bank = ring.bank(job, seq)
        wait_apart(self.nc, dve, self.c, ring.filled.sem, ring.filled.done(job, seq))
        self.moments(dve, "y", seq, [bank[:, t * D:(t + 1) * D] for t in range(TILES)])

    def post_scaled(self, dve, seq, x, ring, job):
        nc, vec = self.nc, self.vec
        bank = ring.bank(job, seq)
        dve.wait_ge(self.rst.sem, self.rst.done("yrstd", seq))
        self.scaled("y", 0, self.yn[:, 0], bank[:, 0:D]).then_inc(vec.sem, 1)
        self.scaled("y", 1, self.yn[:, 1], bank[:, D:2 * D]).then_inc(ring.drained.sem, 1)
        dve.wait_ge(vec.sem, vec.done("yn0", seq))
        ring.wait_drained(dve, job, seq)
        return nc.vector.tensor_tensor(seq.tiles(x), seq.tiles(x), self.yn[:, :, :], ALU.add)


TH, TD = 16, 8
GROUPS = 4
ROWS = 32
BITS = 6
NT = 7


def token_attention(nc, n_seq, x, w, c):
    units = [f"{n}.{kind}" for n in range(GROUPS) for kind in ("i1a", "i1b", "i0")]
    LAG_EXP, LAG_T = 2, 4
    act_front, dve_front = ["xnT", "q0", "q1", "right", "v"], ["k0", "k1", "left0", "left1"]
    act_order, dve_order = [], []
    for i in range(len(units) + LAG_T):
        if i < len(units):
            act_order.append("raw" + units[i])
            dve_order.append("bil" + units[i])
        if i >= LAG_T:
            (act_order if i % 2 == 0 else dve_order).append("pT" + units[i - LAG_T])
    act_order += act_front + ["oT"]
    dve_order += dve_front + ["av", "out"]
    SLOTS = 5

    def unit(name):
        n, kind = name.split(".")
        return int(n), {"i1a": (0, 1), "i1b": (2, 3), "i0": (0, 1, 2, 3)}[kind], int(kind[1])

    with ExitStack() as ctx:
        def sb(name, shape, dt=F32):
            return ctx.enter_context(nc.sbuf_tensor("t_" + name, shape, dt))

        def sem(name):
            return ctx.enter_context(nc.semaphore("t_" + name))

        qT = [sb(f"qT{u}", [P, GROUPS, T]) for u in range(2)]
        kT = [sb(f"kT{u}", [P, GROUPS, T]) for u in range(2)]
        left = [sb(f"left{u}", [P, GROUPS, T]) for u in range(2)]
        right = [sb(f"right{u}", [P, T]) for u in range(2)]
        v = [sb(f"v{u}", [P, TILES, TH, TD + 1]) for u in range(2)]
        xnT = sb("xnT", [P, T])
        bilinear = sb("bilinear", [2 * BITS, TH, ROWS])
        tanh_qk = sb("tanh_qk", [P, 3, BANK])
        scores = sb("scores", [P, SLOTS, BANK])
        neg_max = sb("neg_max", [P, 3, 4])
        pT = sb("pT", [P, len(units), BANK])
        rden = sb("rden", [P, TILES, TH])
        o = sb("o", [P, TILES, D])
        oT = sb("oT", [P, T])
        act_banks = [ctx.enter_context(nc.psum_tensor(f"t_act{i}", [P, BANK], F32)) for i in range(RING)]
        dve_banks = [ctx.enter_context(nc.psum_tensor(f"t_dve{i}", [P, BANK], F32)) for i in range(RING)]
        to_act = Ring(act_banks, sem("act_filled"), sem("act_drained"), act_order, act_front)
        to_dve = Ring(dve_banks, sem("dve_filled"), sem("dve_drained"), dve_order, dve_front)
        vec = Count(sem("vec"), PRE_NORM + ["max" + n for n in units] + ["rden"] + POST_NORM, PRE_NORM)
        rst = Count(sem("rst"), RSQRT, RSQRT[:2])
        shifted = Count(sem("shifted"), units, [])
        exped = Count(sem("exped"), units, [])
        norm = Norm(nc, ctx, "t_", vec, rst, c)
        setup_pool, setup_act, setup_dve, setup_pe = (sem("setup_" + e) for e in ("pool", "act", "dve", "pe"))
        lam, scl = w["scalars"][:, 0:1], w["scalars"][:, 1:2]
        alpha, beta = w["scalars"][:, 2:3], w["scalars"][:, 3:4]
        sig = sb("sig", [P, 2, 3])
        inv_beta = sb("inv_beta", [P, 1])
        tw = sb("tw", [TH, 3, 8])
        tw_sum = sb("tw_sum", [TH, 3])
        twT = sb("twT", [8, TH])

        with nc.Block() as block:
            @block.gpsimd
            def _(pool):
                for u in range(2):
                    nc.gpsimd.memset(v[u][:, :, :, TD:TD + 1], 1.0).then_inc(setup_pool, 1)
                nc.gpsimd.memset(bilinear[:, :, :], 0.0).then_inc(setup_pool, 1)

                def step(front, back):
                    if front:
                        norm.rsqrt(pool, "", front)
                    if back:
                        for i, name in enumerate(units):
                            n, gs, t = unit(name)
                            pool.wait_ge(vec.sem, vec.done("max" + name, back))
                            s = scores[:, i % SLOTS, :].rearrange("p (h j) -> p h j", h=len(gs))
                            nc.gpsimd.tensor_tensor(
                                s, s, neg_max[:, i % 3, 0:len(gs)].unsqueeze(2)
                                .broadcast_to((P, len(gs), BANK // len(gs))), ALU.add)\
                                .then_inc(shifted.sem, 1)
                        norm.rsqrt(pool, "y", back)

                pipeline(pool, n_seq, step)

            @block.vector
            def _(dve):
                nc.vector.reciprocal(inv_beta[:, :], beta).then_inc(setup_dve, 1)
                nc.vector.tensor_reduce(tw_sum[:, 0:1], w["transform"][:, :], AX.X, ALU.max)\
                    .then_inc(setup_dve, 1)
                dve.wait_ge(setup_dve, 2)
                nc.vector.tensor_scalar(tw[:, 0, 0:NT], w["transform"][:, :], tw_sum[:, 0:1], None,
                                        ALU.subtract).then_inc(setup_dve, 1)
                dve.wait_ge(setup_act, 2)
                nc.vector.tensor_scalar(sig[:, :, 1], sig[:, :, 0], 1.0, None, ALU.add)\
                    .then_inc(setup_dve, 1)
                dve.wait_ge(setup_dve, 4)
                nc.vector.reciprocal(sig[:, :, 2], sig[:, :, 1]).then_inc(setup_dve, 1)
                nc.vector.reciprocal(tw_sum[:, 2:3], tw_sum[:, 1:2]).then_inc(setup_dve, 1)
                dve.wait_ge(setup_dve, 6)
                nc.vector.tensor_scalar(tw[:, 2, 0:NT], tw[:, 1, 0:NT], tw_sum[:, 2:3],
                                        sig[0:TH, 1, 2:3], ALU.mult, ALU.mult).then_inc(setup_dve, 1)
                nc.vector.tensor_scalar(tw[:, 2, NT:NT + 1], sig[0:TH, 0, 2:3], 0.5, None, ALU.mult)\
                    .then_inc(setup_dve, 1)
                dve.wait_ge(setup_dve, 7)
                nc.vector.tensor_scalar(tw[:, 2, 0:NT], tw[:, 2, 0:NT], 1.0 / 3.0, None, ALU.mult)\
                    .then_inc(setup_dve, 1)
                dve.wait_ge(setup_pe, 1)
                nc.vector.tensor_copy(twT[:, :], dve_banks[0][0:8, 0:TH]).then_inc(setup_dve, 1)
                dve.wait_ge(setup_pe, 2)
                dve.wait_ge(setup_pool, 3)
                nc.vector.tensor_copy(
                    bilinear[:, :, 0:2 * BITS],
                    dve_banks[1][0:2 * BITS, 0:2 * BITS * TH].rearrange("a (b h) -> a h b", h=TH))\
                    .then_inc(setup_dve, 1)

                def step(front, back):
                    if front:
                        norm.pre(dve, front, x, to_act)
                    if back:
                        for i in range(len(units) + LAG_T):
                            if i < len(units):
                                name = units[i]
                                n, gs, t = unit(name)
                                to_act.wait_drained(dve, "raw" + name, back)
                                to_dve.wait_filled(dve, "bil" + name, back)
                                if i >= SLOTS and (i - SLOTS + LAG_T) % 2 == 0:
                                    to_act.wait_filled(dve, "pT" + units[i - SLOTS], back)
                                nc.vector.scalar_tensor_tensor(
                                    scores[:, i % SLOTS, :], tanh_qk[:, i % 3, :], alpha,
                                    to_dve.bank("bil" + name, back)[:, :], ALU.mult, ALU.add)\
                                    .then_inc(to_dve.drained.sem, 1)
                                to_dve.wait_drained(dve, "bil" + name, back)
                                if i >= 3:
                                    dve.wait_ge(shifted.sem, shifted.done(units[i - 3], back))
                                nc.vector.tensor_reduce(
                                    neg_max[:, i % 3, 0:len(gs)],
                                    scores[:, i % SLOTS, :].rearrange("p (h j) -> p h j", h=len(gs)),
                                    AX.X, ALU.max, negate=True).then_inc(vec.sem, 1)
                            if i >= LAG_T and i % 2 == 1:
                                job = "pT" + units[i - LAG_T]
                                to_dve.wait_filled(dve, job, back)
                                nc.vector.tensor_copy(pT[:, i - LAG_T, :], to_dve.bank(job, back)[:, :])\
                                    .then_inc(to_dve.drained.sem, 1)
                    if front:
                        u = front.parity
                        for name, out in (("k", kT[u]), ("left", left[u])):
                            for i in range(2):
                                to_dve.wait_filled(dve, f"{name}{i}", front)
                                nc.vector.tensor_copy(
                                    out[:, 2 * i:2 * i + 2, :].rearrange("p a t -> p (a t)"),
                                    to_dve.bank(f"{name}{i}", front)[:, :]).then_inc(to_dve.drained.sem, 1)
                    if back:
                        to_dve.wait_filled(dve, "av", back)
                        got = to_dve.bank("av", back)[:, 0:TILES * TH * (TD + 1)].rearrange(
                            "p (a d) -> p a d", d=TD + 1)
                        nc.vector.reciprocal(rden[:, :, :].rearrange("p a h -> p (a h)"), got[:, :, TD])\
                            .then_inc(vec.sem, 1)
                        dve.wait_ge(vec.sem, vec.done("rden", back))
                        nc.vector.tensor_tensor(
                            o[:, :, :].rearrange("p a (h d) -> p (a h) d", d=TD), got[:, :, 0:TD],
                            rden[:, :, :].rearrange("p a h -> p (a h)").unsqueeze(2)
                            .broadcast_to((P, TILES * TH, TD)), ALU.mult).then_inc(to_dve.drained.sem, 1)
                        norm.post(dve, back, x, to_dve, "out")

                pipeline(dve, n_seq, step)

            @block.scalar
            def _(act):
                nc.scalar.activation(sig[:, :, 0], w["scalars"][:, 0:2], ACT.Exp, scale=-1.0)\
                    .then_inc(setup_act, 1)
                act.wait_ge(setup_dve, 3)
                nc.scalar.activation(tw[:, 1, 0:NT], tw[:, 0, 0:NT], ACT.Exp, scale=2.0,
                                     accum_out=tw_sum[:, 1:2]).then_inc(setup_act, 1)

                def step(front, back):
                    if back:
                        for i in range(len(units) + LAG_T):
                            if i < len(units):
                                to_act.wait_filled(act, "raw" + units[i], back)
                                if i >= 3:
                                    to_dve.wait_drained(act, "bil" + units[i - 3], back)
                                nc.scalar.activation(tanh_qk[:, i % 3, :],
                                                     to_act.bank("raw" + units[i], back)[:, :],
                                                     ACT.Tanh, scale=inv_beta[:, :])\
                                    .then_inc(to_act.drained.sem, 1)
                            if 0 <= i - LAG_EXP < len(units):
                                act.wait_ge(shifted.sem, shifted.done(units[i - LAG_EXP], back))
                                s = scores[:, (i - LAG_EXP) % SLOTS, :]
                                nc.scalar.activation(s, s, ACT.Exp).then_inc(exped.sem, 1)
                            if i >= LAG_T and i % 2 == 0:
                                job = "pT" + units[i - LAG_T]
                                to_act.wait_filled(act, job, back)
                                nc.scalar.copy(pT[:, i - LAG_T, :], to_act.bank(job, back)[:, :])\
                                    .then_inc(to_act.drained.sem, 1)
                    if front:
                        u = front.parity
                        to_act.wait_filled(act, "xnT", front)
                        nc.scalar.copy(xnT[:, :], to_act.bank("xnT", front)[:, 0:T])\
                            .then_inc(to_act.drained.sem, 1)
                        for i in range(2):
                            to_act.wait_filled(act, f"q{i}", front)
                            nc.scalar.copy(qT[u][:, 2 * i:2 * i + 2, :].rearrange("p a t -> p (a t)"),
                                           to_act.bank(f"q{i}", front)[:, :])\
                                .then_inc(to_act.drained.sem, 1)
                        to_act.wait_filled(act, "right", front)
                        nc.scalar.activation(right[u][:, :], to_act.bank("right", front)[:, 0:T], ACT.Tanh)\
                            .then_inc(to_act.drained.sem, 1)
                        to_act.wait_filled(act, "v", front)
                        nc.scalar.copy(
                            v[u][:, :, :, 0:TD].rearrange("p a h d -> p (a h) d"),
                            to_act.bank("v", front)[:, 0:T].rearrange("p (a d) -> p a d", d=TD))\
                            .then_inc(to_act.drained.sem, 1)
                    if back:
                        to_act.wait_filled(act, "oT", back)
                        nc.scalar.copy(oT[:, :], to_act.bank("oT", back)[:, 0:T])\
                            .then_inc(to_act.drained.sem, 1)

                pipeline(act, n_seq, step)

            @block.tensor
            def _(pe):
                pe.wait_ge(setup_dve, 9)
                nc.tensor.transpose(dve_banks[0][0:8, 0:TH], tw[:, 2, :], c["ident"][0:TH, 0:TH])\
                    .then_inc(setup_pe, 1)
                pe.wait_ge(setup_dve, 10)
                for b in range(2 * BITS):
                    ins = nc.tensor.matmul(dve_banks[1][0:2 * BITS, b * TH:(b + 1) * TH],
                                           w["basis"][:, b, :], twT[:, :], start=True, stop=True)
                ins.then_inc(setup_pe, 1)
                pe.wait_ge(setup_dve, 11)

                def step(front, back):
                    if back:
                        u = back.parity
                        to_act.wait_drained(pe, "v", back)
                        to_dve.wait_drained(pe, "left1", back)
                        for i in range(len(units) + LAG_T):
                            if i < len(units):
                                n, gs, t = unit(units[i])
                                width = P * (t + 1)
                                raw, bil = "raw" + units[i], "bil" + units[i]
                                to_act.wait_free(pe, raw, back)
                                for s, g in enumerate(gs):
                                    ins = nc.tensor.matmul(
                                        to_act.bank(raw, back)[:, s * width:(s + 1) * width],
                                        qT[u][ROWS * n:ROWS * n + TD, g, P * t:P * t + P],
                                        kT[u][ROWS * n:ROWS * n + TD, g, 0:width], start=True, stop=True)
                                ins.then_inc(to_act.filled.sem, 1)
                                to_dve.wait_free(pe, bil, back)
                                bank = to_dve.bank(bil, back)
                                for s, g in enumerate(gs):
                                    nc.tensor.matmul(
                                        bank[:, s * width:(s + 1) * width],
                                        left[u][ROWS * n:ROWS * n + 2 * BITS, g, P * t:P * t + P],
                                        right[u][ROWS * n:ROWS * n + 2 * BITS, 0:width],
                                        start=True, stop=False)
                                    ins = nc.tensor.matmul(bank[:, (s + 1) * width - P:(s + 1) * width],
                                                           c["ident_bf"][:, :], c["mask_rows"][:, :],
                                                           start=False, stop=True)
                                ins.then_inc(to_dve.filled.sem, 1)
                            if i >= LAG_T:
                                name = units[i - LAG_T]
                                ring = to_act if i % 2 == 0 else to_dve
                                ring.wait_free(pe, "pT" + name, back)
                                pe.wait_ge(exped.sem, exped.done(name, back))
                                for b in range(BANK // P):
                                    ins = nc.tensor.transpose(
                                        ring.bank("pT" + name, back)[:, b * P:(b + 1) * P],
                                        scores[:, (i - LAG_T) % SLOTS, b * P:(b + 1) * P], c["ident"][:, :])
                                ins.then_inc(ring.filled.sem, 1)
                    if front:
                        to_act.wait_free(pe, "xnT", front)
                        for t in range(TILES):
                            pe.wait_ge(vec.sem, vec.done(f"xn{t}", front))
                            ins = nc.tensor.transpose(to_act.bank("xnT", front)[:, t * P:(t + 1) * P],
                                                      norm.xn[:, t], c["ident"][:, :])
                        ins.then_inc(to_act.filled.sem, 1)
                        to_act.wait_drained(pe, "xnT", front)
                        for name, ring, weights in (("q", to_act, w["tq"]), ("k", to_dve, w["tk"])):
                            for i in range(2):
                                ring.wait_free(pe, f"{name}{i}", front)
                                for j in range(2):
                                    g = 2 * i + j
                                    ins = nc.tensor.matmul(
                                        ring.bank(f"{name}{i}", front)[:, j * T:(j + 1) * T],
                                        weights[:, g, :], xnT[:, :], start=True, stop=True)
                                ins.then_inc(ring.filled.sem, 1)
                        to_act.wait_free(pe, "right", front)
                        nc.tensor.matmul(to_act.bank("right", front)[:, 0:T], w["bits"][:, :], xnT[:, :],
                                         start=True, stop=True).then_inc(to_act.filled.sem, 1)
                        to_act.wait_free(pe, "v", front)
                        for t in range(TILES):
                            ins = nc.tensor.matmul(to_act.bank("v", front)[:, t * D:(t + 1) * D],
                                                   xnT[:, t * P:(t + 1) * P], w["tv"][:, :],
                                                   start=True, stop=True)
                        ins.then_inc(to_act.filled.sem, 1)
                        to_act.wait_drained(pe, "right", front)
                        for i in range(2):
                            to_dve.wait_free(pe, f"left{i}", front)
                            for j in range(2):
                                g = 2 * i + j
                                ins = nc.tensor.matmul(
                                    to_dve.bank(f"left{i}", front)[:, j * T:(j + 1) * T],
                                    bilinear[:, 4 * g:4 * g + 4, :].rearrange("a h b -> a (h b)"),
                                    right[front.parity][0:2 * BITS, :], start=True, stop=True)
                            ins.then_inc(to_dve.filled.sem, 1)
                    if back:
                        to_act.wait_drained(pe, "pT" + units[-2], back)
                        if front:
                            to_dve.wait_free(pe, "av", back)
                        else:
                            to_dve.wait_drained(pe, "pT" + units[-1], back)
                        for i, name in enumerate(units):
                            n, gs, t = unit(name)
                            for s, g in enumerate(gs):
                                h = 4 * g + n
                                at = (t * TH + h) * (TD + 1)
                                for j in range(t + 1):
                                    b = s * (t + 1) + j
                                    ins = nc.tensor.matmul(
                                        to_dve.bank("av", back)[:, at:at + TD + 1],
                                        pT[:, i, b * P:(b + 1) * P], v[back.parity][:, j, h, :],
                                        start=j == 0, stop=j == t)
                        ins.then_inc(to_dve.filled.sem, 1)
                        to_act.wait_free(pe, "oT", back)
                        to_dve.wait_drained(pe, "av", back)
                        for t in range(TILES):
                            ins = nc.tensor.transpose(to_act.bank("oT", back)[:, t * P:(t + 1) * P],
                                                      o[:, t], c["ident"][:, :])
                        ins.then_inc(to_act.filled.sem, 1)
                        to_dve.wait_free(pe, "out", back)
                        to_act.wait_drained(pe, "oT", back)
                        for t in range(TILES):
                            ins = nc.tensor.matmul(to_dve.bank("out", back)[:, t * D:(t + 1) * D],
                                                   oT[:, t * P:(t + 1) * P], w["t_out"][:, :],
                                                   start=True, stop=True)
                        ins.then_inc(to_dve.filled.sem, 1)

                pipeline(pe, n_seq, step)


LAYERS, NH, HD = 2, 8, 64
INNER = NH * HD
WINDOW = 64
HID = 341
CHUNKS = [128, 128, 85]
QK_SCALE = 8.0
SPAN = P + WINDOW


def window_attention(nc, n_seq, x, z, w, c, layer):
    first_layer = layer == 0
    units = ["0.0", "0.1", "1.0", "1.1", "1.2", "1.3"]
    LAG = 3
    turns = len(units) + LAG + 1
    values_at = {LAG + 4: "yT0", LAG + 6: "yT1"}
    parts = ["q0", "k0", "q1", "k1"]
    COS, SCALE = 2, 4
    front_at = {1: ["xnT"], 2: ["q0"], 3: ["k0"], 4: ["q1"], 5: ["k1", "q0T"], 6: ["k0T"], 7: ["q1T"], 8: ["k1T"]}
    act_front = [job for i in sorted(front_at) for job in front_at[i]]
    act_order = []
    for i in range(turns):
        act_order += ["s" + units[i]] if i < len(units) else []
        act_order += ["v0"] if i == 0 else []
        act_order += [values_at[i]] if i in values_at else []
        act_order += front_at.get(i, [])
    dve_order = ["v1"] + ["pT" + u for u in units] + ["out"]
    part_events = []
    for i in range(turns):
        if 0 <= i - SCALE < len(parts):
            part_events += [f"{e}.{parts[i - SCALE]}" for e in ("rot", "unit")]
        if 0 <= i - COS < len(parts):
            part_events += [f"{e}.{parts[i - COS]}" for e in ("sum", "clip", "cos")]

    def unit(name):
        t, n = int(name[0]), int(name[2])
        if t == 1:
            return t, [4 * (n // 2) + n % 2 + 2 * i for i in range(2)], SPAN
        return t, [n + 2 * i for i in range(4)], P

    with ExitStack() as ctx:
        pre = f"w{layer}_"

        def sb(name, shape, dt=F32):
            return ctx.enter_context(nc.sbuf_tensor(pre + name, shape, dt))

        def sem(name):
            return ctx.enter_context(nc.semaphore(pre + name))

        table = sb("table", [P, TILES, 4, HD])
        hT = sb("hT", [P, T])
        raw = sb("raw", [P, len(parts), INNER])
        squares = sb("squares", [P, len(parts), INNER])
        swapped = sb("swapped", [P, len(parts), INNER])
        turned = sb("turned", [P, len(parts), INNER])
        lengths = sb("lengths", [P, len(parts), NH])
        inv = sb("inv", [P, len(parts), NH])
        qT = [sb(f"qT{u}", [P, INNER // P, T]) for u in range(2)]
        kT = [sb(f"kT{u}", [P, INNER // P, T]) for u in range(2)]
        v = sb("v", [P, TILES, NH, HD])
        neg_max = sb("neg_max", [P, len(units), 4])
        sums = sb("sums", [P, len(units), 4])
        probs = sb("probs", [P, len(units), BANK])
        pT = sb("pT", [P, len(units), BANK])
        yT = sb("yT", [P, INNER // P, T])
        act_banks = [ctx.enter_context(nc.psum_tensor(f"{pre}act{i}", [P, BANK], F32)) for i in range(6)]
        dve_banks = [ctx.enter_context(nc.psum_tensor(f"{pre}dve{i}", [P, BANK], F32)) for i in range(2)]
        to_act = Ring(act_banks, sem("act_filled"), sem("act_drained"), act_order, act_front)
        to_dve = Ring(dve_banks, sem("dve_filled"), sem("dve_drained"), dve_order, [])
        maxed = Count(sem("maxed"), units, [])
        inverted = Count(sem("inverted"), units, [])
        divided = Count(sem("divided"), units, [])
        turn = Count(sem("turn"), part_events, part_events)
        pool_front = ["keep"] + [f"{e}.{p}" for p in parts for e in ("sin", "inv")]
        gps = Count(sem("gps"), pool_front, pool_front)
        squared = Count(sem("squared"), parts, parts)
        vec = Count(sem("vec"), PRE_NORM, PRE_NORM)
        rst = Count(sem("rst"), RSQRT[:2], RSQRT[:2])
        norm = Norm(nc, ctx, pre, vec, rst, c)
        setup, tables_done = sem("setup"), sem("tables_done")

        def kept(a, i):
            t, hs, width = unit(units[i])
            wide = a.rearrange("p (h j) -> p h j", h=len(hs))
            return wide[:, :, P * (t + 1) - width:]

        with nc.Block() as block:
            @block.gpsimd
            def _(pool):
                for i, name in enumerate(units):
                    if name[0] == "1":
                        nc.gpsimd.memset(probs[:, i, :].rearrange("p (h j) -> p h j", h=2)[:, :, 0:WINDOW],
                                         0.0).then_inc(setup, 1)
                nc.gpsimd.memset(hT[:, 0:1], 0.0).then_inc(setup, 1)
                pool.wait_ge(tables_done, 4)

                def turn_part(j, front):
                    p = parts[j]
                    kind, t, s = "qk".index(p[0]), int(p[1]), j
                    if not front.first:
                        pool.wait_ge(turn.sem, turn.done("unit." + p, front.before()))
                    to_act.wait_drained(pool, p, front)
                    halves = raw[:, s, :].rearrange("p (h a d) -> p h a d", a=2, d=HD // 2)
                    nc.gpsimd.tensor_tensor(
                        swapped[:, s, :].rearrange("p (h a d) -> p h a d", a=2, d=HD // 2),
                        halves[:, :, ::-1, :],
                        table[:, t, 2 * kind + 1, :].rearrange("p (a d) -> p a d", a=2)
                        .unsqueeze(1).broadcast_to((P, NH, 2, HD // 2)), ALU.mult).then_inc(gps.sem, 1)
                    pool.wait_ge(turn.sem, turn.done("clip." + p, front))
                    nc.gpsimd.tensor_tensor(inv[:, s, :], lengths[:, s, :], c["minus_half"][:, 0:NH],
                                            ALU.pow).then_inc(gps.sem, 1)

                def step(front, back, done):
                    if front and first_layer:
                        norm.rsqrt(pool, "", front)
                        pool.wait_ge(vec.sem, vec.done("xn1", front))
                        nc.gpsimd.tensor_copy(front.tiles(z), norm.xn[:, :, :]).then_inc(gps.sem, 1)
                    elif front:
                        if not front.first:
                            to_act.wait_filled(pool, "xnT", front.before())
                        nc.gpsimd.tensor_copy(norm.xn[:, :, :], front.tiles(z)).then_inc(gps.sem, 1)
                    for i in range(turns):
                        if front and 0 <= i - COS < len(parts):
                            turn_part(i - COS, front)
                        if back and 1 <= i <= len(units):
                            name = units[i - 1]
                            t, hs, width = unit(name)
                            pool.wait_ge(inverted.sem, inverted.done(name, back))
                            p = kept(probs[:, i - 1, :], i - 1)
                            nc.gpsimd.tensor_tensor(
                                p, p, sums[:, i - 1, 0:len(hs)].unsqueeze(2).broadcast_to((P, len(hs), width)),
                                ALU.mult).then_inc(divided.sem, 1)

                pipeline3(pool, n_seq, step)

            @block.vector
            def _(dve):
                for kind, scales in enumerate((w["q_scale"], w["k_scale"])):
                    for swap in range(2):
                        row = scales[:, layer, :]
                        if swap:
                            row = scales[:, layer, :].rearrange("p (a d) -> p a d", a=2)[:, ::-1, :]
                        for t in range(TILES):
                            ins = nc.vector.scalar_tensor_tensor(
                                table[:, t, 2 * kind + swap, :].rearrange("p (a d) -> p a d", a=2),
                                c["rotary"][:, t, 2 * kind + swap, :].rearrange("p (a d) -> p a d", a=2),
                                QK_SCALE if kind == 0 else 1.0,
                                row if swap else row.rearrange("p (a d) -> p a d", a=2),
                                ALU.mult, ALU.mult)
                        ins.then_inc(tables_done, 1)
                dve.wait_ge(tables_done, 4)

                def per_head(a):
                    return a.rearrange("p (h d) -> p h d", h=NH)

                def lengths_and_cos(j, front):
                    p = parts[j]
                    kind, t, s = "qk".index(p[0]), int(p[1]), j
                    dve.wait_ge(squared.sem, squared.done(p, front))
                    nc.vector.tensor_reduce(lengths[:, s, :], per_head(squares[:, s, :]), AX.X, ALU.add)\
                        .then_inc(turn.sem, 1)
                    dve.wait_ge(turn.sem, turn.done("sum." + p, front))
                    nc.vector.tensor_scalar(lengths[:, s, :], lengths[:, s, :], 1e-24, None, ALU.max)\
                        .then_inc(turn.sem, 1)
                    if not front.first:
                        to_act.wait_filled(dve, p + "T", front.before())
                    to_act.wait_drained(dve, p, front)
                    nc.vector.tensor_tensor(
                        per_head(turned[:, s, :]), per_head(raw[:, s, :]),
                        table[:, t, 2 * kind, :].unsqueeze(1).broadcast_to((P, NH, HD)), ALU.mult)\
                        .then_inc(turn.sem, 1)

                def add_sin_and_scale(j, front):
                    p, s = parts[j], j
                    dve.wait_ge(turn.sem, turn.done("cos." + p, front))
                    dve.wait_ge(gps.sem, gps.done("sin." + p, front))
                    nc.vector.tensor_tensor(turned[:, s, :], turned[:, s, :], swapped[:, s, :], ALU.add)\
                        .then_inc(turn.sem, 1)
                    dve.wait_ge(turn.sem, turn.done("rot." + p, front))
                    dve.wait_ge(gps.sem, gps.done("inv." + p, front))
                    nc.vector.tensor_tensor(
                        per_head(turned[:, s, :]), per_head(turned[:, s, :]),
                        inv[:, s, :].unsqueeze(2).broadcast_to((P, NH, HD)), ALU.mult).then_inc(turn.sem, 1)

                def step(front, back, done):
                    for i in range(turns):
                        if back and i < len(units):
                            t, hs, width = unit(units[i])
                            to_act.wait_filled(dve, "s" + units[i], back)
                            nc.vector.tensor_reduce(
                                neg_max[:, i, 0:len(hs)],
                                to_act.bank("s" + units[i], back)[:, 0:width * len(hs)].rearrange(
                                    "p (h j) -> p h j", h=len(hs)),
                                AX.X, ALU.max, negate=True).then_inc(maxed.sem, 1)
                        if back and 1 <= i <= len(units):
                            name = units[i - 1]
                            to_act.wait_drained(dve, "s" + name, back)
                            nc.vector.reciprocal(sums[:, i - 1, 0:len(unit(name)[1])],
                                                 sums[:, i - 1, 0:len(unit(name)[1])])\
                                .then_inc(inverted.sem, 1)
                        if done and i == 0:
                            to_dve.wait_filled(dve, "out", done)
                            nc.vector.tensor_tensor(
                                done.tiles(z), done.tiles(z),
                                to_dve.bank("out", done)[:, 0:T].rearrange("p (a d) -> p a d", a=TILES),
                                ALU.add).then_inc(to_dve.drained.sem, 1)
                        if back and i == 0:
                            to_dve.wait_filled(dve, "v1", back)
                            nc.vector.tensor_copy(
                                v[:, 1, :, :],
                                to_dve.bank("v1", back)[:, :].rearrange("p (h d) -> p h d", h=NH))\
                                .then_inc(to_dve.drained.sem, 1)
                        if front and i == 0 and first_layer:
                            if not front.first:
                                dve.wait_ge(gps.sem, gps.done("keep", front.before()))
                            norm.pre(dve, front, x, to_act)
                        if front and 0 <= i - SCALE < len(parts):
                            add_sin_and_scale(i - SCALE, front)
                        if back and LAG <= i < len(units) + LAG:
                            job = "pT" + units[i - LAG]
                            to_dve.wait_filled(dve, job, back)
                            nc.vector.tensor_copy(pT[:, i - LAG, :], to_dve.bank(job, back)[:, :])\
                                .then_inc(to_dve.drained.sem, 1)
                        if front and 0 <= i - COS < len(parts):
                            lengths_and_cos(i - COS, front)

                pipeline3(dve, n_seq, step)

            @block.scalar
            def _(act):
                act.wait_ge(setup, 5)

                def exps(i, back):
                    t, hs, width = unit(units[i])
                    bank = to_act.bank("s" + units[i], back)
                    out = kept(probs[:, i, :], i)
                    if not back.first:
                        to_dve.wait_filled(act, "pT" + units[i], back.before())
                    act.wait_ge(maxed.sem, maxed.done(units[i], back))
                    for s in range(len(hs)):
                        ins = nc.scalar.activation(out[:, s, :], bank[:, s * width:(s + 1) * width], ACT.Exp,
                                                   bias=neg_max[:, i, s:s + 1], accum_out=sums[:, i, s:s + 1])
                    ins.then_inc(to_act.drained.sem, 1)

                def take(job, front):
                    bank, u = to_act.bank(job, front), front.parity
                    if job == "xnT":
                        to_act.wait_filled(act, "xnT", front)
                        nc.scalar.copy(hT[0:HD, :], bank[0:HD, 0:T])
                        nc.scalar.copy(hT[HD:P, 1:T], bank[HD:P, 0:T - 1]).then_inc(to_act.drained.sem, 1)
                    elif job[-1] == "T":
                        t, out = int(job[1]), (qT if job[0] == "q" else kT)[u]
                        to_act.wait_filled(act, job, front)
                        nc.scalar.copy(out[:, :, t * P:(t + 1) * P],
                                       bank[:, :].rearrange("p (a t) -> p a t", a=INNER // P))\
                            .then_inc(to_act.drained.sem, 1)
                    else:
                        j = parts.index(job)
                        to_act.wait_filled(act, job, front)
                        if not front.first:
                            act.wait_ge(turn.sem, turn.done("cos." + job, front.before()))
                            act.wait_ge(gps.sem, gps.done("sin." + job, front.before()))
                        nc.scalar.square(squares[:, j, :], bank[:, :]).then_inc(squared.sem, 1)
                        nc.scalar.copy(raw[:, j, :], bank[:, :]).then_inc(to_act.drained.sem, 1)

                def step(front, back, done):
                    for i in range(turns):
                        if back and i < len(units):
                            exps(i, back)
                        if back and i == 0:
                            to_act.wait_filled(act, "v0", back)
                            nc.scalar.copy(v[:, 0, :, :],
                                           to_act.bank("v0", back)[:, :].rearrange("p (h d) -> p h d", h=NH))\
                                .then_inc(to_act.drained.sem, 1)
                        if back and i in values_at:
                            job = values_at[i]
                            n = int(job[2])
                            to_act.wait_filled(act, job, back)
                            nc.scalar.copy(yT[:, 2 * n:2 * n + 2, :].rearrange("p a t -> p (a t)"),
                                           to_act.bank(job, back)[:, :]).then_inc(to_act.drained.sem, 1)
                        for job in front_at.get(i, []) if front else []:
                            take(job, front)

                pipeline3(act, n_seq, step)

            @block.tensor
            def _(pe):
                def scores(name, back):
                    t, hs, width = unit(name)
                    u, bank = back.parity, to_act.bank("s" + name, back)
                    to_act.wait_free(pe, "s" + name, back)
                    for s, h in enumerate(hs):
                        rows = slice(HD * (h % 2), HD * (h % 2) + HD)
                        out = bank[:, width * s:width * s + width]
                        first_key = P * (t + 1) - width
                        nc.tensor.matmul(out, qT[u][rows, h // 2, P * t:P * t + P],
                                         kT[u][rows, h // 2, first_key:P * (t + 1)], start=True, stop=False)
                        ins = nc.tensor.matmul(out, c["ident_bf"][:, :], c["mask_window"][:, SPAN - width:],
                                               start=False, stop=True)
                    ins.then_inc(to_act.filled.sem, 1)

                def project_values(t, back):
                    ring, job = (to_dve if t else to_act), f"v{t}"
                    ring.wait_free(pe, job, back)
                    nc.tensor.matmul(ring.bank(job, back)[:, :], hT[:, t * P:(t + 1) * P],
                                     w["wqkv"][:, layer, 2 * INNER:3 * INNER], start=True, stop=True)\
                        .then_inc(ring.filled.sem, 1)

                def transposes(i, back):
                    job = "pT" + units[i]
                    to_dve.wait_free(pe, job, back)
                    pe.wait_ge(divided.sem, divided.done(units[i], back))
                    for b in range(BANK // P):
                        ins = nc.tensor.transpose(to_dve.bank(job, back)[:, b * P:(b + 1) * P],
                                                  probs[:, i, b * P:(b + 1) * P], c["ident"][:, :])
                    ins.then_inc(to_dve.filled.sem, 1)

                def values(job, last_unit, back):
                    first_head = 4 * int(job[2])
                    to_act.wait_free(pe, job, back)
                    to_dve.wait_drained(pe, "pT" + last_unit, back)
                    bank = to_act.bank(job, back)
                    for pair in range(2):
                        for j in range(TILES):
                            for t in range(j, TILES):
                                for side in range(2):
                                    h = first_head + 2 * pair + side
                                    i = next(i for i, name in enumerate(units)
                                             if unit(name)[0] == t and h in unit(name)[1])
                                    block_ = unit(units[i])[1].index(h) * (t + 1) + j
                                    ins = nc.tensor.matmul(
                                        bank[HD * side:HD * side + HD, pair * T + t * P:pair * T + (t + 1) * P],
                                        v[:, j, h, :], pT[:, i, block_ * P:(block_ + 1) * P],
                                        start=j == 0, stop=j == t)
                    ins.then_inc(to_act.filled.sem, 1)

                def project(job, front):
                    bank = to_act.bank(job, front)
                    to_act.wait_free(pe, job, front)
                    if job == "xnT":
                        for t in range(TILES):
                            if first_layer:
                                pe.wait_ge(vec.sem, vec.done(f"xn{t}", front))
                            elif t == 0:
                                pe.wait_ge(gps.sem, gps.done("keep", front))
                            ins = nc.tensor.transpose(bank[:, t * P:(t + 1) * P], norm.xn[:, t],
                                                      c["ident"][:, :])
                    elif job[-1] == "T":
                        pe.wait_ge(turn.sem, turn.done("unit." + job[:2], front))
                        for a in range(INNER // P):
                            ins = nc.tensor.transpose(bank[:, a * P:(a + 1) * P],
                                                      turned[:, parts.index(job[:2]), a * P:(a + 1) * P],
                                                      c["ident"][:, :])
                    else:
                        t, at = int(job[1]), "qk".index(job[0]) * INNER
                        if job == parts[0]:
                            to_act.wait_drained(pe, "xnT", front)
                        ins = nc.tensor.matmul(bank[:, :], hT[:, t * P:(t + 1) * P],
                                               w["wqkv"][:, layer, at:at + INNER], start=True, stop=True)
                    ins.then_inc(to_act.filled.sem, 1)

                def step(front, back, done):
                    if back:
                        to_act.wait_drained(pe, "k1T", back)
                    for i in range(turns):
                        if back and i < len(units):
                            scores(units[i], back)
                        if back and i == 0:
                            for t in range(TILES):
                                project_values(t, back)
                        if back and LAG <= i < len(units) + LAG:
                            transposes(i - LAG, back)
                        if back and i in values_at:
                            values(values_at[i], units[i - LAG - 1], back)
                        for job in front_at.get(i, []) if front else []:
                            project(job, front)
                    if back:
                        to_dve.wait_free(pe, "out", back)
                        to_act.wait_drained(pe, "yT1", back)
                        for t in range(TILES):
                            for pair in range(INNER // P):
                                ins = nc.tensor.matmul(to_dve.bank("out", back)[:, t * D:(t + 1) * D],
                                                       yT[:, pair, t * P:(t + 1) * P],
                                                       w["wo"][:, layer, pair, :],
                                                       start=pair == 0, stop=pair == INNER // P - 1)
                        ins.then_inc(to_dve.filled.sem, 1)

                pipeline3(pe, n_seq, step)


def gated_mlp(nc, n_seq, x, z, w, c, layer):
    last_layer = layer == LAYERS - 1
    act_front, dve_front = ["xnT"], ["moved"]
    act_order = ["g0", "g1", "g2"] + act_front
    dve_order = dve_front + ["a0", "a1", "a2", "out"]
    after = ["ystats0", "ystats1", "ymv0", "ymv1", "yn0", "yn1"] if last_layer else []

    with ExitStack() as ctx:
        pre = f"m{layer}_"

        def sb(name, shape, dt=F32):
            return ctx.enter_context(nc.sbuf_tensor(pre + name, shape, dt))

        def sem(name):
            return ctx.enter_context(nc.semaphore(pre + name))

        h = sb("h", [P, TILES, D])
        hT = [sb(f"hT{u}", [P, T]) for u in range(2)]
        gate = sb("gate", [P, 3, T])
        hidden = sb("hidden", [P, 3, T])
        act_banks = [ctx.enter_context(nc.psum_tensor(f"{pre}act{i}", [P, BANK], F32)) for i in range(2)]
        dve_banks = [ctx.enter_context(nc.psum_tensor(f"{pre}dve{i}", [P, BANK], F32)) for i in range(5)]
        to_act = Ring(act_banks, sem("act_filled"), sem("act_drained"), act_order, act_front)
        to_dve = Ring(dve_banks, sem("dve_filled"), sem("dve_drained"), dve_order, dve_front)
        vec = Count(sem("vec"), PRE_NORM + after, PRE_NORM)
        rst = Count(sem("rst"), RSQRT if last_layer else RSQRT[:2], RSQRT[:2])
        gps = Count(sem("gps"), ["own"], ["own"])
        norm = Norm(nc, ctx, pre, vec, rst, c)
        setup = sem("setup")

        with nc.Block() as block:
            @block.gpsimd
            def _(pool):
                nc.gpsimd.memset(hidden[:, 2, :], 1.0).then_inc(setup, 1)

                def step(front, back):
                    if front:
                        if not front.first:
                            pool.wait_ge(vec.sem, vec.done("xn1", front.before()))
                        nc.gpsimd.tensor_copy(h[:, :, 0:D // 2], front.tiles(z)[:, :, 0:D // 2])\
                            .then_inc(gps.sem, 1)
                        norm.rsqrt(pool, "", front)
                    if back and last_layer:
                        norm.rsqrt(pool, "y", back)

                pipeline(pool, n_seq, step)

            @block.vector
            def _(dve):
                dve.wait_ge(setup, 1)

                def step(front, back):
                    if front:
                        to_dve.wait_filled(dve, "moved", front)
                        nc.vector.tensor_copy(
                            h[:, :, D // 2:D],
                            to_dve.bank("moved", front)[:, 0:D].rearrange("p (a d) -> p a d", a=TILES))\
                            .then_inc(to_dve.drained.sem, 1)
                        wait_apart(nc, dve, c, to_dve.drained.sem, to_dve.drained.done("moved", front))
                        dve.wait_ge(gps.sem, gps.done("own", front))
                        norm.moments(dve, "", front, [h[:, t] for t in range(TILES)])
                        dve.wait_ge(rst.sem, rst.done("rstd", front))
                        if not front.first:
                            to_act.wait_filled(dve, "xnT", front.before())
                        for t in range(TILES):
                            norm.scaled("", t, norm.xn[:, t], h[:, t]).then_inc(vec.sem, 1)
                    if back:
                        for n, rows in enumerate(CHUNKS):
                            to_dve.wait_filled(dve, f"a{n}", back)
                            to_act.wait_drained(dve, f"g{n}", back)
                            nc.vector.scalar_tensor_tensor(
                                hidden[0:rows, n, :], to_dve.bank(f"a{n}", back)[0:rows, 0:T],
                                w["b1"][0:rows, layer, 0, n:n + 1], gate[0:rows, n, :], ALU.add, ALU.mult)\
                                .then_inc(to_dve.drained.sem, 1)
                        to_dve.wait_filled(dve, "out", back)
                        nc.vector.tensor_tensor(
                            back.tiles(z), back.tiles(z),
                            to_dve.bank("out", back)[:, 0:T].rearrange("p (a d) -> p a d", a=TILES),
                            ALU.add).then_inc(to_dve.drained.sem, 1)
                        if last_layer:
                            wait_apart(nc, dve, c, to_dve.drained.sem, to_dve.drained.done("out", back))
                            norm.moments(dve, "y", back, [back.tile(z, t) for t in range(TILES)])
                            dve.wait_ge(rst.sem, rst.done("yrstd", back))
                            for t in range(TILES):
                                norm.scaled("y", t, norm.yn[:, t], back.tile(z, t)).then_inc(vec.sem, 1)
                            dve.wait_ge(vec.sem, vec.done("yn1", back))
                            nc.vector.tensor_tensor(back.tiles(x), back.tiles(x), norm.yn[:, :, :], ALU.add)

                pipeline(dve, n_seq, step)

            @block.scalar
            def _(act):
                def step(front, back):
                    if back:
                        for n, rows in enumerate(CHUNKS):
                            to_act.wait_filled(act, f"g{n}", back)
                            nc.scalar.activation(gate[0:rows, n, :], to_act.bank(f"g{n}", back)[0:rows, 0:T],
                                                 ACT.Gelu, bias=w["b1"][0:rows, layer, 1, n:n + 1])\
                                .then_inc(to_act.drained.sem, 1)
                    if front:
                        to_act.wait_filled(act, "xnT", front)
                        nc.scalar.activation(hT[front.parity][:, :], to_act.bank("xnT", front)[:, 0:T],
                                             ACT.Identity, scale=w["ln_g"][:, layer:layer + 1],
                                             bias=w["ln_b"][:, layer:layer + 1])\
                            .then_inc(to_act.drained.sem, 1)

                pipeline(act, n_seq, step)

            @block.tensor
            def _(pe):
                def step(front, back):
                    if front:
                        to_dve.wait_free(pe, "moved", front)
                        bank = to_dve.bank("moved", front)
                        for t in range(TILES):
                            out = bank[:, t * HD:(t + 1) * HD]
                            own, ahead = front.tile(z, t)[:, HD:D], front.tile(z, 0)[:, HD:D]
                            ins = nc.tensor.matmul(out, c["next"][:, 0, :], own, start=True, stop=t == 0)
                            if t == 1:
                                ins = nc.tensor.matmul(out, c["next"][:, 1, :], ahead,
                                                       start=False, stop=True)
                        ins.then_inc(to_dve.filled.sem, 1)
                    if back:
                        u, col = back.parity, 0
                        to_act.wait_drained(pe, "xnT", back)
                        for n, rows in enumerate(CHUNKS):
                            for name, ring, at in (("g", to_act, HID), ("a", to_dve, 0)):
                                ring.wait_free(pe, f"{name}{n}", back)
                                nc.tensor.matmul(ring.bank(f"{name}{n}", back)[0:rows, 0:T],
                                                 w["w1"][:, layer, at + col:at + col + rows], hT[u][:, :],
                                                 start=True, stop=True).then_inc(ring.filled.sem, 1)
                            col += rows
                    if front:
                        to_act.wait_free(pe, "xnT", front)
                        for t in range(TILES):
                            pe.wait_ge(vec.sem, vec.done(f"xn{t}", front))
                            ins = nc.tensor.transpose(to_act.bank("xnT", front)[:, t * P:(t + 1) * P],
                                                      norm.xn[:, t], c["ident"][:, :])
                        ins.then_inc(to_act.filled.sem, 1)
                    if back:
                        to_dve.wait_free(pe, "out", back)
                        to_dve.wait_drained(pe, "a2", back)
                        for t in range(TILES):
                            for n, rows in enumerate(CHUNKS):
                                rows = rows + (n == len(CHUNKS) - 1)
                                ins = nc.tensor.matmul(to_dve.bank("out", back)[:, t * D:(t + 1) * D],
                                                       hidden[0:rows, n, t * P:(t + 1) * P],
                                                       w["w2"][0:rows, layer, n, :],
                                                       start=n == 0, stop=n == len(CHUNKS) - 1)
                        ins.then_inc(to_dve.filled.sem, 1)

                pipeline(pe, n_seq, step)


def ffn_layers(nc, n_seq, x, w, c):
    with nc.sbuf_tensor("z", [P, n_seq * TILES, D], F32) as z:
        for layer in range(LAYERS):
            window_attention(nc, n_seq, x, z, w, c, layer)
            gated_mlp(nc, n_seq, x, z, w, c, layer)


LH, LD = 16, 64


def latent_attention(nc, n_seq, x, w, c):
    pairs = LH * LD // P
    units = ["0.0", "0.1", "1.0", "1.1", "1.2", "1.3", "0.2", "0.3", "1.4", "1.5", "1.6", "1.7"]
    LAG, SLOTS = 3, 6
    turns = len(units) + LAG + 1
    values_at = {LAG + 4: "yT0", LAG + 6: "yT1", LAG + 10: "yT2", LAG + 12: "yT3"}
    front_jobs = ["xnT", "latT"] + [f"{a}{n}" for n in range(4) for a in "qk"]
    front_at = {5 + i: [job] for i, job in enumerate(front_jobs)}
    values_of = {0: "v0.0", 1: "v0.1", 2: "v1.0", 3: "v1.1"}
    act_order = []
    for i in range(turns):
        if i < len(units):
            act_order.append("s" + units[i])
        act_order += [values_of[i]] if i in values_of else []
        act_order += [values_at[i]] if i in values_at else []
        act_order += front_at.get(i, [])
    dve_order = ["pT" + u for u in units] + ["out"]

    def unit(name):
        t, n = int(name[0]), int(name[2])
        if t == 1:
            return t, [4 * (n // 2) + n % 2 + 2 * i for i in range(2)]
        return t, [8 * (n // 2) + n % 2 + 2 * i for i in range(4)]

    with ExitStack() as ctx:
        def sb(name, shape, dt=F32):
            return ctx.enter_context(nc.sbuf_tensor("l_" + name, shape, dt))

        def sem(name):
            return ctx.enter_context(nc.semaphore("l_" + name))

        qT = [sb(f"qT{u}", [P, pairs, T]) for u in range(2)]
        kT = [sb(f"kT{u}", [P, pairs, T]) for u in range(2)]
        v = sb("v", [P, TILES, LH, LD])
        xnT = sb("xnT", [P, T])
        latT = sb("latT", [P, T])
        neg_max = sb("neg_max", [P, len(units), 4])
        sums = sb("sums", [P, len(units), 4])
        probs = sb("probs", [P, SLOTS, BANK])
        pT = sb("pT", [P, len(units), BANK])
        yT = sb("yT", [P, pairs, T])
        act_banks = [ctx.enter_context(nc.psum_tensor(f"l_act{i}", [P, BANK], F32)) for i in range(6)]
        dve_banks = [ctx.enter_context(nc.psum_tensor(f"l_dve{i}", [P, BANK], F32)) for i in range(2)]
        to_act = Ring(act_banks, sem("act_filled"), sem("act_drained"), act_order, front_jobs)
        to_dve = Ring(dve_banks, sem("dve_filled"), sem("dve_drained"), dve_order, [])
        maxed = Count(sem("maxed"), units, [])
        inverted = Count(sem("inverted"), units, [])
        divided = Count(sem("divided"), units, [])
        vec = Count(sem("vec"), PRE_NORM + POST_NORM, PRE_NORM)
        rst = Count(sem("rst"), RSQRT, RSQRT[:2])
        norm = Norm(nc, ctx, "l_", vec, rst, c)

        with nc.Block() as block:
            @block.gpsimd
            def _(pool):
                def step(front, back, done):
                    if done:
                        norm.rsqrt(pool, "y", done)
                    for i, name in enumerate(units if back else [""]):
                        if front and i == (3 if back else 0):
                            norm.rsqrt(pool, "", front)
                        if not back:
                            break
                        t, hs = unit(name)
                        pool.wait_ge(inverted.sem, inverted.done(name, back))
                        p = probs[:, i % SLOTS, :].rearrange("p (h j) -> p h j", h=len(hs))
                        nc.gpsimd.tensor_tensor(
                            p, p, sums[:, i, 0:len(hs)].unsqueeze(2).broadcast_to((P, len(hs), P * (t + 1))),
                            ALU.mult).then_inc(divided.sem, 1)

                pipeline3(pool, n_seq, step)

            @block.vector
            def _(dve):
                def step(front, back, done):
                    if done:
                        norm.post_moments(dve, done, to_dve, "out")
                    for i in range(turns if back else 5):
                        if back and i < len(units):
                            t, hs = unit(units[i])
                            to_act.wait_filled(dve, "s" + units[i], back)
                            nc.vector.tensor_reduce(
                                neg_max[:, i, 0:len(hs)],
                                to_act.bank("s" + units[i], back)[:, :].rearrange("p (h j) -> p h j", h=len(hs)),
                                AX.X, ALU.max, negate=True).then_inc(maxed.sem, 1)
                        if back and 1 <= i <= len(units):
                            name = units[i - 1]
                            to_act.wait_drained(dve, "s" + name, back)
                            nc.vector.reciprocal(sums[:, i - 1, 0:len(unit(name)[1])],
                                                 sums[:, i - 1, 0:len(unit(name)[1])])\
                                .then_inc(inverted.sem, 1)
                        if done and i == 0:
                            norm.post_scaled(dve, done, x, to_dve, "out")
                        if front and i == 3:
                            norm.pre_moments(dve, front, x)
                        if front and i == 4:
                            norm.pre_scaled(dve, front, x, to_act)
                        if back and LAG <= i < len(units) + LAG:
                            job = "pT" + units[i - LAG]
                            to_dve.wait_filled(dve, job, back)
                            nc.vector.tensor_copy(pT[:, i - LAG, :], to_dve.bank(job, back)[:, :])\
                                .then_inc(to_dve.drained.sem, 1)

                pipeline3(dve, n_seq, step)

            @block.scalar
            def _(act):
                def step(front, back, done):
                    for i in range(turns):
                        if back and i < len(units):
                            t, hs = unit(units[i])
                            width = P * (t + 1)
                            bank = to_act.bank("s" + units[i], back)
                            if i >= SLOTS:
                                to_dve.wait_filled(act, "pT" + units[i - SLOTS], back)
                            elif not back.first:
                                to_dve.wait_filled(act, "pT" + units[i - SLOTS], back.before())
                            act.wait_ge(maxed.sem, maxed.done(units[i], back))
                            for s in range(len(hs)):
                                ins = nc.scalar.activation(
                                    probs[:, i % SLOTS, s * width:(s + 1) * width],
                                    bank[:, s * width:(s + 1) * width], ACT.Exp,
                                    bias=neg_max[:, i, s:s + 1], accum_out=sums[:, i, s:s + 1])
                            ins.then_inc(to_act.drained.sem, 1)
                        if back and i in values_of:
                            job = values_of[i]
                            t, half = int(job[1]), int(job[3])
                            to_act.wait_filled(act, job, back)
                            nc.scalar.copy(v[:, t, 8 * half:8 * half + 8, :],
                                           to_act.bank(job, back)[:, :].rearrange("p (h d) -> p h d", h=8))\
                                .then_inc(to_act.drained.sem, 1)
                        if back and i in values_at:
                            job = values_at[i]
                            n = int(job[2])
                            to_act.wait_filled(act, job, back)
                            nc.scalar.copy(yT[:, 2 * n:2 * n + 2, :].rearrange("p a t -> p (a t)"),
                                           to_act.bank(job, back)[:, :]).then_inc(to_act.drained.sem, 1)
                        for job in front_at.get(i, []) if front else []:
                            u = front.parity
                            to_act.wait_filled(act, job, front)
                            bank = to_act.bank(job, front)
                            if job in ("xnT", "latT"):
                                ins = nc.scalar.copy((xnT if job == "xnT" else latT)[:, :], bank[:, 0:T])
                            elif job[0] == "q":
                                n = int(job[1])
                                ins = nc.scalar.mul(qT[u][:, 2 * n:2 * n + 2, :].rearrange("p a t -> p (a t)"),
                                                    bank[:, :], LD ** -0.5)
                            else:
                                n = int(job[1])
                                ins = nc.scalar.copy(kT[u][:, 2 * n:2 * n + 2, :].rearrange("p a t -> p (a t)"),
                                                     bank[:, :])
                            ins.then_inc(to_act.drained.sem, 1)

                pipeline3(act, n_seq, step)

            @block.tensor
            def _(pe):
                def scores(name, back):
                    t, hs = unit(name)
                    width, u = P * (t + 1), back.parity
                    bank = to_act.bank("s" + name, back)
                    to_act.wait_free(pe, "s" + name, back)
                    for s, h in enumerate(hs):
                        rows = slice(LD * (h % 2), LD * (h % 2) + LD)
                        nc.tensor.matmul(bank[:, width * s:width * s + width],
                                         qT[u][rows, h // 2, P * t:P * t + P],
                                         kT[u][rows, h // 2, 0:width], start=True, stop=False)
                        ins = nc.tensor.matmul(bank[:, width * (s + 1) - P:width * (s + 1)],
                                               c["ident_bf"][:, :], c["mask_rows"][:, :],
                                               start=False, stop=True)
                    ins.then_inc(to_act.filled.sem, 1)

                def transposes(name, back):
                    job, slot = "pT" + name, units.index(name) % SLOTS
                    to_dve.wait_free(pe, job, back)
                    pe.wait_ge(divided.sem, divided.done(name, back))
                    for b in range(BANK // P):
                        ins = nc.tensor.transpose(to_dve.bank(job, back)[:, b * P:(b + 1) * P],
                                                  probs[:, slot, b * P:(b + 1) * P], c["ident"][:, :])
                    ins.then_inc(to_dve.filled.sem, 1)

                def values(job, last_unit, back):
                    first_head = 4 * int(job[2])
                    to_act.wait_free(pe, job, back)
                    to_dve.wait_drained(pe, "pT" + last_unit, back)
                    bank = to_act.bank(job, back)
                    for pair in range(2):
                        for j in range(TILES):
                            for t in range(j, TILES):
                                for side in range(2):
                                    h = first_head + 2 * pair + side
                                    i = next(i for i, name in enumerate(units)
                                             if unit(name)[0] == t and h in unit(name)[1])
                                    block_ = unit(units[i])[1].index(h) * (t + 1) + j
                                    ins = nc.tensor.matmul(
                                        bank[LD * side:LD * side + LD, pair * T + t * P:pair * T + (t + 1) * P],
                                        v[:, j, h, :], pT[:, i, block_ * P:(block_ + 1) * P],
                                        start=j == 0, stop=j == t)
                    ins.then_inc(to_act.filled.sem, 1)

                def project(job, front):
                    bank = to_act.bank(job, front)
                    to_act.wait_free(pe, job, front)
                    if job == "xnT":
                        for t in range(TILES):
                            pe.wait_ge(vec.sem, vec.done(f"xn{t}", front))
                            ins = nc.tensor.transpose(bank[:, t * P:(t + 1) * P], norm.xn[:, t],
                                                      c["ident"][:, :])
                    elif job == "latT":
                        to_act.wait_drained(pe, "xnT", front)
                        ins = nc.tensor.matmul(bank[:, 0:T], w["kv_down"][:, :], xnT[:, :],
                                               start=True, stop=True)
                    else:
                        if job == "q0":
                            to_act.wait_drained(pe, "latT", front)
                        weights, source = (w["q"], xnT) if job[0] == "q" else (w["kv_up"], latT)
                        for i in range(2):
                            pair = 2 * int(job[1]) + i
                            ins = nc.tensor.matmul(bank[:, i * T:(i + 1) * T],
                                                   weights[:, pair * P:(pair + 1) * P], source[:, :],
                                                   start=True, stop=True)
                    ins.then_inc(to_act.filled.sem, 1)

                def project_values(job, back):
                    t, half = int(job[1]), int(job[3])
                    at = LH * LD + BANK * half
                    to_act.wait_free(pe, job, back)
                    nc.tensor.matmul(to_act.bank(job, back)[:, :], latT[:, t * P:(t + 1) * P],
                                     w["kv_up"][:, at:at + BANK], start=True, stop=True)\
                        .then_inc(to_act.filled.sem, 1)

                def step(front, back, done):
                    if back:
                        to_act.wait_drained(pe, "k3", back)
                    for i in range(turns):
                        if back and i < len(units):
                            scores(units[i], back)
                        if back and i in values_of:
                            project_values(values_of[i], back)
                        if back and LAG <= i < len(units) + LAG:
                            transposes(units[i - LAG], back)
                        if back and i in values_at:
                            values(values_at[i], units[i - LAG - 1], back)
                        for job in front_at.get(i, []) if front else []:
                            project(job, front)
                    if back:
                        to_dve.wait_free(pe, "out", back)
                        to_act.wait_drained(pe, "yT3", back)
                        for t in range(TILES):
                            for pair in range(pairs):
                                ins = nc.tensor.matmul(to_dve.bank("out", back)[:, t * D:(t + 1) * D],
                                                       yT[:, pair, t * P:(t + 1) * P], w["l_out"][:, pair, :],
                                                       start=pair == 0, stop=pair == pairs - 1)
                        ins.then_inc(to_dve.filled.sem, 1)

                pipeline3(pe, n_seq, step)


EXPERTS, EF = 8, 256
NOT_A_LOGIT, TAKEN = -3.0e38, 3.0e38


def experts_layer(nc, n_seq, x, w, c, out_dram, finished):
    act_front, dve_front = ["xnT"], ["router"]
    act_order = act_front + [f"h{e}" for e in range(EXPERTS)]
    dve_order = dve_front + [f"y{t}.{g}" for g in range(2) for t in range(TILES)]
    route = ["best0", "best1", "pair", "rest0", "rest1", "chosen", "first0", "first1",
             "second", "mix0", "mix1", "weight"]
    sums = [f"sum{e}.{t}" for e in range(EXPERTS) if e % 4 < 3 for t in range(TILES)]

    with ExitStack() as ctx:
        def sb(name, shape, dt=F32):
            return ctx.enter_context(nc.sbuf_tensor("e_" + name, shape, dt))

        def sem(name):
            return ctx.enter_context(nc.semaphore("e_" + name))

        xnT = [sb(f"xnT{u}", [P, T]) for u in range(2)]
        hT = sb("hT", [P, 2, EF // P, T])
        logits = sb("logits", [P, TILES, 2 * EXPERTS])
        best = sb("best", [P, TILES, 8])
        pair = sb("pair", [P, TILES, 8])
        rest = sb("rest", [P, TILES, 2 * EXPERTS])
        diff = sb("diff", [P, TILES])
        lead = sb("lead", [P, TILES])
        second = sb("second", [P, TILES])
        chosen = sb("chosen", [P, TILES, EXPERTS])
        first = sb("first", [P, TILES, EXPERTS])
        weight = [sb(f"weight{u}", [P, TILES, EXPERTS]) for u in range(2)]
        acc = sb("acc", [P, TILES, D])
        act_banks = [ctx.enter_context(nc.psum_tensor(f"e_act{i}", [P, BANK], F32)) for i in range(3)]
        dve_banks = [ctx.enter_context(nc.psum_tensor(f"e_dve{i}", [P, BANK], F32)) for i in range(5)]
        to_act = Ring(act_banks, sem("act_filled"), sem("act_drained"), act_order, act_front)
        to_dve = Ring(dve_banks, sem("dve_filled"), sem("dve_drained"), dve_order, dve_front)
        vec = Count(sem("vec"), PRE_NORM + route + sums + ["ystats0", "ystats1", "ymv0", "ymv1", "yn0", "yn1"],
                    PRE_NORM + route)
        rst = Count(sem("rst"), RSQRT, RSQRT[:2])
        lead_done = Count(sem("lead_done"), ["diff", "lead"], ["diff", "lead"])
        updated = Count(sem("updated"), ["x"], [])
        norm = Norm(nc, ctx, "e_", vec, rst, c)
        setup = sem("setup")

        with nc.Block() as block:
            @block.gpsimd
            def _(pool):
                nc.gpsimd.memset(logits[:, :, EXPERTS:], NOT_A_LOGIT).then_inc(setup, 1)
                nc.gpsimd.memset(pair[:, :, 2:], NOT_A_LOGIT).then_inc(setup, 1)

                def step(front, back):
                    if front:
                        norm.rsqrt(pool, "", front)
                        pool.wait_ge(vec.sem, vec.done("best1", front))
                        nc.gpsimd.tensor_tensor(diff[:, :], best[:, :, 0], best[:, :, 1], ALU.subtract)\
                            .then_inc(lead_done.sem, 1)
                    if back:
                        norm.rsqrt(pool, "y", back)

                pipeline(pool, n_seq, step)

            @block.vector
            def _(dve):
                dve.wait_ge(setup, 2)

                def step(front, back):
                    if front:
                        norm.pre(dve, front, x, to_act)
                        to_dve.wait_filled(dve, "router", front)
                        got = to_dve.bank("router", front)[:, 0:TILES * EXPERTS]
                        nc.vector.tensor_copy(logits[:, :, 0:EXPERTS],
                                              got.rearrange("p (a e) -> p a e", a=TILES))\
                            .then_inc(to_dve.drained.sem, 1)
                        wait_apart(nc, dve, c, to_dve.drained.sem, to_dve.drained.done("router", front))
                        for t in range(TILES):
                            nc.vector.max(best[:, t, :], logits[:, t, 0:EXPERTS]).then_inc(vec.sem, 1)
                        dve.wait_ge(vec.sem, vec.done("best1", front))
                        nc.vector.tensor_copy(pair[:, :, 0:2], best[:, :, 0:2]).then_inc(vec.sem, 1)
                        wait_apart(nc, dve, c, vec.sem, vec.done("pair", front))
                        for t in range(TILES):
                            nc.vector.match_replace(rest[:, t, :], pair[:, t, :], logits[:, t, :], TAKEN)\
                                .then_inc(vec.sem, 1)
                        dve.wait_ge(vec.sem, vec.done("rest1", front))
                        nc.vector.tensor_scalar(chosen[:, :, :], rest[:, :, 0:EXPERTS], TAKEN, None,
                                                ALU.is_equal).then_inc(vec.sem, 1)
                        dve.wait_ge(lead_done.sem, lead_done.done("lead", front))
                        for t in range(TILES):
                            nc.vector.tensor_scalar(first[:, t, :], logits[:, t, 0:EXPERTS],
                                                    best[:, t, 0:1], lead[:, t:t + 1],
                                                    ALU.is_equal, ALU.mult).then_inc(vec.sem, 1)
                        nc.vector.tensor_scalar(second[:, :], lead[:, :], -0.5, 0.5, ALU.mult, ALU.add)\
                            .then_inc(vec.sem, 1)
                        dve.wait_ge(vec.sem, vec.done("second", front))
                        for t in range(TILES):
                            nc.vector.tensor_scalar(first[:, t, :], first[:, t, :], second[:, t:t + 1],
                                                    None, ALU.add).then_inc(vec.sem, 1)
                        dve.wait_ge(vec.sem, vec.done("mix1", front))
                        nc.vector.tensor_tensor(weight[front.parity][:, :, :], first[:, :, :],
                                                chosen[:, :, :], ALU.mult).then_inc(vec.sem, 1)
                    if back:
                        u = back.parity
                        for e in range(EXPERTS):
                            g = e // 4
                            for t in range(TILES):
                                if e % 4 == 0:
                                    to_dve.wait_filled(dve, f"y{t}.{g}", back)
                                bank = to_dve.bank(f"y{t}.{g}", back)
                                y = bank[:, (e % 4) * D:(e % 4 + 1) * D]
                                cw = weight[u][:, t, e:e + 1]
                                if e == 0:
                                    ins = nc.vector.tensor_scalar(acc[:, t], y, cw, None, ALU.mult)
                                else:
                                    if e % 4 == 0:
                                        to_dve.wait_drained(dve, f"y{t}.{g - 1}", back)
                                    else:
                                        dve.wait_ge(vec.sem, vec.done(f"sum{e - 1}.{t}", back))
                                    ins = nc.vector.scalar_tensor_tensor(acc[:, t], y, cw, acc[:, t],
                                                                         ALU.mult, ALU.add)
                                ins.then_inc(to_dve.drained.sem if e % 4 == 3 else vec.sem, 1)
                        wait_apart(nc, dve, c, to_dve.drained.sem, to_dve.drained.done("y1.1", back))
                        norm.moments(dve, "y", back, [acc[:, t] for t in range(TILES)])
                        dve.wait_ge(rst.sem, rst.done("yrstd", back))
                        for t in range(TILES):
                            norm.scaled("y", t, norm.yn[:, t], acc[:, t]).then_inc(vec.sem, 1)
                        dve.wait_ge(vec.sem, vec.done("yn1", back))
                        nc.vector.tensor_tensor(back.tiles(x), back.tiles(x), norm.yn[:, :, :], ALU.add)\
                            .then_inc(updated.sem, 1)

                pipeline(dve, n_seq, step)

            @block.scalar
            def _(act):
                def step(front, back):
                    if front:
                        to_act.wait_filled(act, "xnT", front)
                        nc.scalar.copy(xnT[front.parity][:, :], to_act.bank("xnT", front)[:, 0:T])\
                            .then_inc(to_act.drained.sem, 1)
                        act.wait_ge(lead_done.sem, lead_done.done("diff", front))
                        nc.scalar.activation(lead[:, :], diff[:, :], ACT.Tanh, scale=0.5)\
                            .then_inc(lead_done.sem, 1)
                    if back:
                        for e in range(EXPERTS):
                            to_act.wait_filled(act, f"h{e}", back)
                            nc.scalar.activation(hT[:, e % 2, :, :].rearrange("p a t -> p (a t)"),
                                                 to_act.bank(f"h{e}", back)[:, :], ACT.Silu)\
                                .then_inc(to_act.drained.sem, 1)

                pipeline(act, n_seq, step)

            @block.tensor
            def _(pe):
                def step(front, back):
                    if front:
                        to_act.wait_free(pe, "xnT", front)
                        for t in range(TILES):
                            pe.wait_ge(vec.sem, vec.done(f"xn{t}", front))
                            ins = nc.tensor.transpose(to_act.bank("xnT", front)[:, t * P:(t + 1) * P],
                                                      norm.xn[:, t], c["ident"][:, :])
                        ins.then_inc(to_act.filled.sem, 1)
                        to_act.wait_drained(pe, "xnT", front)
                        to_dve.wait_free(pe, "router", front)
                        for t in range(TILES):
                            ins = nc.tensor.matmul(
                                to_dve.bank("router", front)[:, t * EXPERTS:(t + 1) * EXPERTS],
                                xnT[front.parity][:, t * P:(t + 1) * P], w["router"][:, :],
                                start=True, stop=True)
                        ins.then_inc(to_dve.filled.sem, 1)
                    if back:
                        u = back.parity

                        def hidden(e):
                            to_act.wait_free(pe, f"h{e}", back)
                            for f in range(EF // P):
                                ins = nc.tensor.matmul(to_act.bank(f"h{e}", back)[:, f * T:(f + 1) * T],
                                                       w["e1"][:, e, f * P:(f + 1) * P], xnT[u][:, :],
                                                       start=True, stop=True)
                            ins.then_inc(to_act.filled.sem, 1)

                        def output(e):
                            to_act.wait_drained(pe, f"h{e}", back)
                            for t in range(TILES):
                                job = f"y{t}.{e // 4}"
                                if e % 4 == 0:
                                    to_dve.wait_free(pe, job, back)
                                for f in range(EF // P):
                                    ins = nc.tensor.matmul(
                                        to_dve.bank(job, back)[:, (e % 4) * D:(e % 4 + 1) * D],
                                        hT[:, e % 2, f, t * P:(t + 1) * P], w["e2"][:, e, f, :],
                                        start=f == 0, stop=f == EF // P - 1)
                                if e % 4 == 3:
                                    ins.then_inc(to_dve.filled.sem, 1)

                        hidden(0)
                        for e in range(1, EXPERTS):
                            hidden(e)
                            output(e - 1)
                        output(EXPERTS - 1)

                pipeline(pe, n_seq, step)

            @block.sync
            def _(sp):
                with sp.Fori(0, n_seq) as s:
                    sp.wait_ge(updated.sem, s + 1)
                    sp.dma_start(out_dram[:, bass.ds(s * TILES, TILES), :], x[:, bass.ds(s * TILES, TILES), :])\
                        .then_inc(finished, 16)
                sp.wait_ge(finished, 16 * n_seq)


def load(nc, name, pairs):
    with nc.semaphore(name) as loaded, nc.Block() as block:
        @block.sync
        def _(sp):
            for out, source in pairs:
                sp.dma_start(out, source).then_inc(loaded, 16)
            sp.wait_ge(loaded, 16 * len(pairs))


def chip_constants(nc, ctx, d):
    def sb(name, shape, dt=F32):
        return ctx.enter_context(nc.sbuf_tensor(name, shape, dt))

    c = {
        "ident": sb("ident_sb", [P, P]),
        "ident_bf": sb("ident_bf", [P, P], BF16),
        "mask_rows": sb("mask_rows", [P, P], BF16),
        "mask_cols": sb("mask_cols", [P, P], BF16),
        "mask_window": sb("mask_window", [P, SPAN], BF16),
        "pick": sb("pick_sb", [2 * LH, LH * P], F32R),
        "pick8": sb("pick8_sb", [2 * NH, NH * P], F32R),
        "next": sb("next_sb", [P, 2, P]),
        "minus_half": sb("minus_half", [P, 16]),
        "minus_one": sb("minus_one", [P, 16]),
        "eps": sb("eps", [P, TILES]),
        "carrier": sb("carrier", [P, 1]),
    }
    with ExitStack() as staging:
        def st(name, shape):
            return staging.enter_context(nc.sbuf_tensor(name, shape, F32))

        masks, window = st("masks_f32", [P, 2, P]), st("window_f32", [P, SPAN])
        pick, pick8 = st("pick_f32", [2 * LH, LH * P]), st("pick8_f32", [2 * NH, NH * P])
        ready = c["ready"] = ctx.enter_context(nc.semaphore("constants_ready"))
        load(nc, "constants_loaded", [
            (c["ident"][:, :], d["ident"]), (c["next"][:, :, :], d["next_mat"]),
            (masks[:, :, :], d["masks"]), (window[:, :], d["window_mat"]),
            (pick[:, :], d["pick"]), (pick8[:, :], d["pick8_mat"])])
        with nc.Block() as block:
            @block.vector
            def _(dve):
                for out, source in ((c["ident_bf"], c["ident"][:, :]), (c["mask_rows"], masks[:, 0]),
                                    (c["mask_cols"], masks[:, 1]), (c["mask_window"], window[:, :]),
                                    (c["pick"], pick[:, :]), (c["pick8"], pick8[:, :])):
                    nc.vector.tensor_copy(out[:, :], source).then_inc(ready, 1)
                nc.vector.memset(c["minus_half"][:, :], -0.5).then_inc(ready, 1)
                nc.vector.memset(c["eps"][:, :], LN_EPS).then_inc(ready, 1)
                nc.vector.memset(c["minus_one"][:, :], -1.0).then_inc(ready, 1)
                dve.wait_ge(ready, 9)
    return c


def token_phase(nc, n_seq, x, c, d):
    with ExitStack() as scope:
        def sb(name, shape, dt=F32):
            return scope.enter_context(nc.sbuf_tensor(name + "_sb", shape, dt))

        w = {
            "tq": sb("tq", [D, GROUPS, P]),
            "tk": sb("tk", [D, GROUPS, P]),
            "tv": sb("tv", [D, D]),
            "t_out": sb("t_out", [D, D]),
            "bits": sb("bits", [D, P]),
            "basis": sb("basis", [8, 2 * BITS, 2 * BITS]),
            "transform": sb("transform", [TH, NT]),
            "scalars": sb("scalars", [P, 4]),
        }
        load(nc, "token_loaded", [
            *((w[name][:], d[name]) for name in list(w)[:-1]),
            (w["scalars"][:, :], d["scalars"].partition_broadcast(P))])
        token_attention(nc, n_seq, x, w, c)


def ffn_phase(nc, n_seq, x, c, d):
    with ExitStack() as scope:
        def sb(name, shape, dt=F32):
            return scope.enter_context(nc.sbuf_tensor(name + "_sb", shape, dt))

        c["rotary"] = sb("rotary", [P, TILES, 4, HD])
        w = {
            "wqkv": sb("wqkv", [D, LAYERS, 3 * INNER]),
            "wo": sb("wo", [P, LAYERS, INNER // P, D]),
            "w1": sb("w1", [D, LAYERS, 2 * HID]),
            "w2": sb("w2", [P, LAYERS, 3, D]),
            "b1": sb("b1", [P, LAYERS, 2, 3]),
            "ln_g": sb("ln_g", [D, LAYERS]),
            "ln_b": sb("ln_b", [D, LAYERS]),
            "q_scale": sb("q_scale", [P, LAYERS, HD]),
            "k_scale": sb("k_scale", [P, LAYERS, HD]),
        }
        pairs = [(c["rotary"][:], d["rotary_tab"])]
        pairs += [(w[name][:], d[name]) for name in ("w2", "b1", "ln_g", "ln_b")]
        for layer in range(LAYERS):
            pairs += [
                (w["wqkv"][:, layer], d["L0_ffn_wqkv"][layer]),
                (w["wo"][:, layer], d["L0_ffn_wo"][layer].rearrange("(a p) n -> p a n", p=P)),
                (w["w1"][:, layer], d["L0_ffn_w1"][layer]),
                (w["q_scale"][:, layer], d["L0_ffn_q_scale"][layer].partition_broadcast(P)),
                (w["k_scale"][:, layer], d["L0_ffn_k_scale"][layer].partition_broadcast(P))]
        load(nc, "ffn_loaded", pairs)
        ffn_layers(nc, n_seq, x, w, c)


def latent_phase(nc, n_seq, x, c, d):
    with ExitStack() as scope:
        def sb(name, shape, dt=F32):
            return scope.enter_context(nc.sbuf_tensor(name + "_sb", shape, dt))

        w = {
            "kv_down": sb("kv_down", [D, D]),
            "kv_up": sb("kv_up", [D, 2 * LH * LD]),
            "q": sb("wq", [D, LH * LD]),
            "l_out": sb("l_out", [P, LH * LD // P, D]),
        }
        load(nc, "latent_loaded", [
            (w["kv_down"][:, :], d["L1_attn_w_kv_down"]), (w["kv_up"][:, :], d["L1_attn_w_kv_up"]),
            (w["q"][:, :], d["L1_attn_w_q"]),
            (w["l_out"][:, :, :], d["L1_attn_w_out"].rearrange("(c p) n -> p c n", p=P))])
        latent_attention(nc, n_seq, x, w, c)


def experts_phase(nc, n_seq, x, c, d, finished):
    with ExitStack() as scope:
        def sb(name, shape, dt=F32):
            return scope.enter_context(nc.sbuf_tensor(name + "_sb", shape, dt))

        w = {
            "router": sb("router", [D, EXPERTS]),
            "e1": sb("e1", [D, EXPERTS, EF]),
            "e2": sb("e2", [P, EXPERTS, EF // P, D]),
        }
        load(nc, "experts_loaded", [
            (w["router"][:, :], d["L1_ffn_router_w"]),
            (w["e1"][:, :, :], d["L1_ffn_w1"].rearrange("e d f -> d e f")),
            *((w["e2"][:, e], d["L1_ffn_w2"][e].rearrange("(a p) n -> p a n", p=P))
              for e in range(EXPERTS))])
        experts_layer(nc, n_seq, x, w, c, d["out"].rearrange("(n p) d -> p n d", p=P), finished)


def build(nc, n_seq, d, phases=(token_phase, ffn_phase, latent_phase)):
    with ExitStack() as ctx:
        x = ctx.enter_context(nc.sbuf_tensor("x_sb", [P, n_seq * TILES, D], F32))
        c = chip_constants(nc, ctx, d)
        load(nc, "x_loaded", [(x[:, :, :], d["x"].rearrange("(n p) d -> p n d", p=P))])
        finished = ctx.enter_context(nc.semaphore("finished"))
        for phase in phases:
            phase(nc, n_seq, x, c, d)
        experts_phase(nc, n_seq, x, c, d, finished)


def constants():
    f32 = np.float32
    row, col = np.arange(P)[:, None], np.arange(P)[None]
    causal = np.where(col > row, MASKED, 0.0).astype(f32)
    window = np.arange(SPAN)[None]

    def picker(heads):
        out = np.zeros((2, heads, heads, P), f32)
        for h in range(heads):
            out[:, h, h] = 1.0
        return out.reshape(2 * heads, heads * P)

    half = np.arange(0, HD, 2, dtype=f32)
    inv_freq = (1.0 / 10000.0 ** (half / HD)).astype(f32)
    angle = (np.arange(T, dtype=f32)[:, None] * inv_freq[None]).astype(f32)
    angle = np.concatenate([angle, angle], -1).astype(np.float64)
    base = (half.astype(np.float64) + 0.4 * HD) / (1.4 * HD)
    scale = base[None] ** ((np.arange(T) - T // 2) / float(WINDOW // 2))[:, None]
    scale = np.concatenate([scale, scale], -1)
    sign = np.where(np.arange(HD) < HD // 2, -1.0, 1.0)
    cos, sin = np.cos(angle), np.sin(angle) * sign
    rotary = np.stack([cos * scale, sin * scale, cos / scale, sin / scale], 1)

    following = np.zeros((P, 2, P), f32)
    following[np.arange(P - 1), 0, np.arange(1, P)] = 1.0
    following[P - 1, 1, 0] = 1.0
    return {
        "ident": np.eye(P, dtype=f32),
        "masks": np.ascontiguousarray(np.stack([causal, causal.T], 1)),
        "pick": picker(LH),
        "pick8_mat": picker(NH),
        "window_mat": np.where((window >= row) & (window <= row + WINDOW), 0.0, MASKED).astype(f32),
        "rotary_tab": np.ascontiguousarray(
            rotary.reshape(TILES, P, 4, HD).transpose(1, 0, 2, 3)).astype(f32),
        "next_mat": following,
    }


def layouts(a):
    f32 = np.float32
    qkv = a["L0_attn_qkv_w"].reshape(3, TH, TD, D)

    def grouped(weights):
        out = np.zeros((D, GROUPS, GROUPS, ROWS), f32)
        out[..., :TD] = weights.reshape(GROUPS, GROUPS, TD, D).transpose(3, 0, 1, 2)
        return out.reshape(D, GROUPS, P)

    bits = np.zeros((D, GROUPS, ROWS), f32)
    bits[..., :BITS] = a["L0_attn_hex_w"].T[:, None]
    bits[..., BITS:2 * BITS] = a["L0_attn_q6_w"].T[:, None]
    basis = np.zeros((NT + 1, 2 * BITS, 2 * BITS), f32)
    basis[:NT, BITS:, BITS:] = a["L0_attn_transforms"].transpose(0, 2, 1)
    basis[NT, np.arange(BITS), np.arange(BITS)] = 1.0

    w2 = np.zeros((P, LAYERS, 3, D), f32)
    b1 = np.zeros((P, LAYERS, 2, 3), f32)
    at = 0
    for n, rows in enumerate(CHUNKS):
        w2[:rows, :, n] = a["L0_ffn_w2"][:, at:at + rows].transpose(1, 0, 2)
        for part in range(2):
            b1[:rows, :, part, n] = a["L0_ffn_b1"][:, part * HID + at:part * HID + at + rows].T
        at += rows
    w2[CHUNKS[-1], :, 2] = a["L0_ffn_b2"]
    out = {
        "x": a["L0_attn_x"].reshape(-1, D),
        "tq": grouped(qkv[0]), "tk": grouped(qkv[1]), "tv": qkv[2].reshape(TH * TD, D).T,
        "t_out": a["L0_attn_out_w"].T,
        "bits": bits.reshape(D, P), "basis": basis,
        "transform": a["L0_attn_transform_weights"],
        "scalars": np.concatenate([a["L0_attn_hamming_lambda_logit"].reshape(1),
                                   a["L0_attn_scale_logit"].reshape(1),
                                   a["L0_attn_sips_alpha"], a["L0_attn_sips_beta"]]),
        "w2": w2, "b1": b1, "ln_g": a["L0_ffn_ln_g"].T, "ln_b": a["L0_ffn_ln_b"].T,
    }
    for name in ("L0_ffn_wqkv", "L0_ffn_wo", "L0_ffn_w1", "L0_ffn_q_scale", "L0_ffn_k_scale",
                 "L1_attn_w_kv_down", "L1_attn_w_kv_up", "L1_attn_w_q", "L1_attn_w_out",
                 "L1_ffn_router_w", "L1_ffn_w1", "L1_ffn_w2"):
        out[name] = a[name]
    return {k: np.ascontiguousarray(v) for k, v in out.items()}


def kernel(**inputs):
    import concourse.bacc as bacc
    from concourse.bass_utils import run_bass_kernel_spmd

    given = {k: np.asarray(v) for k, v in inputs.items()}
    n_seq = given["L0_attn_x"].shape[0]
    arrays = {**constants(), **layouts(given)}
    nc = bacc.Bacc("TRN2", target_bir_lowering=False, num_devices=1)
    dram = {k: nc.dram_tensor(k, v.shape, F32, kind="ExternalInput").ap() for k, v in arrays.items()}
    dram["out"] = nc.dram_tensor("out", (n_seq * T, D), F32, kind="ExternalOutput").ap()
    build(nc, n_seq, dram)
    result = run_bass_kernel_spmd(nc, [arrays], core_ids=[0])
    return result.results[0]["out"].reshape(n_seq, T, D)
```

```python
from contextlib import ExitStack

import numpy as np

import concourse.bass as bass
from concourse import mybir

F32 = mybir.dt.float32
F32R = mybir.dt.float32r
BF16 = mybir.dt.bfloat16
ACT = mybir.ActivationFunctionType
ALU = mybir.AluOpType
AX = mybir.AxisListType

P = 128
D = 128
T = 256
TILES = T // P
BANK = 512
RING = 4
LN_EPS = 1e-5
MASKED = -1e30


class Seq:

    def __init__(self, number, parity, of):
        self.number, self.parity, self.of = number, parity, of
        self.first = isinstance(number, int) and number == 0

    def before(self):
        return Seq(self.number - 1, 1 - self.parity, self.of)

    def tiles(self, whole):
        return whole[:, bass.ds(self.number * TILES, TILES), :]

    def tile(self, whole, t):
        return whole[:, bass.ds(self.number * TILES + t, 1), :].rearrange("p a d -> p (a d)")


def pipeline(eng, n_seq, step):
    def at(number):
        return Seq(number, number % 2, n_seq) if 0 <= number < n_seq else None

    for s in range(4):
        step(at(s), at(s - 1), at(s - 2))
    with eng.Fori(0, (n_seq - 4) // 2) as k:
        step(Seq(k * 2 + 4, 0, n_seq), Seq(k * 2 + 3, 1, n_seq), Seq(k * 2 + 2, 0, n_seq))
        step(Seq(k * 2 + 5, 1, n_seq), Seq(k * 2 + 4, 0, n_seq), Seq(k * 2 + 3, 1, n_seq))
    for s in range(n_seq, n_seq + 2):
        step(at(s), at(s - 1), at(s - 2))


def lagging(i, lag, units, back, done):
    return (i - lag, back) if i >= lag else (i - lag + units, done)


class Count:

    def __init__(self, sem, order, front=(), done=()):
        self.sem, self.order = sem, list(order)
        assert len(set(self.order)) == len(self.order)
        self.part = {e: 0 if e in front else 2 if e in done else 1 for e in self.order}

    def events(self, step, of):
        return [e for e in self.order if 0 <= step - self.part[e] < of]

    def place(self, event, seq):
        step = seq.number + self.part[event]
        if isinstance(step, int):
            return sum(len(self.events(s, seq.of)) for s in range(step)) \
                + self.events(step, seq.of).index(event)
        filling = len(self.events(0, seq.of)) + len(self.events(1, seq.of))
        return step * len(self.order) + (filling - 2 * len(self.order) + self.order.index(event))

    def done(self, event, seq):
        return self.place(event, seq) + 1

    def slot(self, event, seq, slots):
        if isinstance(seq.number, int):
            return self.place(event, seq) % slots
        filling = len(self.events(0, seq.of)) + len(self.events(1, seq.of))
        odd = (seq.parity + self.part[event]) % 2
        return (odd * len(self.order) + filling + self.order.index(event)) % slots


class Ring:

    def __init__(self, banks, filled, drained, order, front=(), done=()):
        assert 2 * len(order) % len(banks) == 0
        self.banks = banks
        self.filled, self.drained = Count(filled, order, front, done), Count(drained, order, front, done)

    def bank(self, job, seq):
        return self.banks[self.filled.slot(job, seq, len(self.banks))]

    def wait_free(self, pe, job, seq):
        ring = len(self.banks)
        place = self.filled.place(job, seq)
        if not (isinstance(place, int) and place < ring):
            pe.wait_ge(self.drained.sem, place - (ring - 1))

    def wait_filled(self, eng, job, seq):
        eng.wait_ge(self.filled.sem, self.filled.done(job, seq))

    def wait_drained(self, eng, job, seq):
        eng.wait_ge(self.drained.sem, self.drained.done(job, seq))


def wait_apart(nc, eng, c, sem, value):
    eng.wait_ge(sem, value)
    nc.vector.tensor_copy(c["carrier"][:, 0:1], c["eps"][:, 0:1])


PRE_NORM = ["stats0", "stats1", "mv0", "mv1", "xn0", "xn1"]
POST_NORM = ["ystats0", "ystats1", "ymv0", "ymv1", "yn0"]
COPIED_NORM = POST_NORM + ["yn1"]
RSQRT = ["var", "rstd", "yvar", "yrstd"]


class Norm:

    def __init__(self, nc, ctx, prefix, vec, rst, c):
        def sb(name, shape):
            return ctx.enter_context(nc.sbuf_tensor(prefix + name, shape, F32))

        self.nc, self.vec, self.rst, self.c = nc, vec, rst, c
        self.stats = {"": sb("stats", [P, TILES, 6]), "y": sb("ystats", [P, TILES, 6])}
        self.mv = {"": sb("mv", [P, TILES, 2]), "y": sb("ymv", [P, TILES, 2])}
        self.var = {"": sb("var", [P, TILES]), "y": sb("yvar", [P, TILES])}
        self.rstd = {"": sb("rstd", [P, TILES]), "y": sb("yrstd", [P, TILES])}
        self.xn = sb("xn", [P, TILES, D])
        self.yn = sb("yn", [P, TILES, D])

    def rsqrt(self, pool, which, seq):
        nc, vec, rst = self.nc, self.vec, self.rst
        pool.wait_ge(vec.sem, vec.done(which + "mv1", seq))
        nc.gpsimd.tensor_tensor(self.var[which][:, :], self.mv[which][:, :, 1], self.c["eps"][:, 0:TILES],
                                ALU.add)\
            .then_inc(rst.sem, 1)
        pool.wait_ge(rst.sem, rst.done(which + "var", seq))
        nc.gpsimd.tensor_tensor(self.rstd[which][:, :], self.var[which][:, :],
                                self.c["minus_half"][:, 0:TILES], ALU.pow).then_inc(rst.sem, 1)

    def moments(self, dve, which, seq, tiles):
        nc, vec = self.nc, self.vec
        for t in range(TILES):
            nc.vector.bn_stats(self.stats[which][:, t], tiles[t]).then_inc(vec.sem, 1)
        wait_apart(nc, dve, self.c, vec.sem, vec.done(f"{which}stats{TILES - 1}", seq))
        for t in range(TILES):
            nc.vector.bn_aggr(self.mv[which][:, t], self.stats[which][:, t]).then_inc(vec.sem, 1)

    def scaled(self, which, t, out, tile):
        mv, rstd = self.mv[which], self.rstd[which]
        return self.nc.vector.tensor_scalar(out, tile, mv[:, t, 0:1], rstd[:, t:t + 1],
                                            ALU.subtract, ALU.mult)

    def pre(self, dve, seq, x, to_act):
        self.pre_moments(dve, seq, x)
        self.pre_scaled(dve, seq, x, to_act)

    def pre_moments(self, dve, seq, x):
        self.moments(dve, "", seq, [seq.tile(x, t) for t in range(TILES)])

    def pre_scaled(self, dve, seq, x, to_act, keep=None):
        dve.wait_ge(self.rst.sem, self.rst.done("rstd", seq))
        for t in range(TILES if keep is not None else 0):
            self.scaled("", t, seq.tile(keep, t), seq.tile(x, t))
        if not seq.first:
            to_act.wait_filled(dve, "xnT", seq.before())
        for t in range(TILES):
            self.scaled("", t, self.xn[:, t], seq.tile(x, t)).then_inc(self.vec.sem, 1)

    def post(self, dve, seq, x, ring, job):
        self.post_moments(dve, seq, ring, job)
        return self.post_scaled(dve, seq, x, ring, job)

    def post_moments(self, dve, seq, ring, job):
        bank = ring.bank(job, seq)
        wait_apart(self.nc, dve, self.c, ring.filled.sem, ring.filled.done(job, seq))
        self.moments(dve, "y", seq, [bank[:, t * D:(t + 1) * D] for t in range(TILES)])

    def post_scaled(self, dve, seq, x, ring, job):
        nc, vec = self.nc, self.vec
        bank = ring.bank(job, seq)
        dve.wait_ge(self.rst.sem, self.rst.done("yrstd", seq))
        self.scaled("y", 0, self.yn[:, 0], bank[:, 0:D]).then_inc(vec.sem, 1)
        self.scaled("y", 1, self.yn[:, 1], bank[:, D:2 * D]).then_inc(ring.drained.sem, 1)
        dve.wait_ge(vec.sem, vec.done("yn0", seq))
        ring.wait_drained(dve, job, seq)
        return nc.vector.tensor_tensor(seq.tiles(x), seq.tiles(x), self.yn[:, :, :], ALU.add)

    def post_copied_moments(self, dve, seq, y):
        self.moments(dve, "y", seq, [y[:, t] for t in range(TILES)])

    def post_copied_scaled(self, dve, seq, x, y):
        nc, vec = self.nc, self.vec
        dve.wait_ge(self.rst.sem, self.rst.done("yrstd", seq))
        for t in range(TILES):
            self.scaled("y", t, self.yn[:, t], y[:, t]).then_inc(vec.sem, 1)
        dve.wait_ge(vec.sem, vec.done("yn1", seq))
        return nc.vector.tensor_tensor(seq.tiles(x), seq.tiles(x), self.yn[:, :, :], ALU.add)


TH, TD = 16, 8
GROUPS = 4
ROWS = 32
BITS = 6
NT = 7


def token_attention(nc, n_seq, x, w, c):
    units = [f"{n}.{kind}" for n in range(GROUPS) for kind in ("i1a", "i1b", "i0")]
    turns = len(units)
    SHIFT, EXP, LAG, SLOTS, TANHS = 1, 2, 4, 6, 4
    VALUES, LATE_VALUES = {LAG + 3: "yT0", LAG + 6: "yT1"}, {LAG + 9 - turns: "yT2", LAG + 13 - turns: "yT3"}
    PROJECT = LAG + 2
    DIVIDE, BACK, OUT = LAG + 2, LAG + 4, LAG + 5
    front_at = {3: ["xnT"], 4: ["right"], 5: ["q0"], 6: ["k0"], 7: ["q1"], 8: ["k1"], 9: ["left0"],
                10: ["left1"]}
    front_jobs = [job for i in sorted(front_at) for job in front_at[i]]
    act_front = ["xnT", "right"]
    dve_front = [job for job in front_jobs if job not in act_front]
    act_order, dve_order = [], []
    for i in range(turns):
        act_order.append("raw" + units[i])
        dve_order.append("bil" + units[i])
        act_order += ["v0", "v1"] if i == PROJECT else []
        (dve_order if i % 2 else act_order).append("pT" + units[i - LAG])
        act_order += [jobs[i] for jobs in (VALUES, LATE_VALUES) if i in jobs]
        for job in front_at.get(i, []):
            (act_order if job in act_front else dve_order).append(job)
        act_order += {BACK: ["oT"], OUT: ["out"]}.get(i, [])
        dve_order += ["o0", "o1"] if i == DIVIDE else []

    def late(lag):
        return units[turns - lag:]

    def in_turns(lag):
        return late(lag) + units[:turns - lag]

    def unit(name):
        n, kind = name.split(".")
        return int(n), {"i1a": (0, 1), "i1b": (2, 3), "i0": (0, 1, 2, 3)}[kind], int(kind[1])

    with ExitStack() as ctx:
        def sb(name, shape, dt=F32):
            return ctx.enter_context(nc.sbuf_tensor("t_" + name, shape, dt))

        def sem(name):
            return ctx.enter_context(nc.semaphore("t_" + name))

        q = [sb(f"q{u}", [P, GROUPS, T], F32R) for u in range(2)]
        k = [sb(f"k{u}", [P, GROUPS, T], F32R) for u in range(2)]
        left = [sb(f"left{u}", [P, GROUPS, T], F32R) for u in range(2)]
        right = [sb(f"right{u}", [P, GROUPS, 2, T], F32R) for u in range(2)]
        bits = sb("bits", [P, T])
        high = sb("high", [P, 2, BANK], F32R)
        v = sb("v", [P, TILES, TH, ROWS])
        xnT = [sb(f"xnT{u}", [P, T]) for u in range(2)]
        bilinear = sb("bilinear", [2 * BITS, TH, ROWS])
        tanh_qk = sb("tanh_qk", [P, TANHS, BANK])
        probs = sb("probs", [P, SLOTS, BANK])
        neg_max = sb("neg_max", [P, len(units), 4])
        pT = sb("pT", [P, len(units), BANK])
        yT = sb("yT", [P, GROUPS, T])
        inv_den = sb("inv_den", [P, TILES, GROUPS, GROUPS])
        o = sb("o", [P, TILES, D])
        oT = sb("oT", [P, T])
        y = sb("y", [P, TILES, D])
        act_banks = [ctx.enter_context(nc.psum_tensor(f"t_act{i}", [P, BANK], F32)) for i in range(RING)]
        dve_banks = [ctx.enter_context(nc.psum_tensor(f"t_dve{i}", [P, BANK], F32)) for i in range(RING)]
        late_jobs = ["pT" + name for name in late(LAG)] + ["yT2", "yT3", "o0", "o1", "oT", "out"]
        to_act = Ring(act_banks, sem("act_filled"), sem("act_drained"), act_order, act_front, late_jobs)
        to_dve = Ring(dve_banks, sem("dve_filled"), sem("dve_drained"), dve_order, dve_front, late_jobs)
        maxed = Count(sem("maxed"), units)
        exped = Count(sem("exped"), in_turns(EXP), [], late(EXP))
        den = Count(sem("den"), ["o0", "o1"], [], ["o0", "o1"])
        shifted = Count(sem("shifted"), in_turns(SHIFT), [], late(SHIFT))
        rounded = Count(sem("rounded"), dve_front, dve_front)
        split = Count(sem("split"), ["low"], ["low"])
        vec = Count(sem("vec"), PRE_NORM + COPIED_NORM, PRE_NORM, COPIED_NORM)
        rst = Count(sem("rst"), RSQRT, RSQRT[:2], RSQRT[2:])
        norm = Norm(nc, ctx, "t_", vec, rst, c)
        setup_pool, setup_act, setup_dve, setup_pe = (sem("setup_" + e) for e in ("pool", "act", "dve", "pe"))
        lam, scl = w["scalars"][:, 0:1], w["scalars"][:, 1:2]
        alpha, beta = w["scalars"][:, 2:3], w["scalars"][:, 3:4]
        sig = sb("sig", [P, 2, 3])
        inv_beta = sb("inv_beta", [P, 1])
        tw = sb("tw", [TH, 3, 8])
        tw_sum = sb("tw_sum", [TH, 3])
        twT = sb("twT", [8, TH])

        with nc.Block() as block:
            @block.gpsimd
            def _(pool):
                nc.gpsimd.memset(bilinear[:, :, :], 0.0).then_inc(setup_pool, 1)
                nc.gpsimd.memset(v[:, :, :, :], 0.0).then_inc(setup_pool, 1)
                for u in range(2):
                    nc.gpsimd.memset(right[u][:, :, :, :].bitcast(F32), 0.0).then_inc(setup_pool, 1)
                pool.wait_ge(setup_pool, 4)
                nc.gpsimd.memset(v[:, :, :, TD:TD + 1], 1.0).then_inc(setup_pool, 1)

                def step(front, back, done):
                    for i in range(turns):
                        j, seq = lagging(i, SHIFT, turns, back, done)
                        if seq:
                            n, gs, t = unit(units[j])
                            pool.wait_ge(maxed.sem, maxed.done(units[j], seq))
                            p = probs[:, j % SLOTS, :].rearrange("p (h j) -> p h j", h=len(gs))
                            nc.gpsimd.tensor_tensor(
                                p, p, neg_max[:, j, 0:len(gs)].unsqueeze(2)
                                .broadcast_to((P, len(gs), P * (t + 1))), ALU.add).then_inc(shifted.sem, 1)
                        if front and i == 0:
                            norm.rsqrt(pool, "", front)
                        if done and i == OUT + 1:
                            norm.rsqrt(pool, "y", done)

                pipeline(pool, n_seq, step)

            @block.vector
            def _(dve):
                nc.vector.reciprocal(inv_beta[:, :], beta).then_inc(setup_dve, 1)
                nc.vector.tensor_reduce(tw_sum[:, 0:1], w["transform"][:, :], AX.X, ALU.max)\
                    .then_inc(setup_dve, 1)
                dve.wait_ge(setup_dve, 2)
                nc.vector.tensor_scalar(tw[:, 0, 0:NT], w["transform"][:, :], tw_sum[:, 0:1], None,
                                        ALU.subtract).then_inc(setup_dve, 1)
                dve.wait_ge(setup_act, 2)
                nc.vector.tensor_scalar(sig[:, :, 1], sig[:, :, 0], 1.0, None, ALU.add)\
                    .then_inc(setup_dve, 1)
                dve.wait_ge(setup_dve, 4)
                nc.vector.reciprocal(sig[:, :, 2], sig[:, :, 1]).then_inc(setup_dve, 1)
                nc.vector.reciprocal(tw_sum[:, 2:3], tw_sum[:, 1:2]).then_inc(setup_dve, 1)
                dve.wait_ge(setup_dve, 6)
                nc.vector.tensor_scalar(tw[:, 2, 0:NT], tw[:, 1, 0:NT], tw_sum[:, 2:3],
                                        sig[0:TH, 1, 2:3], ALU.mult, ALU.mult).then_inc(setup_dve, 1)
                nc.vector.tensor_scalar(tw[:, 2, NT:NT + 1], sig[0:TH, 0, 2:3], 0.5, None, ALU.mult)\
                    .then_inc(setup_dve, 1)
                dve.wait_ge(setup_dve, 7)
                nc.vector.tensor_scalar(tw[:, 2, 0:NT], tw[:, 2, 0:NT], 1.0 / 3.0, None, ALU.mult)\
                    .then_inc(setup_dve, 1)
                dve.wait_ge(setup_pe, 1)
                nc.vector.tensor_copy(twT[:, :], dve_banks[0][0:8, 0:TH]).then_inc(setup_dve, 1)
                dve.wait_ge(setup_pe, 2)
                dve.wait_ge(setup_pool, 1)
                for copy in range(2):
                    nc.vector.tensor_copy(
                        bilinear[:, :, 2 * BITS * copy:2 * BITS * (copy + 1)],
                        dve_banks[1][0:2 * BITS, 0:2 * BITS * TH].rearrange("a (b h) -> a h b", h=TH))\
                        .then_inc(setup_dve, 1)

                def combine(i, back):
                    name = units[i]
                    n, gs, t = unit(name)
                    to_act.wait_drained(dve, "raw" + name, back)
                    to_dve.wait_filled(dve, "bil" + name, back)
                    before, seq = (i - SLOTS, back) if i >= SLOTS else (i - SLOTS + len(units), None)
                    if before % 2 == LAG % 2 and (seq or not back.first):
                        to_act.wait_filled(dve, "pT" + units[before], seq or back.before())
                    nc.vector.scalar_tensor_tensor(
                        probs[:, i % SLOTS, :], tanh_qk[:, i % TANHS, :], alpha,
                        to_dve.bank("bil" + name, back)[:, :], ALU.mult, ALU.add)\
                        .then_inc(to_dve.drained.sem, 1)
                    to_dve.wait_drained(dve, "bil" + name, back)
                    nc.vector.tensor_reduce(
                        neg_max[:, i, 0:len(gs)],
                        probs[:, i % SLOTS, :].rearrange("p (h j) -> p h j", h=len(gs)),
                        AX.X, ALU.max, negate=True).then_inc(maxed.sem, 1)

                def step(front, back, done):
                    for i in range(turns):
                        if back:
                            combine(i, back)
                        if front and i == 0:
                            norm.pre_moments(dve, front, x)
                        if front and i == 1:
                            norm.pre_scaled(dve, front, x, to_act)
                        j, seq = lagging(i, LAG, turns, back, done)
                        if seq and i % 2 == 1:
                            job = "pT" + units[j]
                            to_dve.wait_filled(dve, job, seq)
                            nc.vector.tensor_copy(pT[:, j, :], to_dve.bank(job, seq)[:, :])\
                                .then_inc(to_dve.drained.sem, 1)
                        if done and i == OUT + 1:
                            wait_apart(nc, dve, c, to_act.drained.sem, to_act.drained.done("out", done))
                            norm.post_copied_moments(dve, done, y)
                        if done and i == OUT + 2:
                            norm.post_copied_scaled(dve, done, x, y)
                        if front and i == 6:
                            to_act.wait_drained(dve, "right", front)
                            for n in range(GROUPS):
                                rows = slice(ROWS * n, ROWS * (n + 1))
                                parts = right[front.parity][rows, n]
                                ins = nc.vector.tensor_tensor(parts[:, 1, :], bits[rows, :],
                                                              parts[:, 0, :].bitcast(F32), ALU.subtract)
                            ins.then_inc(split.sem, 1)
                        for job in front_at.get(i, []) if front else []:
                            if job in dve_front:
                                u, j = front.parity, dve_front.index(job)
                                out, g = {"q": q, "k": k, "l": left}[job[0]][u], 2 * int(job[-1])
                                low_rows = w["low_rows"][:, "qkl".index(job[0]):"qkl".index(job[0]) + 1]
                                dve.wait_ge(rounded.sem, rounded.done(job, front))
                                nc.vector.scalar_tensor_tensor(
                                    out[:, g:g + 2, :].rearrange("p a t -> p (a t)"),
                                    high[:, j % 2, :].bitcast(F32), low_rows,
                                    to_dve.bank(job, front)[:, :], ALU.mult, ALU.add)\
                                    .then_inc(to_dve.drained.sem, 1)
                        for t in range(TILES if done and i == DIVIDE else 0):
                            job = f"o{t}"
                            bank = to_dve.bank(job, done)[:, :].rearrange("p (n g r) -> p n g r", n=GROUPS,
                                                                          g=GROUPS)
                            to_dve.wait_filled(dve, job, done)
                            nc.vector.reciprocal(inv_den[:, t], bank[:, :, :, TD]).then_inc(den.sem, 1)
                            dve.wait_ge(den.sem, den.done(job, done))
                            nc.vector.tensor_tensor(
                                o[:, t, :].rearrange("p (g n d) -> p n g d", g=GROUPS, n=GROUPS),
                                bank[:, :, :, 0:TD],
                                inv_den[:, t].unsqueeze(3).broadcast_to((P, GROUPS, GROUPS, TD)), ALU.mult)\
                                .then_inc(to_dve.drained.sem, 1)

                pipeline(dve, n_seq, step)

            @block.scalar
            def _(act):
                nc.scalar.activation(sig[:, :, 0], w["scalars"][:, 0:2], ACT.Exp, scale=-1.0)\
                    .then_inc(setup_act, 1)
                act.wait_ge(setup_dve, 3)
                nc.scalar.activation(tw[:, 1, 0:NT], tw[:, 0, 0:NT], ACT.Exp, scale=2.0,
                                     accum_out=tw_sum[:, 1:2]).then_inc(setup_act, 1)

                def step(front, back, done):
                    for i in range(turns):
                        if back:
                            to_act.wait_filled(act, "raw" + units[i], back)
                            if i >= TANHS:
                                to_dve.wait_drained(act, "bil" + units[i - TANHS], back)
                            elif not back.first:
                                to_dve.wait_drained(act, "bil" + units[i - TANHS], back.before())
                            nc.scalar.activation(tanh_qk[:, i % TANHS, :],
                                                 to_act.bank("raw" + units[i], back)[:, :],
                                                 ACT.Tanh, scale=inv_beta[:, :])\
                                .then_inc(to_act.drained.sem, 1)
                        j, seq = lagging(i, EXP, turns, back, done)
                        if seq:
                            act.wait_ge(shifted.sem, shifted.done(units[j], seq))
                            p = probs[:, j % SLOTS, :]
                            nc.scalar.activation(p, p, ACT.Exp).then_inc(exped.sem, 1)
                        for t in range(TILES if back and i == PROJECT else 0):
                            to_act.wait_filled(act, f"v{t}", back)
                            nc.scalar.copy(v[:, t, :, 0:TD],
                                           to_act.bank(f"v{t}", back)[:, 0:D].rearrange("p (h d) -> p h d", d=TD))\
                                .then_inc(to_act.drained.sem, 1)
                        j, seq = lagging(i, LAG, turns, back, done)
                        if seq and i % 2 == 0:
                            job = "pT" + units[j]
                            to_act.wait_filled(act, job, seq)
                            nc.scalar.copy(pT[:, j, :], to_act.bank(job, seq)[:, :])\
                                .then_inc(to_act.drained.sem, 1)
                        for jobs, seq in ((VALUES, back), (LATE_VALUES, done)):
                            if i in jobs and seq:
                                to_act.wait_filled(act, jobs[i], seq)
                                nc.scalar.copy(yT[:, int(jobs[i][2]), :], to_act.bank(jobs[i], seq)[:, 0:T])\
                                    .then_inc(to_act.drained.sem, 1)
                        for job in front_at.get(i, []) if front else []:
                            if job == "xnT":
                                to_act.wait_filled(act, "xnT", front)
                                nc.scalar.copy(xnT[front.parity][:, :], to_act.bank("xnT", front)[:, 0:T])\
                                    .then_inc(to_act.drained.sem, 1)
                            elif job == "right":
                                to_act.wait_filled(act, "right", front)
                                if not front.first:
                                    act.wait_ge(split.sem, split.done("low", front.before()))
                                nc.scalar.activation(bits[:, :], to_act.bank("right", front)[:, 0:T],
                                                     ACT.Tanh)
                                for n in range(GROUPS):
                                    rows = slice(ROWS * n, ROWS * (n + 1))
                                    ins = nc.scalar.activation(right[front.parity][rows, n, 0, :],
                                                               to_act.bank("right", front)[rows, 0:T],
                                                               ACT.Tanh)
                                ins.then_inc(to_act.drained.sem, 1)
                            else:
                                j = dve_front.index(job)
                                to_dve.wait_filled(act, job, front)
                                if j >= 2:
                                    to_dve.wait_drained(act, dve_front[j - 2], front)
                                elif not front.first:
                                    to_dve.wait_drained(act, dve_front[j - 2], front.before())
                                nc.scalar.copy(high[:, j % 2, :], to_dve.bank(job, front)[:, :])\
                                    .then_inc(rounded.sem, 1)
                        if done and i == BACK:
                            to_act.wait_filled(act, "oT", done)
                            nc.scalar.copy(oT[:, :], to_act.bank("oT", done)[:, 0:T])\
                                .then_inc(to_act.drained.sem, 1)
                        if done and i == OUT:
                            to_act.wait_filled(act, "out", done)
                            nc.scalar.copy(y[:, :, :].rearrange("p a d -> p (a d)"),
                                           to_act.bank("out", done)[:, 0:T]).then_inc(to_act.drained.sem, 1)

                pipeline(act, n_seq, step)

            @block.tensor
            def _(pe):
                pe.wait_ge(setup_dve, 9)
                nc.tensor.transpose(dve_banks[0][0:8, 0:TH], tw[:, 2, :], c["ident"][0:TH, 0:TH])\
                    .then_inc(setup_pe, 1)
                pe.wait_ge(setup_dve, 10)
                for b in range(2 * BITS):
                    ins = nc.tensor.matmul(dve_banks[1][0:2 * BITS, b * TH:(b + 1) * TH],
                                           w["basis"][:, b, :], twT[:, :], start=True, stop=True)
                ins.then_inc(setup_pe, 1)
                pe.wait_ge(setup_dve, 12)
                pe.wait_ge(setup_pool, 5)

                def scores(i, back):
                    u, name = back.parity, units[i]
                    n, gs, t = unit(name)
                    width, rows = P * (t + 1), slice(ROWS * n, ROWS * (n + 1))
                    raw, bil = to_act.bank("raw" + name, back), to_dve.bank("bil" + name, back)
                    to_act.wait_free(pe, "raw" + name, back)
                    for s, g in enumerate(gs):
                        ins = nc.tensor.matmul(raw[:, s * width:(s + 1) * width],
                                               q[u][rows, g, P * t:P * t + P], k[u][rows, g, 0:width],
                                               start=True, stop=True)
                    ins.then_inc(to_act.filled.sem, 1)
                    to_dve.wait_free(pe, "bil" + name, back)
                    for s, g in enumerate(gs):
                        for part in range(2):
                            nc.tensor.matmul(bil[:, s * width:(s + 1) * width],
                                             left[u][:, g, P * t:P * t + P], right[u][:, n, part, 0:width],
                                             start=part == 0, stop=False)
                        ins = nc.tensor.matmul(bil[:, (s + 1) * width - P:(s + 1) * width],
                                               c["ident_bf"][:, :], c["mask_rows"][:, :],
                                               start=False, stop=True)
                    ins.then_inc(to_dve.filled.sem, 1)

                def transposes(i, back):
                    ring, job = (to_dve if i % 2 else to_act), "pT" + units[i]
                    ring.wait_free(pe, job, back)
                    pe.wait_ge(exped.sem, exped.done(units[i], back))
                    for b in range(BANK // P):
                        ins = nc.tensor.transpose(ring.bank(job, back)[:, b * P:(b + 1) * P],
                                                  probs[:, i % SLOTS, b * P:(b + 1) * P], c["ident"][:, :])
                    ins.then_inc(ring.filled.sem, 1)

                def values(job, back):
                    bank, n = to_act.bank(job, back), int(job[2])
                    to_act.wait_free(pe, job, back)
                    for i in (3 * n + 1, 3 * n + 2):
                        (to_dve if i % 2 else to_act).wait_drained(pe, "pT" + units[i], back)
                    for j in range(TILES):
                        for t in range(j, TILES):
                            for g in range(GROUPS):
                                i = 3 * n + (2 if t == 0 else g // 2)
                                at = g * P if t == 0 else (g % 2) * T + j * P
                                ins = nc.tensor.matmul(bank[ROWS * g:ROWS * (g + 1), t * P:(t + 1) * P],
                                                       v[:, j, 4 * g + n, :], pT[:, i, at:at + P],
                                                       start=j == 0, stop=j == t)
                    ins.then_inc(to_act.filled.sem, 1)

                def project(job, front):
                    ring = to_act if job in act_front else to_dve
                    bank = ring.bank(job, front)
                    ring.wait_free(pe, job, front)
                    if job == "xnT":
                        for t in range(TILES):
                            pe.wait_ge(vec.sem, vec.done(f"xn{t}", front))
                            ins = nc.tensor.transpose(bank[:, t * P:(t + 1) * P], norm.xn[:, t],
                                                      c["ident"][:, :])
                    elif job == "right":
                        to_act.wait_drained(pe, "xnT", front)
                        ins = nc.tensor.matmul(bank[:, 0:T], w["bits"][:, :], xnT[front.parity][:, :],
                                               start=True, stop=True)
                    else:
                        for j in range(2):
                            g = 2 * int(job[-1]) + j
                            if job[0] == "l":
                                if job == "left0" and j == 0:
                                    to_act.wait_drained(pe, "right", front)
                                weights = bilinear[:, 4 * g:4 * g + 4, :].rearrange("a h b -> a (h b)")
                                source = bits[0:2 * BITS, :]
                            else:
                                weights, source = w["t" + job[0]][:, g, :], xnT[front.parity][:, :]
                            ins = nc.tensor.matmul(bank[:, j * T:(j + 1) * T], weights, source,
                                                   start=True, stop=True)
                    ins.then_inc(ring.filled.sem, 1)

                def step(front, back, done):
                    if back:
                        to_dve.wait_drained(pe, "left1", back)
                        pe.wait_ge(split.sem, split.done("low", back))
                    for i in range(turns):
                        if back:
                            scores(i, back)
                        for t in range(TILES if back and i == PROJECT else 0):
                            to_act.wait_free(pe, f"v{t}", back)
                            nc.tensor.matmul(to_act.bank(f"v{t}", back)[:, 0:D],
                                             xnT[back.parity][:, t * P:(t + 1) * P], w["tv"][:, :],
                                             start=True, stop=True).then_inc(to_act.filled.sem, 1)
                        j, seq = lagging(i, LAG, turns, back, done)
                        if seq:
                            transposes(j, seq)
                        for jobs, seq in ((VALUES, back), (LATE_VALUES, done)):
                            if i in jobs and seq:
                                values(jobs[i], seq)
                        for job in front_at.get(i, []) if front else []:
                            project(job, front)
                        for t in range(TILES if done and i == DIVIDE else 0):
                            to_dve.wait_free(pe, f"o{t}", done)
                            to_act.wait_drained(pe, "yT3", done)
                            for n in range(GROUPS):
                                ins = nc.tensor.transpose(to_dve.bank(f"o{t}", done)[:, n * P:(n + 1) * P],
                                                          yT[:, n, t * P:(t + 1) * P], c["ident"][:, :])
                            ins.then_inc(to_dve.filled.sem, 1)
                        if done and i == BACK:
                            to_act.wait_free(pe, "oT", done)
                            to_dve.wait_drained(pe, "o1", done)
                            for t in range(TILES):
                                ins = nc.tensor.transpose(to_act.bank("oT", done)[:, t * P:(t + 1) * P],
                                                          o[:, t], c["ident"][:, :])
                            ins.then_inc(to_act.filled.sem, 1)
                        if done and i == OUT:
                            if back:
                                to_act.wait_free(pe, "out", done)
                            to_act.wait_drained(pe, "oT", done)
                            for t in range(TILES):
                                ins = nc.tensor.matmul(to_act.bank("out", done)[:, t * D:(t + 1) * D],
                                                       oT[:, t * P:(t + 1) * P], w["t_out"][:, :],
                                                       start=True, stop=True)
                            ins.then_inc(to_act.filled.sem, 1)

                pipeline(pe, n_seq, step)


LAYERS, NH, HD = 2, 8, 64
INNER = NH * HD
WINDOW = 64
HID = 341
CHUNKS = [128, 128, 85]
QK_SCALE = 8.0
SPAN = P + WINDOW


def normalise(nc, n_seq, x, z, c):
    tiles = n_seq * TILES
    with ExitStack() as ctx:
        def sb(name, shape):
            return ctx.enter_context(nc.sbuf_tensor("n_" + name, shape, F32))

        stats, mv = sb("stats", [P, tiles, 6]), sb("mv", [P, tiles, 2])
        var, rstd = sb("var", [P, tiles]), sb("rstd", [P, tiles])
        measured, added, inverted, written = (
            ctx.enter_context(nc.semaphore("n_" + name)) for name in ("measured", "added", "inverted", "written"))

        with nc.Block() as block:
            @block.vector
            def _(dve):
                for t in range(tiles):
                    nc.vector.bn_stats(stats[:, t], x[:, t]).then_inc(measured, 1)
                for t in range(tiles):
                    dve.wait_ge(measured, t + 1)
                    nc.vector.bn_aggr(mv[:, t], stats[:, t]).then_inc(measured, 1)
                for t in range(tiles):
                    if t % TILES == 0:
                        dve.wait_ge(inverted, t // TILES + 1)
                    nc.vector.tensor_scalar(z[:, t], x[:, t], mv[:, t, 0:1], rstd[:, t:t + 1],
                                            ALU.subtract, ALU.mult).then_inc(written, 1)
                dve.wait_ge(written, tiles)

            @block.gpsimd
            def _(pool):
                for t in range(0, tiles, TILES):
                    both = slice(t, t + TILES)
                    pool.wait_ge(measured, tiles + t + TILES)
                    nc.gpsimd.tensor_tensor(var[:, both], mv[:, both, 1], c["eps"][:, 0:TILES], ALU.add)\
                        .then_inc(added, 1)
                    pool.wait_ge(added, t // TILES + 1)
                    nc.gpsimd.tensor_tensor(rstd[:, both], var[:, both], c["minus_half"][:, 0:TILES],
                                            ALU.pow).then_inc(inverted, 1)


def window_attention(nc, n_seq, z, w, c, layer):
    units = ["0.0", "0.1", "1.0", "1.1", "1.2", "1.3"]
    turns = len(units)
    SCORES, DIVIDE, LAG = 2, 3, 5
    values_at = {LAG + 4 - turns: "yT0", LAG + 6 - turns: "yT1"}
    parts = ["q0", "k0", "q1", "k1"]
    COS, SCALE, PROJECT = 1, 2, turns - 1
    project_at = {0: ["zT"], 1: ["q0", "k0"], 2: ["q1"], 3: ["k1"]}
    front_T_at, back_T_at = {3: "q0T", 4: "k0T", 5: "q1T"}, {0: "k1T"}
    act_order, dve_order, part_events, pool_events = [], [], [], []
    for i in range(turns):
        act_order += ["s" + units[i - SCORES]] + project_at.get(i, [])
        act_order += [values_at[i]] if i in values_at else []
        act_order += [at[i] for at in (front_T_at, back_T_at) if i in at]
        act_order += ["v0"] if i == PROJECT else []
        dve_order += ["pT" + units[i - LAG]] + (["v1", "out"] if i == PROJECT else [])
        if 0 <= i - SCALE < len(parts):
            part_events += [f"{e}.{parts[i - SCALE]}" for e in ("rot", "unit")]
        if 0 <= i - COS < len(parts):
            part_events += [f"{e}.{parts[i - COS]}" for e in ("sum", "clip", "cos")]
            pool_events += [f"{e}.{parts[i - COS]}" for e in ("sin", "inv")]
    act_front = [job for i in range(turns) for job in project_at.get(i, [])] + list(front_T_at.values())

    def late(lag):
        return units[turns - lag:]

    def in_turns(lag):
        return late(lag) + units[:turns - lag]

    def unit(name):
        t, n = int(name[0]), int(name[2])
        if t == 1:
            return t, [4 * (n // 2) + n % 2 + 2 * i for i in range(2)], SPAN
        return t, [n + 2 * i for i in range(4)], P

    with ExitStack() as ctx:
        pre = f"w{layer}_"

        def sb(name, shape, dt=F32):
            return ctx.enter_context(nc.sbuf_tensor(pre + name, shape, dt))

        def sem(name):
            return ctx.enter_context(nc.semaphore(pre + name))

        table = sb("table", [P, TILES, 4, HD])
        z_copy = sb("z_copy", [P, TILES, D])
        hT = [sb(f"hT{u}", [P, T]) for u in range(2)]
        raw = sb("raw", [P, len(parts), INNER])
        squares = sb("squares", [P, len(parts), INNER])
        swapped = sb("swapped", [P, len(parts), INNER])
        turned = sb("turned", [P, len(parts), INNER])
        lengths = sb("lengths", [P, len(parts), NH])
        inv = sb("inv", [P, len(parts), NH])
        qT = [sb(f"qT{u}", [P, INNER // P, T]) for u in range(2)]
        kT = [sb(f"kT{u}", [P, INNER // P, T]) for u in range(2)]
        v = sb("v", [P, TILES, NH, HD])
        neg_max = sb("neg_max", [P, len(units), 4])
        sums = sb("sums", [P, len(units), 4])
        probs = sb("probs", [P, len(units), BANK])
        pT = sb("pT", [P, len(units), BANK])
        yT = sb("yT", [P, INNER // P, T])
        act_banks = [ctx.enter_context(nc.psum_tensor(f"{pre}act{i}", [P, BANK], F32)) for i in range(6)]
        dve_banks = [ctx.enter_context(nc.psum_tensor(f"{pre}dve{i}", [P, BANK], F32)) for i in range(2)]
        to_act = Ring(act_banks, sem("act_filled"), sem("act_drained"), act_order, act_front,
                      ["s" + name for name in late(SCORES)] + ["yT0", "yT1"])
        to_dve = Ring(dve_banks, sem("dve_filled"), sem("dve_drained"), dve_order, [],
                      ["pT" + name for name in late(LAG)] + ["out"])
        maxed = Count(sem("maxed"), in_turns(SCORES), [], late(SCORES))
        inverted = Count(sem("inverted"), in_turns(DIVIDE), [], late(DIVIDE))
        divided = Count(sem("divided"), in_turns(DIVIDE), [], late(DIVIDE))
        turn = Count(sem("turn"), part_events, part_events)
        gps = Count(sem("gps"), pool_events, pool_events)
        squared = Count(sem("squared"), parts, parts)
        copied = Count(sem("copied"), ["z0", "z1"], ["z0", "z1"])
        setup, tables_done = sem("setup"), sem("tables_done")

        def kept(a, i):
            t, hs, width = unit(units[i])
            wide = a.rearrange("p (h j) -> p h j", h=len(hs))
            return wide[:, :, P * (t + 1) - width:]

        with nc.Block() as block:
            @block.gpsimd
            def _(pool):
                for i, name in enumerate(units):
                    if name[0] == "1":
                        nc.gpsimd.memset(probs[:, i, :].rearrange("p (h j) -> p h j", h=2)[:, :, 0:WINDOW],
                                         0.0).then_inc(setup, 1)
                for u in range(2):
                    nc.gpsimd.memset(hT[u][:, 0:1], 0.0).then_inc(setup, 1)
                pool.wait_ge(tables_done, 4)

                def turn_part(j, front):
                    p = parts[j]
                    kind, t, s = "qk".index(p[0]), int(p[1]), j
                    if not front.first:
                        pool.wait_ge(turn.sem, turn.done("unit." + p, front.before()))
                    to_act.wait_drained(pool, p, front)
                    halves = raw[:, s, :].rearrange("p (h a d) -> p h a d", a=2, d=HD // 2)
                    nc.gpsimd.tensor_tensor(
                        swapped[:, s, :].rearrange("p (h a d) -> p h a d", a=2, d=HD // 2),
                        halves[:, :, ::-1, :],
                        table[:, t, 2 * kind + 1, :].rearrange("p (a d) -> p a d", a=2)
                        .unsqueeze(1).broadcast_to((P, NH, 2, HD // 2)), ALU.mult).then_inc(gps.sem, 1)
                    pool.wait_ge(turn.sem, turn.done("clip." + p, front))
                    nc.gpsimd.tensor_tensor(inv[:, s, :], lengths[:, s, :], c["minus_half"][:, 0:NH],
                                            ALU.pow).then_inc(gps.sem, 1)

                def step(front, back, done):
                    for i in range(turns):
                        j, seq = lagging(i, DIVIDE, turns, back, done)
                        if seq:
                            t, hs, width = unit(units[j])
                            pool.wait_ge(inverted.sem, inverted.done(units[j], seq))
                            p = kept(probs[:, j, :], j)
                            nc.gpsimd.tensor_tensor(
                                p, p, sums[:, j, 0:len(hs)].unsqueeze(2).broadcast_to((P, len(hs), width)),
                                ALU.mult).then_inc(divided.sem, 1)
                        if front and 0 <= i - COS < len(parts):
                            turn_part(i - COS, front)

                pipeline(pool, n_seq, step)

            @block.vector
            def _(dve):
                for kind, scales in enumerate((w["q_scale"], w["k_scale"])):
                    for swap in range(2):
                        row = scales[:, layer, :]
                        if swap:
                            row = scales[:, layer, :].rearrange("p (a d) -> p a d", a=2)[:, ::-1, :]
                        for t in range(TILES):
                            ins = nc.vector.scalar_tensor_tensor(
                                table[:, t, 2 * kind + swap, :].rearrange("p (a d) -> p a d", a=2),
                                c["rotary"][:, t, 2 * kind + swap, :].rearrange("p (a d) -> p a d", a=2),
                                QK_SCALE if kind == 0 else 1.0,
                                row if swap else row.rearrange("p (a d) -> p a d", a=2),
                                ALU.mult, ALU.mult)
                        ins.then_inc(tables_done, 1)
                dve.wait_ge(tables_done, 4)

                def per_head(a):
                    return a.rearrange("p (h d) -> p h d", h=NH)

                def lengths_and_cos(j, front):
                    p = parts[j]
                    kind, t, s = "qk".index(p[0]), int(p[1]), j
                    dve.wait_ge(squared.sem, squared.done(p, front))
                    nc.vector.tensor_reduce(lengths[:, s, :], per_head(squares[:, s, :]), AX.X, ALU.add)\
                        .then_inc(turn.sem, 1)
                    dve.wait_ge(turn.sem, turn.done("sum." + p, front))
                    nc.vector.tensor_scalar(lengths[:, s, :], lengths[:, s, :], 1e-24, None, ALU.max)\
                        .then_inc(turn.sem, 1)
                    if not front.first:
                        to_act.wait_filled(dve, p + "T", front.before())
                    to_act.wait_drained(dve, p, front)
                    nc.vector.tensor_tensor(
                        per_head(turned[:, s, :]), per_head(raw[:, s, :]),
                        table[:, t, 2 * kind, :].unsqueeze(1).broadcast_to((P, NH, HD)), ALU.mult)\
                        .then_inc(turn.sem, 1)

                def add_sin_and_scale(j, front):
                    p, s = parts[j], j
                    dve.wait_ge(turn.sem, turn.done("cos." + p, front))
                    dve.wait_ge(gps.sem, gps.done("sin." + p, front))
                    nc.vector.tensor_tensor(turned[:, s, :], turned[:, s, :], swapped[:, s, :], ALU.add)\
                        .then_inc(turn.sem, 1)
                    dve.wait_ge(turn.sem, turn.done("rot." + p, front))
                    dve.wait_ge(gps.sem, gps.done("inv." + p, front))
                    nc.vector.tensor_tensor(
                        per_head(turned[:, s, :]), per_head(turned[:, s, :]),
                        inv[:, s, :].unsqueeze(2).broadcast_to((P, NH, HD)), ALU.mult).then_inc(turn.sem, 1)

                def step(front, back, done):
                    for i in range(turns):
                        if front and i == 0:
                            if not front.first:
                                to_act.wait_filled(dve, "zT", front.before())
                            for t in range(TILES):
                                nc.vector.tensor_scalar(z_copy[:, t], front.tile(z, t), 1.0, None, ALU.mult)\
                                    .then_inc(copied.sem, 1)
                        j, seq = lagging(i, SCORES, turns, back, done)
                        if seq:
                            t, hs, width = unit(units[j])
                            to_act.wait_filled(dve, "s" + units[j], seq)
                            nc.vector.tensor_reduce(
                                neg_max[:, j, 0:len(hs)],
                                to_act.bank("s" + units[j], seq)[:, 0:width * len(hs)].rearrange(
                                    "p (h j) -> p h j", h=len(hs)),
                                AX.X, ALU.max, negate=True).then_inc(maxed.sem, 1)
                        j, seq = lagging(i, DIVIDE, turns, back, done)
                        if seq:
                            heads = len(unit(units[j])[1])
                            to_act.wait_drained(dve, "s" + units[j], seq)
                            nc.vector.reciprocal(sums[:, j, 0:heads], sums[:, j, 0:heads])\
                                .then_inc(inverted.sem, 1)
                        j, seq = lagging(i, LAG, turns, back, done)
                        if seq:
                            job = "pT" + units[j]
                            to_dve.wait_filled(dve, job, seq)
                            nc.vector.tensor_copy(pT[:, j, :], to_dve.bank(job, seq)[:, :])\
                                .then_inc(to_dve.drained.sem, 1)
                        if front and 0 <= i - SCALE < len(parts):
                            add_sin_and_scale(i - SCALE, front)
                        if front and 0 <= i - COS < len(parts):
                            lengths_and_cos(i - COS, front)
                        if back and i == PROJECT:
                            to_dve.wait_filled(dve, "v1", back)
                            nc.vector.tensor_copy(
                                v[:, 1, :, :],
                                to_dve.bank("v1", back)[:, :].rearrange("p (h d) -> p h d", h=NH))\
                                .then_inc(to_dve.drained.sem, 1)
                        if done and i == PROJECT:
                            to_dve.wait_filled(dve, "out", done)
                            nc.vector.tensor_tensor(
                                done.tiles(z), done.tiles(z),
                                to_dve.bank("out", done)[:, 0:T].rearrange("p (a d) -> p a d", a=TILES),
                                ALU.add).then_inc(to_dve.drained.sem, 1)

                pipeline(dve, n_seq, step)

            @block.scalar
            def _(act):
                act.wait_ge(setup, 6)

                def exps(i, back):
                    t, hs, width = unit(units[i])
                    bank = to_act.bank("s" + units[i], back)
                    out = kept(probs[:, i, :], i)
                    if not back.first:
                        to_dve.wait_filled(act, "pT" + units[i], back.before())
                    act.wait_ge(maxed.sem, maxed.done(units[i], back))
                    for s in range(len(hs)):
                        ins = nc.scalar.activation(out[:, s, :], bank[:, s * width:(s + 1) * width], ACT.Exp,
                                                   bias=neg_max[:, i, s:s + 1], accum_out=sums[:, i, s:s + 1])
                    ins.then_inc(to_act.drained.sem, 1)

                def take(job, front):
                    bank, u = to_act.bank(job, front), front.parity
                    if job == "zT":
                        to_act.wait_filled(act, "zT", front)
                        nc.scalar.copy(hT[u][0:HD, :], bank[0:HD, 0:T])
                        nc.scalar.copy(hT[u][HD:P, 1:T], bank[HD:P, 0:T - 1]).then_inc(to_act.drained.sem, 1)
                    elif job[-1] == "T":
                        t, out = int(job[1]), (qT if job[0] == "q" else kT)[u]
                        to_act.wait_filled(act, job, front)
                        nc.scalar.copy(out[:, :, t * P:(t + 1) * P],
                                       bank[:, :].rearrange("p (a t) -> p a t", a=INNER // P))\
                            .then_inc(to_act.drained.sem, 1)
                    else:
                        j = parts.index(job)
                        to_act.wait_filled(act, job, front)
                        if not front.first:
                            act.wait_ge(turn.sem, turn.done("cos." + job, front.before()))
                            act.wait_ge(gps.sem, gps.done("sin." + job, front.before()))
                        nc.scalar.square(squares[:, j, :], bank[:, :]).then_inc(squared.sem, 1)
                        nc.scalar.copy(raw[:, j, :], bank[:, :]).then_inc(to_act.drained.sem, 1)

                def step(front, back, done):
                    for i in range(turns):
                        j, seq = lagging(i, SCORES, turns, back, done)
                        if seq:
                            exps(j, seq)
                        for job in project_at.get(i, []) if front else []:
                            take(job, front)
                        if done and i in values_at:
                            job = values_at[i]
                            n = int(job[2])
                            to_act.wait_filled(act, job, done)
                            nc.scalar.copy(yT[:, 2 * n:2 * n + 2, :].rearrange("p a t -> p (a t)"),
                                           to_act.bank(job, done)[:, :]).then_inc(to_act.drained.sem, 1)
                        if front and i in front_T_at:
                            take(front_T_at[i], front)
                        if back and i in back_T_at:
                            take(back_T_at[i], back)
                        if back and i == PROJECT:
                            to_act.wait_filled(act, "v0", back)
                            nc.scalar.copy(v[:, 0, :, :],
                                           to_act.bank("v0", back)[:, :].rearrange("p (h d) -> p h d", h=NH))\
                                .then_inc(to_act.drained.sem, 1)

                pipeline(act, n_seq, step)

            @block.tensor
            def _(pe):
                def scores(name, back):
                    t, hs, width = unit(name)
                    u, bank = back.parity, to_act.bank("s" + name, back)
                    to_act.wait_free(pe, "s" + name, back)
                    for s, h in enumerate(hs):
                        rows = slice(HD * (h % 2), HD * (h % 2) + HD)
                        out = bank[:, width * s:width * s + width]
                        first_key = P * (t + 1) - width
                        nc.tensor.matmul(out, qT[u][rows, h // 2, P * t:P * t + P],
                                         kT[u][rows, h // 2, first_key:P * (t + 1)], start=True, stop=False)
                        ins = nc.tensor.matmul(out, c["ident_bf"][:, :], c["mask_window"][:, SPAN - width:],
                                               start=False, stop=True)
                    ins.then_inc(to_act.filled.sem, 1)

                def project_values(t, back):
                    ring, job = (to_dve if t else to_act), f"v{t}"
                    ring.wait_free(pe, job, back)
                    nc.tensor.matmul(ring.bank(job, back)[:, :], hT[back.parity][:, t * P:(t + 1) * P],
                                     w["wqkv"][:, layer, 2 * INNER:3 * INNER], start=True, stop=True)\
                        .then_inc(ring.filled.sem, 1)

                def transposes(i, back):
                    job = "pT" + units[i]
                    to_dve.wait_free(pe, job, back)
                    pe.wait_ge(divided.sem, divided.done(units[i], back))
                    for b in range(BANK // P):
                        ins = nc.tensor.transpose(to_dve.bank(job, back)[:, b * P:(b + 1) * P],
                                                  probs[:, i, b * P:(b + 1) * P], c["ident"][:, :])
                    ins.then_inc(to_dve.filled.sem, 1)

                def values(job, last_unit, back):
                    first_head = 4 * int(job[2])
                    to_act.wait_free(pe, job, back)
                    to_dve.wait_drained(pe, "pT" + last_unit, back)
                    bank = to_act.bank(job, back)
                    for pair in range(2):
                        for j in range(TILES):
                            for t in range(j, TILES):
                                for side in range(2):
                                    h = first_head + 2 * pair + side
                                    i = next(i for i, name in enumerate(units)
                                             if unit(name)[0] == t and h in unit(name)[1])
                                    block_ = unit(units[i])[1].index(h) * (t + 1) + j
                                    ins = nc.tensor.matmul(
                                        bank[HD * side:HD * side + HD, pair * T + t * P:pair * T + (t + 1) * P],
                                        v[:, j, h, :], pT[:, i, block_ * P:(block_ + 1) * P],
                                        start=j == 0, stop=j == t)
                    ins.then_inc(to_act.filled.sem, 1)

                def project(job, front):
                    bank = to_act.bank(job, front)
                    to_act.wait_free(pe, job, front)
                    if job == "zT":
                        for t in range(TILES):
                            pe.wait_ge(copied.sem, copied.done(f"z{t}", front))
                            ins = nc.tensor.transpose(bank[:, t * P:(t + 1) * P], z_copy[:, t],
                                                      c["ident"][:, :])
                    elif job[-1] == "T":
                        pe.wait_ge(turn.sem, turn.done("unit." + job[:2], front))
                        for a in range(INNER // P):
                            ins = nc.tensor.transpose(bank[:, a * P:(a + 1) * P],
                                                      turned[:, parts.index(job[:2]), a * P:(a + 1) * P],
                                                      c["ident"][:, :])
                    else:
                        t, at = int(job[1]), "qk".index(job[0]) * INNER
                        if job == parts[0]:
                            to_act.wait_drained(pe, "zT", front)
                        ins = nc.tensor.matmul(bank[:, :], hT[front.parity][:, t * P:(t + 1) * P],
                                               w["wqkv"][:, layer, at:at + INNER], start=True, stop=True)
                    ins.then_inc(to_act.filled.sem, 1)

                def step(front, back, done):
                    for i in range(turns):
                        if back and i == SCORES:
                            to_act.wait_drained(pe, "k1T", back)
                        j, seq = lagging(i, SCORES, turns, back, done)
                        if seq:
                            scores(units[j], seq)
                        for job in project_at.get(i, []) if front else []:
                            project(job, front)
                        if done and i in values_at:
                            values(values_at[i], units[i - LAG - 1], done)
                        j, seq = lagging(i, LAG, turns, back, done)
                        if seq:
                            transposes(j, seq)
                        if front and i in front_T_at:
                            project(front_T_at[i], front)
                        if back and i in back_T_at:
                            project(back_T_at[i], back)
                        if back and i == PROJECT:
                            for t in range(TILES):
                                project_values(t, back)
                        if done and i == PROJECT:
                            to_dve.wait_free(pe, "out", done)
                            to_act.wait_drained(pe, "yT1", done)
                            for t in range(TILES):
                                for pair in range(INNER // P):
                                    ins = nc.tensor.matmul(to_dve.bank("out", done)[:, t * D:(t + 1) * D],
                                                           yT[:, pair, t * P:(t + 1) * P],
                                                           w["wo"][:, layer, pair, :],
                                                           start=pair == 0, stop=pair == INNER // P - 1)
                            ins.then_inc(to_dve.filled.sem, 1)

                pipeline(pe, n_seq, step)


def gated_mlp(nc, n_seq, x, z, w, c, layer):
    last_layer = layer == LAYERS - 1
    act_front, dve_front = ["xnT"], ["moved"]
    act_order = ["g0", "g1", "g2"] + act_front
    dve_order = dve_front + ["a0", "a1", "a2", "out"]
    after = ["ystats0", "ystats1", "ymv0", "ymv1", "yn0", "yn1"] if last_layer else []

    with ExitStack() as ctx:
        pre = f"m{layer}_"

        def sb(name, shape, dt=F32):
            return ctx.enter_context(nc.sbuf_tensor(pre + name, shape, dt))

        def sem(name):
            return ctx.enter_context(nc.semaphore(pre + name))

        h = sb("h", [P, TILES, D])
        hT = [sb(f"hT{u}", [P, T]) for u in range(2)]
        gate = sb("gate", [P, 3, T])
        hidden = sb("hidden", [P, 3, T])
        act_banks = [ctx.enter_context(nc.psum_tensor(f"{pre}act{i}", [P, BANK], F32)) for i in range(2)]
        dve_banks = [ctx.enter_context(nc.psum_tensor(f"{pre}dve{i}", [P, BANK], F32)) for i in range(5)]
        to_act = Ring(act_banks, sem("act_filled"), sem("act_drained"), act_order, act_front)
        to_dve = Ring(dve_banks, sem("dve_filled"), sem("dve_drained"), dve_order, dve_front)
        vec = Count(sem("vec"), after[:4] + PRE_NORM + after[4:], PRE_NORM, after)
        rst = Count(sem("rst"), (RSQRT[2:] if last_layer else []) + RSQRT[:2], RSQRT[:2], RSQRT[2:])
        own = Count(sem("own"), ["own"], ["own"])
        norm = Norm(nc, ctx, pre, vec, rst, c)
        setup = sem("setup")

        with nc.Block() as block:
            @block.gpsimd
            def _(pool):
                nc.gpsimd.memset(hidden[:, 2, :], 1.0).then_inc(setup, 1)

                def step(front, back, done):
                    if done and last_layer:
                        norm.rsqrt(pool, "y", done)
                    if front:
                        norm.rsqrt(pool, "", front)

                pipeline(pool, n_seq, step)

            @block.vector
            def _(dve):
                dve.wait_ge(setup, 1)

                def step(front, back, done):
                    if done and last_layer:
                        wait_apart(nc, dve, c, to_dve.drained.sem, to_dve.drained.done("out", done))
                        norm.moments(dve, "y", done, [done.tile(z, t) for t in range(TILES)])
                    if front:
                        if not front.first:
                            dve.wait_ge(vec.sem, vec.done("xn1", front.before()))
                        nc.vector.tensor_scalar(h[:, :, 0:D // 2], front.tiles(z)[:, :, 0:D // 2], 1.0, None,
                                                ALU.mult).then_inc(own.sem, 1)
                        to_dve.wait_filled(dve, "moved", front)
                        nc.vector.tensor_copy(
                            h[:, :, D // 2:D],
                            to_dve.bank("moved", front)[:, 0:D].rearrange("p (a d) -> p a d", a=TILES))\
                            .then_inc(to_dve.drained.sem, 1)
                        dve.wait_ge(own.sem, own.done("own", front))
                        wait_apart(nc, dve, c, to_dve.drained.sem, to_dve.drained.done("moved", front))
                        norm.moments(dve, "", front, [h[:, t] for t in range(TILES)])
                        dve.wait_ge(rst.sem, rst.done("rstd", front))
                        if not front.first:
                            to_act.wait_filled(dve, "xnT", front.before())
                        for t in range(TILES):
                            norm.scaled("", t, norm.xn[:, t], h[:, t]).then_inc(vec.sem, 1)
                    if done and last_layer:
                        dve.wait_ge(rst.sem, rst.done("yrstd", done))
                        for t in range(TILES):
                            norm.scaled("y", t, norm.yn[:, t], done.tile(z, t)).then_inc(vec.sem, 1)
                        dve.wait_ge(vec.sem, vec.done("yn1", done))
                        nc.vector.tensor_tensor(done.tiles(x), done.tiles(x), norm.yn[:, :, :], ALU.add)
                    if back:
                        for n, rows in enumerate(CHUNKS):
                            to_dve.wait_filled(dve, f"a{n}", back)
                            to_act.wait_drained(dve, f"g{n}", back)
                            nc.vector.scalar_tensor_tensor(
                                hidden[0:rows, n, :], to_dve.bank(f"a{n}", back)[0:rows, 0:T],
                                w["b1"][0:rows, layer, 0, n:n + 1], gate[0:rows, n, :], ALU.add, ALU.mult)\
                                .then_inc(to_dve.drained.sem, 1)
                        to_dve.wait_filled(dve, "out", back)
                        nc.vector.tensor_tensor(
                            back.tiles(z), back.tiles(z),
                            to_dve.bank("out", back)[:, 0:T].rearrange("p (a d) -> p a d", a=TILES),
                            ALU.add).then_inc(to_dve.drained.sem, 1)

                pipeline(dve, n_seq, step)

            @block.scalar
            def _(act):
                def step(front, back, done):
                    if back:
                        for n, rows in enumerate(CHUNKS):
                            to_act.wait_filled(act, f"g{n}", back)
                            nc.scalar.activation(gate[0:rows, n, :], to_act.bank(f"g{n}", back)[0:rows, 0:T],
                                                 ACT.Gelu, bias=w["b1"][0:rows, layer, 1, n:n + 1])\
                                .then_inc(to_act.drained.sem, 1)
                    if front:
                        to_act.wait_filled(act, "xnT", front)
                        nc.scalar.activation(hT[front.parity][:, :], to_act.bank("xnT", front)[:, 0:T],
                                             ACT.Identity, scale=w["ln_g"][:, layer:layer + 1],
                                             bias=w["ln_b"][:, layer:layer + 1])\
                            .then_inc(to_act.drained.sem, 1)

                pipeline(act, n_seq, step)

            @block.tensor
            def _(pe):
                def step(front, back, done):
                    if front:
                        to_dve.wait_free(pe, "moved", front)
                        bank = to_dve.bank("moved", front)
                        for t in range(TILES):
                            out = bank[:, t * HD:(t + 1) * HD]
                            own, ahead = front.tile(z, t)[:, HD:D], front.tile(z, 0)[:, HD:D]
                            ins = nc.tensor.matmul(out, c["next"][:, 0, :], own, start=True, stop=t == 0)
                            if t == 1:
                                ins = nc.tensor.matmul(out, c["next"][:, 1, :], ahead,
                                                       start=False, stop=True)
                        ins.then_inc(to_dve.filled.sem, 1)
                    if back:
                        u, col = back.parity, 0
                        to_act.wait_drained(pe, "xnT", back)
                        for n, rows in enumerate(CHUNKS):
                            for name, ring, at in (("g", to_act, HID), ("a", to_dve, 0)):
                                ring.wait_free(pe, f"{name}{n}", back)
                                nc.tensor.matmul(ring.bank(f"{name}{n}", back)[0:rows, 0:T],
                                                 w["w1"][:, layer, at + col:at + col + rows], hT[u][:, :],
                                                 start=True, stop=True).then_inc(ring.filled.sem, 1)
                            col += rows
                    if front:
                        to_act.wait_free(pe, "xnT", front)
                        for t in range(TILES):
                            pe.wait_ge(vec.sem, vec.done(f"xn{t}", front))
                            ins = nc.tensor.transpose(to_act.bank("xnT", front)[:, t * P:(t + 1) * P],
                                                      norm.xn[:, t], c["ident"][:, :])
                        ins.then_inc(to_act.filled.sem, 1)
                    if back:
                        to_dve.wait_free(pe, "out", back)
                        to_dve.wait_drained(pe, "a2", back)
                        for t in range(TILES):
                            for n, rows in enumerate(CHUNKS):
                                rows = rows + (n == len(CHUNKS) - 1)
                                ins = nc.tensor.matmul(to_dve.bank("out", back)[:, t * D:(t + 1) * D],
                                                       hidden[0:rows, n, t * P:(t + 1) * P],
                                                       w["w2"][0:rows, layer, n, :],
                                                       start=n == 0, stop=n == len(CHUNKS) - 1)
                        ins.then_inc(to_dve.filled.sem, 1)

                pipeline(pe, n_seq, step)


def ffn_layers(nc, n_seq, x, w, c):
    with nc.sbuf_tensor("z", [P, n_seq * TILES, D], F32) as z:
        normalise(nc, n_seq, x, z, c)
        for layer in range(LAYERS):
            window_attention(nc, n_seq, z, w, c, layer)
            gated_mlp(nc, n_seq, x, z, w, c, layer)


LH, LD = 16, 64


def latent_attention(nc, n_seq, x, w, c):
    pairs = LH * LD // P
    units = ["0.0", "0.1", "1.0", "1.1", "1.2", "1.3", "0.2", "0.3", "1.4", "1.5", "1.6", "1.7"]
    turns = len(units)
    DIVIDE, LAG, SLOTS = 1, 3, 6
    values_at = {LAG + 4: "yT0", LAG + 6: "yT1"}
    late_values_at = {LAG + 10 - turns: "yT2", LAG + 12 - turns: "yT3"}
    OUT = 5
    projected_at = {4: ["v0.0"], 5: ["v0.1", "v1.0"], 6: ["v1.1"]}
    front_at = {1: ["xnT"], 2: ["latT"], **{3 + 2 * n: [f"q{n}"] for n in range(4)},
                **{4 + 2 * n: [f"k{n}"] for n in range(4)}}
    front_jobs = [job for i in sorted(front_at) for job in front_at[i]]
    act_order, dve_order = [], []
    for i in range(turns):
        act_order += ["s" + units[i]] + projected_at.get(i, [])
        act_order += [at[i] for at in (values_at, late_values_at) if i in at] + front_at.get(i, [])
        dve_order += ["pT" + units[i - LAG]] + (["out"] if i == OUT else [])
    late_units = units[turns - LAG:]

    def unit(name):
        t, n = int(name[0]), int(name[2])
        if t == 1:
            return t, [4 * (n // 2) + n % 2 + 2 * i for i in range(2)]
        return t, [8 * (n // 2) + n % 2 + 2 * i for i in range(4)]

    with ExitStack() as ctx:
        def sb(name, shape, dt=F32):
            return ctx.enter_context(nc.sbuf_tensor("l_" + name, shape, dt))

        def sem(name):
            return ctx.enter_context(nc.semaphore("l_" + name))

        qT = [sb(f"qT{u}", [P, pairs, T]) for u in range(2)]
        kT = [sb(f"kT{u}", [P, pairs, T]) for u in range(2)]
        v = sb("v", [P, TILES, LH, LD])
        xnT = sb("xnT", [P, T])
        latT = [sb(f"latT{u}", [P, T]) for u in range(2)]
        neg_max = sb("neg_max", [P, len(units), 4])
        sums = sb("sums", [P, len(units), 4])
        probs = sb("probs", [P, SLOTS, BANK])
        pT = sb("pT", [P, len(units), BANK])
        yT = sb("yT", [P, pairs, T])
        y = sb("y", [P, TILES, D])
        act_banks = [ctx.enter_context(nc.psum_tensor(f"l_act{i}", [P, BANK], F32)) for i in range(6)]
        dve_banks = [ctx.enter_context(nc.psum_tensor(f"l_dve{i}", [P, BANK], F32)) for i in range(2)]
        to_act = Ring(act_banks, sem("act_filled"), sem("act_drained"), act_order, front_jobs,
                      late_values_at.values())
        to_dve = Ring(dve_banks, sem("dve_filled"), sem("dve_drained"), dve_order, [],
                      ["pT" + name for name in late_units] + ["out"])
        maxed = Count(sem("maxed"), units)
        turned = units[-DIVIDE:] + units[:-DIVIDE]
        inverted = Count(sem("inverted"), turned, [], units[-DIVIDE:])
        divided = Count(sem("divided"), turned, [], units[-DIVIDE:])
        vec = Count(sem("vec"), PRE_NORM + COPIED_NORM, PRE_NORM, COPIED_NORM)
        rst = Count(sem("rst"), RSQRT, RSQRT[:2], RSQRT[2:])
        norm = Norm(nc, ctx, "l_", vec, rst, c)

        with nc.Block() as block:
            @block.gpsimd
            def _(pool):
                def step(front, back, done):
                    for i in range(turns):
                        if front and i == 0:
                            norm.rsqrt(pool, "", front)
                        if done and i == OUT + 1:
                            norm.rsqrt(pool, "y", done)
                        j, seq = lagging(i, DIVIDE, turns, back, done)
                        if seq:
                            t, hs = unit(units[j])
                            pool.wait_ge(inverted.sem, inverted.done(units[j], seq))
                            p = probs[:, j % SLOTS, :].rearrange("p (h j) -> p h j", h=len(hs))
                            nc.gpsimd.tensor_tensor(
                                p, p, sums[:, j, 0:len(hs)].unsqueeze(2)
                                .broadcast_to((P, len(hs), P * (t + 1))), ALU.mult).then_inc(divided.sem, 1)

                pipeline(pool, n_seq, step)

            @block.vector
            def _(dve):
                def step(front, back, done):
                    for i in range(turns):
                        if back:
                            t, hs = unit(units[i])
                            to_act.wait_filled(dve, "s" + units[i], back)
                            nc.vector.tensor_reduce(
                                neg_max[:, i, 0:len(hs)],
                                to_act.bank("s" + units[i], back)[:, :].rearrange("p (h j) -> p h j", h=len(hs)),
                                AX.X, ALU.max, negate=True).then_inc(maxed.sem, 1)
                        j, seq = lagging(i, DIVIDE, turns, back, done)
                        if seq:
                            heads = len(unit(units[j])[1])
                            to_act.wait_drained(dve, "s" + units[j], seq)
                            nc.vector.reciprocal(sums[:, j, 0:heads], sums[:, j, 0:heads])\
                                .then_inc(inverted.sem, 1)
                        if front and i == 0:
                            norm.pre_moments(dve, front, x)
                        if front and i == 1:
                            norm.pre_scaled(dve, front, x, to_act)
                        j, seq = lagging(i, LAG, turns, back, done)
                        if seq:
                            job = "pT" + units[j]
                            to_dve.wait_filled(dve, job, seq)
                            nc.vector.tensor_copy(pT[:, j, :], to_dve.bank(job, seq)[:, :])\
                                .then_inc(to_dve.drained.sem, 1)
                        if done and i == OUT:
                            to_dve.wait_filled(dve, "out", done)
                            nc.vector.tensor_copy(y[:, :, :].rearrange("p a d -> p (a d)"),
                                                  to_dve.bank("out", done)[:, 0:T])\
                                .then_inc(to_dve.drained.sem, 1)
                            wait_apart(nc, dve, c, to_dve.drained.sem, to_dve.drained.done("out", done))
                            norm.post_copied_moments(dve, done, y)
                        if done and i == OUT + 2:
                            norm.post_copied_scaled(dve, done, x, y)

                pipeline(dve, n_seq, step)

            @block.scalar
            def _(act):
                def step(front, back, done):
                    for i in range(turns):
                        if back:
                            t, hs = unit(units[i])
                            width = P * (t + 1)
                            bank = to_act.bank("s" + units[i], back)
                            if i >= SLOTS:
                                to_dve.wait_filled(act, "pT" + units[i - SLOTS], back)
                            elif not back.first:
                                to_dve.wait_filled(act, "pT" + units[i - SLOTS], back.before())
                            act.wait_ge(maxed.sem, maxed.done(units[i], back))
                            for s in range(len(hs)):
                                ins = nc.scalar.activation(
                                    probs[:, i % SLOTS, s * width:(s + 1) * width],
                                    bank[:, s * width:(s + 1) * width], ACT.Exp,
                                    bias=neg_max[:, i, s:s + 1], accum_out=sums[:, i, s:s + 1])
                            ins.then_inc(to_act.drained.sem, 1)
                        for job in projected_at.get(i, []) if back else []:
                            t, half = int(job[1]), int(job[3])
                            to_act.wait_filled(act, job, back)
                            nc.scalar.copy(v[:, t, 8 * half:8 * half + 8, :],
                                           to_act.bank(job, back)[:, :].rearrange("p (h d) -> p h d", h=8))\
                                .then_inc(to_act.drained.sem, 1)
                        for at, seq in ((values_at, back), (late_values_at, done)):
                            if i in at and seq:
                                n = int(at[i][2])
                                to_act.wait_filled(act, at[i], seq)
                                nc.scalar.copy(yT[:, 2 * n:2 * n + 2, :].rearrange("p a t -> p (a t)"),
                                               to_act.bank(at[i], seq)[:, :]).then_inc(to_act.drained.sem, 1)
                        for job in front_at.get(i, []) if front else []:
                            u, bank = front.parity, to_act.bank(job, front)
                            to_act.wait_filled(act, job, front)
                            if job in ("xnT", "latT"):
                                ins = nc.scalar.copy((xnT if job == "xnT" else latT[u])[:, :], bank[:, 0:T])
                            else:
                                n, out = int(job[1]), {"q": qT, "k": kT}[job[0]][u]
                                ins = nc.scalar.mul(out[:, 2 * n:2 * n + 2, :].rearrange("p a t -> p (a t)"),
                                                    bank[:, :], LD ** -0.5 if job[0] == "q" else 1.0)
                            ins.then_inc(to_act.drained.sem, 1)

                pipeline(act, n_seq, step)

            @block.tensor
            def _(pe):
                def scores(name, back):
                    t, hs = unit(name)
                    width, u = P * (t + 1), back.parity
                    bank = to_act.bank("s" + name, back)
                    to_act.wait_free(pe, "s" + name, back)
                    for s, h in enumerate(hs):
                        rows = slice(LD * (h % 2), LD * (h % 2) + LD)
                        nc.tensor.matmul(bank[:, width * s:width * s + width],
                                         qT[u][rows, h // 2, P * t:P * t + P],
                                         kT[u][rows, h // 2, 0:width], start=True, stop=False)
                        ins = nc.tensor.matmul(bank[:, width * (s + 1) - P:width * (s + 1)],
                                               c["ident_bf"][:, :], c["mask_rows"][:, :],
                                               start=False, stop=True)
                    ins.then_inc(to_act.filled.sem, 1)

                def transposes(name, back):
                    job, slot = "pT" + name, units.index(name) % SLOTS
                    to_dve.wait_free(pe, job, back)
                    pe.wait_ge(divided.sem, divided.done(name, back))
                    for b in range(BANK // P):
                        ins = nc.tensor.transpose(to_dve.bank(job, back)[:, b * P:(b + 1) * P],
                                                  probs[:, slot, b * P:(b + 1) * P], c["ident"][:, :])
                    ins.then_inc(to_dve.filled.sem, 1)

                def values(job, last_unit, back):
                    first_head = 4 * int(job[2])
                    if job == "yT0":
                        to_act.wait_drained(pe, "v1.1", back)
                    else:
                        to_act.wait_free(pe, job, back)
                    to_dve.wait_drained(pe, "pT" + last_unit, back)
                    bank = to_act.bank(job, back)
                    for pair in range(2):
                        for j in range(TILES):
                            for t in range(j, TILES):
                                for side in range(2):
                                    h = first_head + 2 * pair + side
                                    i = next(i for i, name in enumerate(units)
                                             if unit(name)[0] == t and h in unit(name)[1])
                                    block_ = unit(units[i])[1].index(h) * (t + 1) + j
                                    ins = nc.tensor.matmul(
                                        bank[LD * side:LD * side + LD, pair * T + t * P:pair * T + (t + 1) * P],
                                        v[:, j, h, :], pT[:, i, block_ * P:(block_ + 1) * P],
                                        start=j == 0, stop=j == t)
                    ins.then_inc(to_act.filled.sem, 1)

                def project(job, front):
                    bank = to_act.bank(job, front)
                    to_act.wait_free(pe, job, front)
                    if job == "xnT":
                        for t in range(TILES):
                            pe.wait_ge(vec.sem, vec.done(f"xn{t}", front))
                            ins = nc.tensor.transpose(bank[:, t * P:(t + 1) * P], norm.xn[:, t],
                                                      c["ident"][:, :])
                    elif job == "latT":
                        to_act.wait_drained(pe, "xnT", front)
                        ins = nc.tensor.matmul(bank[:, 0:T], w["kv_down"][:, :], xnT[:, :],
                                               start=True, stop=True)
                    else:
                        if job == "k0":
                            to_act.wait_drained(pe, "latT", front)
                        weights, source = (w["q"], xnT) if job[0] == "q" else (w["kv_up"], latT[front.parity])
                        for i in range(2):
                            pair = 2 * int(job[1]) + i
                            ins = nc.tensor.matmul(bank[:, i * T:(i + 1) * T],
                                                   weights[:, pair * P:(pair + 1) * P], source[:, :],
                                                   start=True, stop=True)
                    ins.then_inc(to_act.filled.sem, 1)

                def project_values(job, back):
                    t, half = int(job[1]), int(job[3])
                    at = LH * LD + BANK * half
                    to_act.wait_free(pe, job, back)
                    nc.tensor.matmul(to_act.bank(job, back)[:, :], latT[back.parity][:, t * P:(t + 1) * P],
                                     w["kv_up"][:, at:at + BANK], start=True, stop=True)\
                        .then_inc(to_act.filled.sem, 1)

                def step(front, back, done):
                    if back:
                        to_act.wait_drained(pe, "k3", back)
                    for i in range(turns):
                        if back:
                            scores(units[i], back)
                        for job in projected_at.get(i, []) if back else []:
                            project_values(job, back)
                        j, seq = lagging(i, LAG, turns, back, done)
                        if seq:
                            transposes(units[j], seq)
                        if back and i in values_at:
                            values(values_at[i], units[i - LAG - 1], back)
                        if done and i in late_values_at:
                            values(late_values_at[i], units[i - LAG - 1], done)
                        for job in front_at.get(i, []) if front else []:
                            project(job, front)
                        if done and i == OUT:
                            to_dve.wait_free(pe, "out", done)
                            to_act.wait_drained(pe, "yT3", done)
                            for t in range(TILES):
                                for pair in range(pairs):
                                    ins = nc.tensor.matmul(to_dve.bank("out", done)[:, t * D:(t + 1) * D],
                                                           yT[:, pair, t * P:(t + 1) * P],
                                                           w["l_out"][:, pair, :],
                                                           start=pair == 0, stop=pair == pairs - 1)
                            ins.then_inc(to_dve.filled.sem, 1)

                pipeline(pe, n_seq, step)


EXPERTS, EF = 8, 256
NOT_A_LOGIT, TAKEN = -3.0e38, 3.0e38


def experts_layer(nc, n_seq, x, w, c, out_dram, finished):
    turns = EXPERTS
    half = EXPERTS // 2
    LATE_SUM, SUM, XNT, ROUTER, ROUTE = 1, half + 1, 3, 4, 6
    act_order = [f"h{e}" for e in range(XNT + 1)] + ["xnT"] + [f"h{e}" for e in range(XNT + 1, EXPERTS)]
    late_outputs = ["y0.1", "y1.1"]
    dve_order = late_outputs + ["y0.0", "y1.0", "router"]
    places = ["best0", "best1", "pair", "rest0", "rest1", "chosen"]
    mixes = ["first0", "first1", "second", "mix0", "mix1", "weight"]
    sums = [f"sum{e}.{t}" for e in range(half - 1) for t in range(TILES)]
    late_sums = [f"sum{e}.{t}" for e in range(half, EXPERTS - 1) for t in range(TILES)]
    moments = PRE_NORM[:4]
    vec_order = moments + late_sums + PRE_NORM[4:] + COPIED_NORM + sums + places + mixes
    vec_front, vec_done = PRE_NORM + places + mixes, late_sums + COPIED_NORM

    with ExitStack() as ctx:
        def sb(name, shape, dt=F32):
            return ctx.enter_context(nc.sbuf_tensor("e_" + name, shape, dt))

        def sem(name):
            return ctx.enter_context(nc.semaphore("e_" + name))

        xnT = [sb(f"xnT{u}", [P, T]) for u in range(2)]
        hT = sb("hT", [P, 2, EF // P, T])
        logits = sb("logits", [P, TILES, 2 * EXPERTS])
        best = sb("best", [P, TILES, 8])
        pair = sb("pair", [P, TILES, 8])
        rest = sb("rest", [P, TILES, 2 * EXPERTS])
        diff = sb("diff", [P, TILES])
        lead = sb("lead", [P, TILES])
        second = sb("second", [P, TILES])
        chosen = sb("chosen", [P, TILES, EXPERTS])
        first = sb("first", [P, TILES, EXPERTS])
        weight = [sb(f"weight{u}", [P, TILES, EXPERTS]) for u in range(2)]
        acc = sb("acc", [P, TILES, D])
        act_banks = [ctx.enter_context(nc.psum_tensor(f"e_act{i}", [P, BANK], F32)) for i in range(3)]
        dve_banks = [ctx.enter_context(nc.psum_tensor(f"e_dve{i}", [P, BANK], F32)) for i in range(5)]
        to_act = Ring(act_banks, sem("act_filled"), sem("act_drained"), act_order, ["xnT"])
        to_dve = Ring(dve_banks, sem("dve_filled"), sem("dve_drained"), dve_order, ["router"], late_outputs)
        vec = Count(sem("vec"), vec_order, vec_front, vec_done)
        rst = Count(sem("rst"), RSQRT, RSQRT[:2], RSQRT[2:])
        lead_done = Count(sem("lead_done"), ["diff", "lead"], ["diff", "lead"])
        updated = Count(sem("updated"), ["x"], [], ["x"])
        norm = Norm(nc, ctx, "e_", vec, rst, c)
        setup = sem("setup")

        with nc.Block() as block:
            @block.gpsimd
            def _(pool):
                nc.gpsimd.memset(logits[:, :, EXPERTS:], NOT_A_LOGIT).then_inc(setup, 1)
                nc.gpsimd.memset(pair[:, :, 2:], NOT_A_LOGIT).then_inc(setup, 1)

                def step(front, back, done):
                    if front:
                        norm.rsqrt(pool, "", front)
                    if done:
                        norm.rsqrt(pool, "y", done)
                    if front:
                        pool.wait_ge(vec.sem, vec.done("best1", front))
                        nc.gpsimd.tensor_tensor(diff[:, :], best[:, :, 0], best[:, :, 1], ALU.subtract)\
                            .then_inc(lead_done.sem, 1)

                pipeline(pool, n_seq, step)

            @block.vector
            def _(dve):
                dve.wait_ge(setup, 2)

                def choose(front):
                    to_dve.wait_filled(dve, "router", front)
                    got = to_dve.bank("router", front)[:, 0:TILES * EXPERTS]
                    nc.vector.tensor_copy(logits[:, :, 0:EXPERTS],
                                          got.rearrange("p (a e) -> p a e", a=TILES))\
                        .then_inc(to_dve.drained.sem, 1)
                    wait_apart(nc, dve, c, to_dve.drained.sem, to_dve.drained.done("router", front))
                    for t in range(TILES):
                        nc.vector.max(best[:, t, :], logits[:, t, 0:EXPERTS]).then_inc(vec.sem, 1)
                    dve.wait_ge(vec.sem, vec.done("best1", front))
                    nc.vector.tensor_copy(pair[:, :, 0:2], best[:, :, 0:2]).then_inc(vec.sem, 1)
                    wait_apart(nc, dve, c, vec.sem, vec.done("pair", front))
                    for t in range(TILES):
                        nc.vector.match_replace(rest[:, t, :], pair[:, t, :], logits[:, t, :], TAKEN)\
                            .then_inc(vec.sem, 1)
                    dve.wait_ge(vec.sem, vec.done("rest1", front))
                    nc.vector.tensor_scalar(chosen[:, :, :], rest[:, :, 0:EXPERTS], TAKEN, None,
                                            ALU.is_equal).then_inc(vec.sem, 1)

                def mix(front):
                    dve.wait_ge(lead_done.sem, lead_done.done("lead", front))
                    for t in range(TILES):
                        nc.vector.tensor_scalar(first[:, t, :], logits[:, t, 0:EXPERTS],
                                                best[:, t, 0:1], lead[:, t:t + 1],
                                                ALU.is_equal, ALU.mult).then_inc(vec.sem, 1)
                    nc.vector.tensor_scalar(second[:, :], lead[:, :], -0.5, 0.5, ALU.mult, ALU.add)\
                        .then_inc(vec.sem, 1)
                    dve.wait_ge(vec.sem, vec.done("second", front))
                    for t in range(TILES):
                        nc.vector.tensor_scalar(first[:, t, :], first[:, t, :], second[:, t:t + 1],
                                                None, ALU.add).then_inc(vec.sem, 1)
                    dve.wait_ge(vec.sem, vec.done("mix1", front))
                    nc.vector.tensor_tensor(weight[front.parity][:, :, :], first[:, :, :],
                                            chosen[:, :, :], ALU.mult).then_inc(vec.sem, 1)

                def add_outputs(g, seq):
                    for e in range(half * g, half * (g + 1)):
                        for t in range(TILES):
                            if e % half == 0:
                                to_dve.wait_filled(dve, f"y{t}.{g}", seq)
                            y = to_dve.bank(f"y{t}.{g}", seq)[:, (e % half) * D:(e % half + 1) * D]
                            cw = weight[seq.parity][:, t, e:e + 1]
                            if e == 0:
                                ins = nc.vector.tensor_scalar(acc[:, t], y, cw, None, ALU.mult)
                            else:
                                if e % half == 0:
                                    to_dve.wait_drained(dve, f"y{t}.{g - 1}", seq)
                                else:
                                    dve.wait_ge(vec.sem, vec.done(f"sum{e - 1}.{t}", seq))
                                ins = nc.vector.scalar_tensor_tensor(acc[:, t], y, cw, acc[:, t],
                                                                     ALU.mult, ALU.add)
                            ins.then_inc(to_dve.drained.sem if e % half == half - 1 else vec.sem, 1)

                def step(front, back, done):
                    if front:
                        norm.pre_moments(dve, front, x)
                    if done:
                        add_outputs(1, done)
                    if front:
                        norm.pre_scaled(dve, front, x, to_act)
                    if done:
                        wait_apart(nc, dve, c, to_dve.drained.sem, to_dve.drained.done("y1.1", done))
                        norm.post_copied_moments(dve, done, acc)
                        norm.post_copied_scaled(dve, done, x, acc).then_inc(updated.sem, 1)
                    if back:
                        add_outputs(0, back)
                    if front:
                        choose(front)
                        mix(front)

                pipeline(dve, n_seq, step)

            @block.scalar
            def _(act):
                def step(front, back, done):
                    for i in range(turns):
                        if back:
                            to_act.wait_filled(act, f"h{i}", back)
                            nc.scalar.activation(hT[:, i % 2, :, :].rearrange("p a t -> p (a t)"),
                                                 to_act.bank(f"h{i}", back)[:, :], ACT.Silu)\
                                .then_inc(to_act.drained.sem, 1)
                        if front and i == XNT:
                            to_act.wait_filled(act, "xnT", front)
                            nc.scalar.copy(xnT[front.parity][:, :], to_act.bank("xnT", front)[:, 0:T])\
                                .then_inc(to_act.drained.sem, 1)
                        if front and i == ROUTE:
                            act.wait_ge(lead_done.sem, lead_done.done("diff", front))
                            nc.scalar.activation(lead[:, :], diff[:, :], ACT.Tanh, scale=0.5)\
                                .then_inc(lead_done.sem, 1)

                pipeline(act, n_seq, step)

            @block.tensor
            def _(pe):
                def hidden(e, back):
                    to_act.wait_free(pe, f"h{e}", back)
                    for f in range(EF // P):
                        ins = nc.tensor.matmul(to_act.bank(f"h{e}", back)[:, f * T:(f + 1) * T],
                                               w["e1"][:, e, f * P:(f + 1) * P], xnT[back.parity][:, :],
                                               start=True, stop=True)
                    ins.then_inc(to_act.filled.sem, 1)

                def output(e, seq):
                    to_act.wait_drained(pe, f"h{e}", seq)
                    for t in range(TILES):
                        job = f"y{t}.{e // half}"
                        if e % half == 0:
                            to_dve.wait_free(pe, job, seq)
                        for f in range(EF // P):
                            ins = nc.tensor.matmul(
                                to_dve.bank(job, seq)[:, (e % half) * D:(e % half + 1) * D],
                                hT[:, e % 2, f, t * P:(t + 1) * P], w["e2"][:, e, f, :],
                                start=f == 0, stop=f == EF // P - 1)
                        if e % half == half - 1:
                            ins.then_inc(to_dve.filled.sem, 1)

                def step(front, back, done):
                    for i in range(turns):
                        if back:
                            if i == 0:
                                to_act.wait_drained(pe, "xnT", back)
                            hidden(i, back)
                        e, seq = lagging(i, 1, turns, back, done)
                        if seq:
                            output(e, seq)
                        if front and i == XNT:
                            to_act.wait_free(pe, "xnT", front)
                            for t in range(TILES):
                                pe.wait_ge(vec.sem, vec.done(f"xn{t}", front))
                                ins = nc.tensor.transpose(to_act.bank("xnT", front)[:, t * P:(t + 1) * P],
                                                          norm.xn[:, t], c["ident"][:, :])
                            ins.then_inc(to_act.filled.sem, 1)
                        if front and i == ROUTER:
                            to_act.wait_drained(pe, "xnT", front)
                            to_dve.wait_free(pe, "router", front)
                            for t in range(TILES):
                                ins = nc.tensor.matmul(
                                    to_dve.bank("router", front)[:, t * EXPERTS:(t + 1) * EXPERTS],
                                    xnT[front.parity][:, t * P:(t + 1) * P], w["router"][:, :],
                                    start=True, stop=True)
                            ins.then_inc(to_dve.filled.sem, 1)

                pipeline(pe, n_seq, step)

            @block.sync
            def _(sp):
                with sp.Fori(0, n_seq) as s:
                    sp.wait_ge(updated.sem, s + 1)
                    sp.dma_start(out_dram[:, bass.ds(s * TILES, TILES), :], x[:, bass.ds(s * TILES, TILES), :])\
                        .then_inc(finished, 16)
                sp.wait_ge(finished, 16 * n_seq)


def load(nc, name, pairs):
    with nc.semaphore(name) as loaded, nc.Block() as block:
        @block.sync
        def _(sp):
            for out, source in pairs:
                sp.dma_start(out, source).then_inc(loaded, 16)
            sp.wait_ge(loaded, 16 * len(pairs))


def chip_constants(nc, ctx, d):
    def sb(name, shape, dt=F32):
        return ctx.enter_context(nc.sbuf_tensor(name, shape, dt))

    c = {
        "ident": sb("ident_sb", [P, P]),
        "ident_bf": sb("ident_bf", [P, P], BF16),
        "mask_rows": sb("mask_rows", [P, P], BF16),
        "mask_cols": sb("mask_cols", [P, P], BF16),
        "mask_window": sb("mask_window", [P, SPAN], BF16),
        "pick": sb("pick_sb", [2 * LH, LH * P], F32R),
        "pick8": sb("pick8_sb", [2 * NH, NH * P], F32R),
        "next": sb("next_sb", [P, 2, P]),
        "minus_half": sb("minus_half", [P, 16]),
        "minus_one": sb("minus_one", [P, 16]),
        "eps": sb("eps", [P, TILES]),
        "carrier": sb("carrier", [P, 1]),
    }
    with ExitStack() as staging:
        def st(name, shape):
            return staging.enter_context(nc.sbuf_tensor(name, shape, F32))

        masks, window = st("masks_f32", [P, 2, P]), st("window_f32", [P, SPAN])
        pick, pick8 = st("pick_f32", [2 * LH, LH * P]), st("pick8_f32", [2 * NH, NH * P])
        ready = c["ready"] = ctx.enter_context(nc.semaphore("constants_ready"))
        load(nc, "constants_loaded", [
            (c["ident"][:, :], d["ident"]), (c["next"][:, :, :], d["next_mat"]),
            (masks[:, :, :], d["masks"]), (window[:, :], d["window_mat"]),
            (pick[:, :], d["pick"]), (pick8[:, :], d["pick8_mat"])])
        with nc.Block() as block:
            @block.vector
            def _(dve):
                for out, source in ((c["ident_bf"], c["ident"][:, :]), (c["mask_rows"], masks[:, 0]),
                                    (c["mask_cols"], masks[:, 1]), (c["mask_window"], window[:, :]),
                                    (c["pick"], pick[:, :]), (c["pick8"], pick8[:, :])):
                    nc.vector.tensor_copy(out[:, :], source).then_inc(ready, 1)
                nc.vector.memset(c["minus_half"][:, :], -0.5).then_inc(ready, 1)
                nc.vector.memset(c["eps"][:, :], LN_EPS).then_inc(ready, 1)
                nc.vector.memset(c["minus_one"][:, :], -1.0).then_inc(ready, 1)
                dve.wait_ge(ready, 9)
    return c


def token_phase(nc, n_seq, x, c, d):
    with ExitStack() as scope:
        def sb(name, shape, dt=F32):
            return scope.enter_context(nc.sbuf_tensor(name + "_sb", shape, dt))

        w = {
            "tq": sb("tq", [D, GROUPS, P]),
            "tk": sb("tk", [D, GROUPS, P]),
            "tv": sb("tv", [D, D]),
            "t_out": sb("t_out", [D, D]),
            "low_rows": sb("low_rows", [P, 3]),
            "bits": sb("bits", [D, P]),
            "basis": sb("basis", [8, 2 * BITS, 2 * BITS]),
            "transform": sb("transform", [TH, NT]),
            "scalars": sb("scalars", [P, 4]),
        }
        load(nc, "token_loaded", [
            *((w[name][:], d[name]) for name in list(w)[:-1]),
            (w["scalars"][:, :], d["scalars"].partition_broadcast(P))])
        token_attention(nc, n_seq, x, w, c)


def ffn_phase(nc, n_seq, x, c, d):
    with ExitStack() as scope:
        def sb(name, shape, dt=F32):
            return scope.enter_context(nc.sbuf_tensor(name + "_sb", shape, dt))

        c["rotary"] = sb("rotary", [P, TILES, 4, HD])
        w = {
            "wqkv": sb("wqkv", [D, LAYERS, 3 * INNER]),
            "wo": sb("wo", [P, LAYERS, INNER // P, D]),
            "w1": sb("w1", [D, LAYERS, 2 * HID]),
            "w2": sb("w2", [P, LAYERS, 3, D]),
            "b1": sb("b1", [P, LAYERS, 2, 3]),
            "ln_g": sb("ln_g", [D, LAYERS]),
            "ln_b": sb("ln_b", [D, LAYERS]),
            "q_scale": sb("q_scale", [P, LAYERS, HD]),
            "k_scale": sb("k_scale", [P, LAYERS, HD]),
        }
        pairs = [(c["rotary"][:], d["rotary_tab"])]
        pairs += [(w[name][:], d[name]) for name in ("w2", "b1", "ln_g", "ln_b")]
        for layer in range(LAYERS):
            pairs += [
                (w["wqkv"][:, layer], d["L0_ffn_wqkv"][layer]),
                (w["wo"][:, layer], d["L0_ffn_wo"][layer].rearrange("(a p) n -> p a n", p=P)),
                (w["w1"][:, layer], d["L0_ffn_w1"][layer]),
                (w["q_scale"][:, layer], d["L0_ffn_q_scale"][layer].partition_broadcast(P)),
                (w["k_scale"][:, layer], d["L0_ffn_k_scale"][layer].partition_broadcast(P))]
        load(nc, "ffn_loaded", pairs)
        ffn_layers(nc, n_seq, x, w, c)


def latent_phase(nc, n_seq, x, c, d):
    with ExitStack() as scope:
        def sb(name, shape, dt=F32):
            return scope.enter_context(nc.sbuf_tensor(name + "_sb", shape, dt))

        w = {
            "kv_down": sb("kv_down", [D, D]),
            "kv_up": sb("kv_up", [D, 2 * LH * LD]),
            "q": sb("wq", [D, LH * LD]),
            "l_out": sb("l_out", [P, LH * LD // P, D]),
        }
        load(nc, "latent_loaded", [
            (w["kv_down"][:, :], d["L1_attn_w_kv_down"]), (w["kv_up"][:, :], d["L1_attn_w_kv_up"]),
            (w["q"][:, :], d["L1_attn_w_q"]),
            (w["l_out"][:, :, :], d["L1_attn_w_out"].rearrange("(c p) n -> p c n", p=P))])
        latent_attention(nc, n_seq, x, w, c)


def experts_phase(nc, n_seq, x, c, d, finished):
    with ExitStack() as scope:
        def sb(name, shape, dt=F32):
            return scope.enter_context(nc.sbuf_tensor(name + "_sb", shape, dt))

        w = {
            "router": sb("router", [D, EXPERTS]),
            "e1": sb("e1", [D, EXPERTS, EF]),
            "e2": sb("e2", [P, EXPERTS, EF // P, D]),
        }
        load(nc, "experts_loaded", [
            (w["router"][:, :], d["L1_ffn_router_w"]),
            (w["e1"][:, :, :], d["L1_ffn_w1"].rearrange("e d f -> d e f")),
            *((w["e2"][:, e], d["L1_ffn_w2"][e].rearrange("(a p) n -> p a n", p=P))
              for e in range(EXPERTS))])
        experts_layer(nc, n_seq, x, w, c, d["out"].rearrange("(n p) d -> p n d", p=P), finished)


def build(nc, n_seq, d, phases=(token_phase, ffn_phase, latent_phase)):
    with ExitStack() as ctx:
        x = ctx.enter_context(nc.sbuf_tensor("x_sb", [P, n_seq * TILES, D], F32))
        c = chip_constants(nc, ctx, d)
        load(nc, "x_loaded", [(x[:, :, :], d["x"].rearrange("(n p) d -> p n d", p=P))])
        finished = ctx.enter_context(nc.semaphore("finished"))
        for phase in phases:
            phase(nc, n_seq, x, c, d)
        experts_phase(nc, n_seq, x, c, d, finished)


def constants():
    f32 = np.float32
    row, col = np.arange(P)[:, None], np.arange(P)[None]
    causal = np.where(col > row, MASKED, 0.0).astype(f32)
    window = np.arange(SPAN)[None]

    def picker(heads):
        out = np.zeros((2, heads, heads, P), f32)
        for h in range(heads):
            out[:, h, h] = 1.0
        return out.reshape(2 * heads, heads * P)

    half = np.arange(0, HD, 2, dtype=f32)
    inv_freq = (1.0 / 10000.0 ** (half / HD)).astype(f32)
    angle = (np.arange(T, dtype=f32)[:, None] * inv_freq[None]).astype(f32)
    angle = np.concatenate([angle, angle], -1).astype(np.float64)
    base = (half.astype(np.float64) + 0.4 * HD) / (1.4 * HD)
    scale = base[None] ** ((np.arange(T) - T // 2) / float(WINDOW // 2))[:, None]
    scale = np.concatenate([scale, scale], -1)
    sign = np.where(np.arange(HD) < HD // 2, -1.0, 1.0)
    cos, sin = np.cos(angle), np.sin(angle) * sign
    rotary = np.stack([cos * scale, sin * scale, cos / scale, sin / scale], 1)

    following = np.zeros((P, 2, P), f32)
    following[np.arange(P - 1), 0, np.arange(1, P)] = 1.0
    following[P - 1, 1, 0] = 1.0
    place = np.arange(P) % ROWS
    low_rows = np.stack([place // TD % 2 == 1, place // (2 * TD) == 1, place // (2 * BITS) == 1], 1)
    return {
        "low_rows": -low_rows.astype(f32),
        "ident": np.eye(P, dtype=f32),
        "masks": np.ascontiguousarray(np.stack([causal, causal.T], 1)),
        "pick": picker(LH),
        "pick8_mat": picker(NH),
        "window_mat": np.where((window >= row) & (window <= row + WINDOW), 0.0, MASKED).astype(f32),
        "rotary_tab": np.ascontiguousarray(
            rotary.reshape(TILES, P, 4, HD).transpose(1, 0, 2, 3)).astype(f32),
        "next_mat": following,
    }


def layouts(a):
    f32 = np.float32
    qkv = a["L0_attn_qkv_w"].reshape(3, TH, TD, D)

    def grouped(weights):
        out = np.repeat(weights.reshape(GROUPS, GROUPS, 1, TD, D), ROWS // TD, axis=2)
        return out.transpose(4, 0, 1, 2, 3).reshape(D, GROUPS, P)

    bits = np.zeros((D, GROUPS, ROWS), f32)
    for copy in range(2):
        bits[..., 2 * BITS * copy:2 * BITS * copy + BITS] = a["L0_attn_hex_w"].T[:, None]
        bits[..., 2 * BITS * copy + BITS:2 * BITS * copy + 2 * BITS] = a["L0_attn_q6_w"].T[:, None]
    basis = np.zeros((NT + 1, 2 * BITS, 2 * BITS), f32)
    basis[:NT, BITS:, BITS:] = a["L0_attn_transforms"].transpose(0, 2, 1)
    basis[NT, np.arange(BITS), np.arange(BITS)] = 1.0

    w2 = np.zeros((P, LAYERS, 3, D), f32)
    b1 = np.zeros((P, LAYERS, 2, 3), f32)
    at = 0
    for n, rows in enumerate(CHUNKS):
        w2[:rows, :, n] = a["L0_ffn_w2"][:, at:at + rows].transpose(1, 0, 2)
        for part in range(2):
            b1[:rows, :, part, n] = a["L0_ffn_b1"][:, part * HID + at:part * HID + at + rows].T
        at += rows
    w2[CHUNKS[-1], :, 2] = a["L0_ffn_b2"]
    out = {
        "x": a["L0_attn_x"].reshape(-1, D),
        "tq": grouped(qkv[0]), "tk": grouped(qkv[1]), "tv": qkv[2].reshape(TH * TD, D).T,
        "t_out": a["L0_attn_out_w"].T,
        "bits": bits.reshape(D, P), "basis": basis,
        "transform": a["L0_attn_transform_weights"],
        "scalars": np.concatenate([a["L0_attn_hamming_lambda_logit"].reshape(1),
                                   a["L0_attn_scale_logit"].reshape(1),
                                   a["L0_attn_sips_alpha"], a["L0_attn_sips_beta"]]),
        "w2": w2, "b1": b1, "ln_g": a["L0_ffn_ln_g"].T, "ln_b": a["L0_ffn_ln_b"].T,
    }
    for name in ("L0_ffn_wqkv", "L0_ffn_wo", "L0_ffn_w1", "L0_ffn_q_scale", "L0_ffn_k_scale",
                 "L1_attn_w_kv_down", "L1_attn_w_kv_up", "L1_attn_w_q", "L1_attn_w_out",
                 "L1_ffn_router_w", "L1_ffn_w1", "L1_ffn_w2"):
        out[name] = a[name]
    return {k: np.ascontiguousarray(v) for k, v in out.items()}


def kernel(**inputs):
    import concourse.bacc as bacc
    from concourse.bass_utils import run_bass_kernel_spmd

    given = {k: np.asarray(v) for k, v in inputs.items()}
    n_seq = given["L0_attn_x"].shape[0]
    arrays = {**constants(), **layouts(given)}
    nc = bacc.Bacc("TRN2", target_bir_lowering=False, num_devices=1)
    dram = {k: nc.dram_tensor(k, v.shape, F32, kind="ExternalInput").ap() for k, v in arrays.items()}
    dram["out"] = nc.dram_tensor("out", (n_seq * T, D), F32, kind="ExternalOutput").ap()
    build(nc, n_seq, dram)
    result = run_bass_kernel_spmd(nc, [arrays], core_ids=[0])
    return result.results[0]["out"].reshape(n_seq, T, D)
```
